# Optimizing a Trainium2 kernel written in Bass

```python
import numpy as np
import jax
import jax.numpy as jnp

def _softmax(x, axis=-1):
    return jax.nn.softmax(x, axis=axis)

def _gelu(x):
    return jax.nn.gelu(x, approximate=True)

def _silu(x):
    return jax.nn.silu(x)

def _sigmoid(x):
    return jax.nn.sigmoid(x)

def _layernorm(x, axis=-1, eps=1e-05):
    m = jnp.mean(x, axis=axis, keepdims=True)
    v = jnp.var(x, axis=axis, keepdims=True)
    return (x - m) / jnp.sqrt(v + eps)

def _scatter_add(tgt, idx, src, axis=0):
    return tgt.at[idx].add(src)

def _segment_sum(src, seg, n):
    return jax.ops.segment_sum(src, seg, n)
kernel_name = 'mk_flamingo_gated_d1_seqx_r4_8cf5c3'

def setup_inputs(seed: int=0):
    np.random.seed(seed)
    _w = jnp.asarray

    def _rec_inputs():
        import jax
        import jax.numpy as jnp
        _rk = jax.random.key(seed)
        x = -0.0005207 + 1.001 * jax.random.normal(jax.random.fold_in(_rk, 1), (4, 512, 512), jnp.float32)
        _lenS = 512 - jax.random.randint(jax.random.fold_in(_rk, 7), (4,), 0, max(1, 512 // 4) + 1, jnp.int32)
        _lenS2 = 512 - jax.random.randint(jax.random.fold_in(_rk, 8), (4,), 0, max(1, 512 // 4) + 1, jnp.int32)
        _ctx_2048P = jax.random.normal(jax.random.fold_in(_rk, 12), (4, 16, 512), jnp.float32)
        _ctx_2048c = jax.random.dirichlet(jax.random.fold_in(_rk, 512), 0.3 * jnp.ones((16,), jnp.float32), (4, 512))
        _ctx_2048t = jnp.einsum('bsk,bkd->bsd', _ctx_2048c, _ctx_2048P)
        _ctx_2048t = _ctx_2048t * jax.lax.rsqrt(jnp.mean(jnp.square(_ctx_2048t)) + 1e-12) * 0.953939
        ctx_2048 = -5.72187e-05 + 0.999849 * (_ctx_2048t + 0.3 * jax.random.normal(jax.random.fold_in(_rk, 612), (4, 512, 512), jnp.float32))
        _validS = jnp.arange(512)[None, :] < _lenS[:, None]
        _validS2 = jnp.arange(512)[None, :] < _lenS2[:, None]
        _causal = jnp.tril(jnp.ones((512, 512), dtype=bool))
        mask_BxSx4224_bf0 = jnp.logical_not(jnp.ones((4, 512, 1056), dtype=bool))
        _g = jax.random.normal(jax.random.fold_in(_rk, 9001), (2, 1), jnp.float32)
        _g = jnp.sign(_g) * jnp.maximum(jnp.abs(_g), 1.0) + (_g == 0) * 1.0
        g_xattn = _g[0]
        g_ffn = _g[1]
        return (x, ctx_2048, mask_BxSx4224_bf0, g_xattn, g_ffn)
    x, ctx_2048, mask_BxSx4224_bf0, g_xattn, g_ffn = _rec_inputs()

    def _L0_xattn_setup():
        import jax, jax.numpy as jnp
        import numpy as np
        import math
        DIM = 512
        B, Q_LEN, KV_LEN = (8, 128, 1024)
        key = jax.random.key(seed)
        ks = jax.random.split(key, 8)
        x = jax.random.normal(ks[0], (B, Q_LEN, DIM), dtype=jnp.float32)
        mask = jnp.zeros((B, Q_LEN, KV_LEN + Q_LEN), dtype=bool)
        k_cache = jax.random.normal(ks[1], (B, KV_LEN, DIM), dtype=jnp.float32)
        v_cache = jax.random.normal(ks[2], (B, KV_LEN, DIM), dtype=jnp.float32)
        scale = 1.0 / math.sqrt(DIM)
        wq = jax.random.normal(ks[3], (DIM, DIM), dtype=jnp.float32) * scale
        wk = jax.random.normal(ks[4], (DIM, DIM), dtype=jnp.float32) * scale
        wv = jax.random.normal(ks[5], (DIM, DIM), dtype=jnp.float32) * scale
        wo = jax.random.normal(ks[6], (DIM, DIM), dtype=jnp.float32) * scale
        return {'x': x, 'mask': mask, 'k_cache': k_cache, 'v_cache': v_cache, 'wq': wq, 'wk': wk, 'wv': wv, 'wo': wo}
    _L0_xattn_all = _L0_xattn_setup()
    _L0_xattn_in = {k: v for k, v in _L0_xattn_all.items() if k in ('wq', 'wk', 'wv', 'wo')}
    del _L0_xattn_all

    def _L0_ffn_setup():
        import jax, jax.numpy as jnp
        import numpy as np
        HIDDEN = 512
        EXPERT_FF = 352
        NUM_EXPERTS = 16
        NUM_SHARED = 2
        SHARED_FF = EXPERT_FF * NUM_SHARED
        TOP_K = 4
        SCALE = 1.0
        BATCH, SEQ = (1, 512)

        def _moe_forward(hidden_states, Wg, W1, W2, W3, W1s, W2s, W3s):
            B, S, D = hidden_states.shape
            x = hidden_states.reshape(-1, D)
            T = x.shape[0]
            E = Wg.shape[0]
            shared = jax.nn.silu(x @ W1s.T) * (x @ W3s.T) @ W2s.T
            logits = x @ Wg.T
            probs = jax.nn.softmax(logits.astype(jnp.float32), axis=-1)
            topk_w, sel = jax.lax.top_k(probs, TOP_K)
            topk_w = topk_w.astype(x.dtype) * SCALE
            combine = jnp.zeros((T, E), x.dtype).at[jnp.arange(T)[:, None], sel].add(topk_w)
            h = jax.nn.silu(jnp.einsum('td,efd->etf', x, W1)) * jnp.einsum('td,efd->etf', x, W3)
            routed = jnp.einsum('etf,edf->td', h * combine.T[:, :, None], W2)
            return (shared + routed).reshape(B, S, D)
        key = jax.random.key(seed)
        ks = jax.random.split(key, 8)
        std = 0.02
        return {'hidden_states': jax.random.normal(ks[0], (BATCH, SEQ, HIDDEN), dtype=jnp.float32), 'Wg': jax.random.normal(ks[1], (NUM_EXPERTS, HIDDEN), dtype=jnp.float32) * std, 'W1': jax.random.normal(ks[2], (NUM_EXPERTS, EXPERT_FF, HIDDEN), dtype=jnp.float32) * std, 'W2': jax.random.normal(ks[3], (NUM_EXPERTS, HIDDEN, EXPERT_FF), dtype=jnp.float32) * std, 'W3': jax.random.normal(ks[4], (NUM_EXPERTS, EXPERT_FF, HIDDEN), dtype=jnp.float32) * std, 'W1s': jax.random.normal(ks[5], (SHARED_FF, HIDDEN), dtype=jnp.float32) * std, 'W2s': jax.random.normal(ks[6], (HIDDEN, SHARED_FF), dtype=jnp.float32) * std, 'W3s': jax.random.normal(ks[7], (SHARED_FF, HIDDEN), dtype=jnp.float32) * std}
    _L0_ffn_all = _L0_ffn_setup()
    _L0_ffn_in = {k: v for k, v in _L0_ffn_all.items() if k in ('Wg', 'W1', 'W2', 'W3', 'W1s', 'W2s', 'W3s')}
    del _L0_ffn_all
    return {'x': x, 'ctx_2048': ctx_2048, 'mask_BxSx4224_bf0': mask_BxSx4224_bf0, 'g_xattn': g_xattn, 'g_ffn': g_ffn, 'L0_xattn_wq': _L0_xattn_in['wq'], 'L0_xattn_wk': _L0_xattn_in['wk'], 'L0_xattn_wv': _L0_xattn_in['wv'], 'L0_xattn_wo': _L0_xattn_in['wo'], 'L0_ffn_Wg': _L0_ffn_in['Wg'], 'L0_ffn_W1': _L0_ffn_in['W1'], 'L0_ffn_W2': _L0_ffn_in['W2'], 'L0_ffn_W3': _L0_ffn_in['W3'], 'L0_ffn_W1s': _L0_ffn_in['W1s'], 'L0_ffn_W2s': _L0_ffn_in['W2s'], 'L0_ffn_W3s': _L0_ffn_in['W3s']}

def reference(x, ctx_2048, mask_BxSx4224_bf0, g_xattn, g_ffn, L0_xattn_wq, L0_xattn_wk, L0_xattn_wv, L0_xattn_wo, L0_ffn_Wg, L0_ffn_W1, L0_ffn_W2, L0_ffn_W3, L0_ffn_W1s, L0_ffn_W2s, L0_ffn_W3s):
    import jax
    import jax.numpy as jnp

    def _L0_xattn_ref(x, mask, k_cache, v_cache, wq, wk, wv, wo):
        import jax, jax.numpy as jnp
        import numpy as np
        import math
        DIM = 512
        B, Q_LEN, KV_LEN = (8, 128, 1024)
        q = jnp.einsum('bsd,ed->bse', x, wq)
        k_new = jnp.einsum('bsd,ed->bse', x, wk)
        v_new = jnp.einsum('bsd,ed->bse', x, wv)
        k = jnp.concatenate([k_cache, k_new], axis=1)
        v = jnp.concatenate([v_cache, v_new], axis=1)
        scale = 1.0 / math.sqrt(q.shape[-1])
        scores = jnp.einsum('bqd,bkd->bqk', q, k) * scale
        attn = jax.nn.softmax(scores, axis=-1)
        out = jnp.einsum('bqk,bkd->bqd', attn, v)
        return jnp.einsum('bqd,ed->bqe', out, wo)

    def _L0_ffn_ref(hidden_states, Wg, W1, W2, W3, W1s, W2s, W3s):
        import jax, jax.numpy as jnp
        import numpy as np
        HIDDEN = 512
        EXPERT_FF = 352
        NUM_EXPERTS = 16
        NUM_SHARED = 2
        SHARED_FF = EXPERT_FF * NUM_SHARED
        TOP_K = 4
        SCALE = 1.0
        BATCH, SEQ = (1, 512)

        def _moe_forward(hidden_states, Wg, W1, W2, W3, W1s, W2s, W3s):
            B, S, D = hidden_states.shape
            x = hidden_states.reshape(-1, D)
            T = x.shape[0]
            E = Wg.shape[0]
            shared = jax.nn.silu(x @ W1s.T) * (x @ W3s.T) @ W2s.T
            logits = x @ Wg.T
            probs = jax.nn.softmax(logits.astype(jnp.float32), axis=-1)
            topk_w, sel = jax.lax.top_k(probs, TOP_K)
            topk_w = topk_w.astype(x.dtype) * SCALE
            combine = jnp.zeros((T, E), x.dtype).at[jnp.arange(T)[:, None], sel].add(topk_w)
            h = jax.nn.silu(jnp.einsum('td,efd->etf', x, W1)) * jnp.einsum('td,efd->etf', x, W3)
            routed = jnp.einsum('etf,edf->td', h * combine.T[:, :, None], W2)
            return (shared + routed).reshape(B, S, D)
        return _moe_forward(hidden_states, Wg, W1, W2, W3, W1s, W2s, W3s)
    x = x + jnp.tanh(g_xattn[0]) * _L0_xattn_ref(_layernorm(x, axis=-1), mask_BxSx4224_bf0, ctx_2048, ctx_2048, L0_xattn_wq, L0_xattn_wk, L0_xattn_wv, L0_xattn_wo)
    x = x + jnp.tanh(g_ffn[0]) * _L0_ffn_ref(_layernorm(x, axis=-1), L0_ffn_Wg, L0_ffn_W1, L0_ffn_W2, L0_ffn_W3, L0_ffn_W1s, L0_ffn_W2s, L0_ffn_W3s)
    return x

_drawn_inputs = setup_inputs


def setup_inputs(seed=0):
    import zlib

    import numpy as np

    out = dict(_drawn_inputs(seed))
    spreads = {}
    factors = {'L0_ffn_Wg': 7.872,
     'L0_ffn_W1': 6.834,
     'L0_ffn_W2': 6.741,
     'L0_ffn_W3': 6.705,
     'L0_ffn_W1s': 8.0,
     'L0_ffn_W2s': 8.0,
     'L0_ffn_W3s': 8.0}
    for name, (base, spread) in spreads.items():
        noise = np.random.default_rng([zlib.crc32(name.encode()), seed]).standard_normal(out[name].shape)
        drawn = base * np.exp(spread * noise) if base else spread * noise
        out[name] = jnp.asarray(drawn.astype(out[name].dtype))
    for name, factor in factors.items():
        out[name] = (out[name] * factor).astype(out[name].dtype)
    return out
```

```python
from contextlib import ExitStack

import concourse.bass as bass
from concourse import mybir

F32 = mybir.dt.float32
F32R = mybir.dt.float32r
F16 = mybir.dt.float16
I32 = mybir.dt.int32
ALU = mybir.AluOpType
ACT = mybir.ActivationFunctionType
AX = mybir.AxisListType

P = 128
B, S, D = 4, 512, 512
T = B * S
NT = T // P
IT = S // P
DC = D // P
KC = 2 * S // P
E, FF, TOPK = 16, 352, 4
FC = 3
FT = FF - 2 * P
SF = 704
SC = 6
ST = SF - 5 * P
TILES_MAX = 80
REST = TILES_MAX - T * TOPK // P
EPS = 1e-5
SCALE = float(D) ** -0.5


class Count:

    def __init__(self, start=0):
        self.base, self.n = start, 0

    def up(self, k=1):
        self.n += k
        return self.base + self.n

    @property
    def now(self):
        return self.base + self.n

    def enter(self, i, per):
        self.start, self.per = self.base + self.n, per
        self.base, self.n = i * per + self.start, 0

    def leave(self, passes):
        assert self.n == self.per, (self.n, self.per)
        self.base, self.n = self.start + passes * self.per, 0


def hold(nc, eng, keep):
    idle = keep["idle"]
    if eng is nc.vector:
        eng.memset(idle[:, 0:1], 0.0)
    elif eng is nc.scalar:
        eng.activation(idle[:, 1:2], idle[:, 2:3], ACT.Copy)
    else:
        eng.tensor_tensor(idle[:, 3:4], idle[:, 4:5], idle[:, 4:5], ALU.add)


TERMS = ((0, 0), (0, 1), (1, 0))


def tripled(pe, out, pairs):
    n = 0
    for a, b in pairs:
        for i, j in TERMS:
            last = pe.matmul(out, a[i], b[j], start=(n == 0), stop=(n == 3 * len(pairs) - 1))
            n += 1
    return last


class Sbuf:

    def __init__(self, nc, at):
        self.nc, self.at = nc, at

    def __call__(self, name, shape, dt):
        size = {F32: 4, F32R: 4, I32: 4, F16: 2}[dt]
        for n in shape[1:]:
            size *= n
        t = self.nc.alloc_sbuf_tensor_at(name, shape, dt, offset=self.at)
        self.at += -(-size // 32) * 32
        return t

    def split(self, name, shape):
        hi = self(name + "_hi", shape, F32R)
        at = self.at
        lo = self(name + "_lo", shape, F32R)
        end, self.at = self.at, at
        raw = self(name + "_raw", shape, F32)
        self.at = end
        return hi, lo, raw


def attention_phase(nc, io, mem, keep, first_free):
    sb = Sbuf(nc, first_free)
    wq_hi, wq_lo, wq_raw = sb.split("wq", [P, DC, D])
    wk_hi, wk_lo, wk_raw = sb.split("wk", [P, DC, D])
    wv_hi, wv_lo, wv_raw = sb.split("wv", [P, DC, D])
    wo_hi, wo_lo, wo_raw = sb.split("wo", [P, DC, D])
    ctxT_hi, ctxT_lo, ctxT_raw = sb.split("ctxT", [P, DC, S])
    ctx_hi, ctx_lo, ctx_raw = sb.split("ctx", [P, IT, D])
    xnT_hi, xnT_lo = sb("xnT_hi", [P, DC, S], F32R), sb("xnT_lo", [P, DC, S], F32R)
    q_hi, q_lo = sb("q_hi", [P, DC, S], F32R), sb("q_lo", [P, DC, S], F32R)
    k_hi, k_lo = sb("k_hi", [P, DC, S], F32R), sb("k_lo", [P, DC, S], F32R)
    prob = sb("prob", [P, 2 * S], F32)
    at = sb.at
    pT_hi, pT_lo = sb("pT_hi", [P, KC, S], F32R), sb("pT_lo", [P, KC, S], F32R)
    over = Sbuf(nc, at)
    xn2T = over("xn2T", [P, DC, S], F32)
    over = Sbuf(nc, at + 4 * KC * S)
    above = over("above", [P, IT, E, E], F32)
    level = over("level", [P, IT, E, E], F32)
    x_t = sb("x_t", [P, IT, D], F32)
    r_t = sb("r_t", [P, IT, D], F32)
    assert sb.at <= nc.sbuf_usable_end, sb.at

    ident, probs, ranks, gates = (keep[k] for k in ("ident", "probs", "ranks", "gates"))
    small = Sbuf(nc, keep["phase_at"])
    wg = small("router_w", [P, DC, E], F32)
    tri = small("lower_index", [P, E, E], F32)
    half = small("minus_half", [P, IT], F32)
    stats = small("ln_stats", [P, IT, 6], F32)
    mv = small("ln_mv", [P, IT, 2], F32)
    var = small("ln_var", [P, IT], F32)
    rstd = small("ln_rstd", [P, IT], F32)
    stats2 = small("ln2_stats", [P, IT, 6], F32)
    mv2 = small("ln2_mv", [P, IT, 2], F32)
    var2 = small("ln2_var", [P, IT], F32)
    rstd2 = small("ln2_rstd", [P, IT], F32)
    top = small("row_max", [P, IT], F32)
    bias = small("exp_bias", [P, IT], F32)
    total = small("exp_total", [P, IT], F32)
    inv = small("out_scale", [P, IT], F32)
    lg = small("router_logits", [P, IT, E], F32)
    lx = small("router_exps", [P, IT, E], F32)
    lm = small("router_max", [P, IT], F32)
    ls = small("router_sum", [P, IT], F32)
    li = small("router_inv", [P, IT], F32)

    assert small.at <= first_free

    x_d = io["x"].rearrange("(b i p) d -> b p i d", b=B, p=P)
    x2_d = mem["x2"].rearrange("(b i p) d -> b p i d", b=B, p=P)
    xn2_d = mem["xn2"].rearrange("(b i p) d -> b p i d", b=B, p=P)
    ctx_d = io["ctx"].rearrange("b (i p) d -> b p i d", p=P)
    ctxT_d = io["ctxT"].rearrange("b (c p) s -> b p c s", p=P)
    w_d = {k: io[k].rearrange("(c p) e -> p c e", p=P) for k in ("wq", "wk", "wv", "wo")}

    with ExitStack() as c:
        sem = lambda n: c.enter_context(nc.semaphore(n))
        ps_s = c.enter_context(nc.psum_tensor("ps_scores", [P, 2, 2 * S], F32))
        ps_t = c.enter_context(nc.psum_tensor("ps_transposed", [P, 2, 4, P], F32))
        ps_m = c.enter_context(nc.psum_tensor("ps_products", [P, 2, D], F32))
        x_in, res_in = sem("x_in"), sem("res_in")
        raw_in = {k: sem(k + "_raw_in") for k in ("wq", "wk", "wv", "wo")}
        ctxT_raw_in, ctx_raw_in, small_in = sem("ctxT_raw_in"), sem("ctx_raw_in"), sem("small_in")
        hi_in = {k: sem(k + "_hi_in") for k in ("wq", "wk", "wv", "wo")}
        ctxT_hi_in, ctx_hi_in = sem("ctxT_hi_in"), sem("ctx_hi_in")
        w_ready = {k: sem(k + "_ready") for k in ("wq", "wk", "wv", "wo")}
        ctxT_ready, ctx_ready = sem("ctxT_ready"), sem("ctx_ready")
        made, const_ready = sem("made"), sem("const_ready")
        var_ready, rstd_ready = sem("var_ready"), sem("rstd_ready")
        xn_ready, xn2_ready = sem("xn_ready"), sem("xn2_ready")
        x2_out, xn2_out = sem("x2_out"), sem("xn2_out")
        m_ready, m_hi, m_free = sem("m_ready"), sem("m_hi"), sem("m_free")
        t_ready, t_hi, t_free = sem("t_ready"), sem("t_hi"), sem("t_free")
        s_ready, bias_ready, p_ready = sem("s_ready"), sem("bias_ready"), sem("p_ready")
        lx_in, lx_ready = sem("router_shifted"), sem("router_exp_ready")
        gate_ready, step = sem("gate_ready"), sem("dve_step")
        block = c.enter_context(nc.Block())

        @block.sync
        def _(sp):
            sp.dma_start(x_t[:], x_d[0]).then_inc(x_in, 16)
            for k, t in (("wq", wq_raw), ("wk", wk_raw)):
                sp.dma_start(t[:], w_d[k]).then_inc(raw_in[k], 16)
            sp.dma_start(ctxT_raw[:], ctxT_d[0]).then_inc(ctxT_raw_in, 16)
            sp.dma_start(wv_raw[:], w_d["wv"]).then_inc(raw_in["wv"], 16)
            sp.dma_start(ctx_raw[:], ctx_d[0]).then_inc(ctx_raw_in, 16)
            sp.dma_start(wo_raw[:], w_d["wo"]).then_inc(raw_in["wo"], 16)
            sp.dma_start(wg[:], io["wg"].rearrange("(c p) e -> p c e", p=P)).then_inc(small_in, 16)
            sp.dma_start(gates[:, 0:1], io["gx"].partition_broadcast(P)).then_inc(small_in, 16)
            sp.dma_start(gates[:, 1:2], io["gf"].partition_broadcast(P)).then_inc(small_in, 16)
            sp.dma_start(r_t[:], x_d[0]).then_inc(res_in, 16)

            def stores(b):
                sp.wait_ge(m_free, b * 22 + 20)
                sp.dma_start(x2_d[b], r_t[:]).then_inc(x2_out, 16)
                sp.wait_ge(xn2_ready, b + 1)
                sp.dma_start(xn2_d[b], r_t[:]).then_inc(xn2_out, 16)

            with sp.Fori(1, B) as b:
                sp.wait_ge(t_ready, b * 16 - 12)
                sp.dma_start(x_t[:], x_d[b]).then_inc(x_in, 16)
                sp.wait_ge(s_ready, b * 4)
                sp.dma_start(ctxT_raw[:], ctxT_d[b]).then_inc(ctxT_raw_in, 16)
                sp.wait_ge(m_ready, b * 22 - 6)
                sp.dma_start(ctx_raw[:], ctx_d[b]).then_inc(ctx_raw_in, 16)
                stores(b - 1)
                sp.wait_ge(t_ready, b * 16 + 4)
                sp.wait_ge(xn2_out, b * 16)
                sp.dma_start(r_t[:], x_d[b]).then_inc(res_in, 16)
            stores(B - 1)
            sp.wait_ge(x2_out, 16 * B)
            sp.wait_ge(xn2_out, 16 * B)

        @block.gpsimd
        def _(pool):
            pool.dma_start(wq_hi[:], w_d["wq"]).then_inc(hi_in["wq"], 16)
            pool.dma_start(wk_hi[:], w_d["wk"]).then_inc(hi_in["wk"], 16)
            pool.memset(half[:], -0.5).then_inc(made, 1)
            pool.memset(keep["idle"][:, 2:5], 0.0).then_inc(made, 1)
            pool.memset(ident[:], 0.0).then_inc(made, 1)
            pool.memset(tri[:], 1.0).then_inc(made, 1)
            pool.wait_ge(made, 4)
            pool.affine_select(out=ident[:], in_=ident[:], compare_op=ALU.not_equal, fill=1.0, base=0,
                               pattern=[[-1, P]], channel_multiplier=1).then_inc(const_ready, 1)
            pool.affine_select(out=tri[:], in_=tri[:], compare_op=ALU.is_gt, fill=0.0, base=0,
                               pattern=[[1, E], [-1, E]], channel_multiplier=0).then_inc(const_ready, 1)
            pool.dma_start(ctxT_hi[:], ctxT_d[0]).then_inc(ctxT_hi_in, 16)
            pool.dma_start(wv_hi[:], w_d["wv"]).then_inc(hi_in["wv"], 16)
            pool.dma_start(ctx_hi[:], ctx_d[0]).then_inc(ctx_hi_in, 16)
            pool.dma_start(wo_hi[:], w_d["wo"]).then_inc(hi_in["wo"], 16)

            def root(v, r, n):
                pool.wait_ge(var_ready, n)
                pool.tensor_tensor(r[:], v[:], half[:], ALU.pow).then_inc(rstd_ready, 1)

            def low(hi, lo, raw, hi_sem, raw_sem, n, ready):
                pool.wait_ge(hi_sem, n)
                pool.wait_ge(raw_sem, n)
                pool.tensor_tensor(lo[:], raw[:], hi[:], ALU.subtract).then_inc(ready, 1)

            root(var, rstd, 1)
            low(wk_hi, wk_lo, wk_raw, hi_in["wk"], raw_in["wk"], 16, w_ready["wk"])
            low(ctxT_hi, ctxT_lo, ctxT_raw, ctxT_hi_in, ctxT_raw_in, 16, ctxT_ready)
            low(wv_hi, wv_lo, wv_raw, hi_in["wv"], raw_in["wv"], 16, w_ready["wv"])
            low(ctx_hi, ctx_lo, ctx_raw, ctx_hi_in, ctx_raw_in, 16, ctx_ready)
            low(wo_hi, wo_lo, wo_raw, hi_in["wo"], raw_in["wo"], 16, w_ready["wo"])
            with pool.Fori(1, B) as b:
                pool.wait_ge(s_ready, b * 4)
                pool.dma_start(ctxT_hi[:], ctxT_d[b]).then_inc(ctxT_hi_in, 16)
                root(var, rstd, b * 2)
                low(ctxT_hi, ctxT_lo, ctxT_raw, ctxT_hi_in, ctxT_raw_in, b * 16 + 16, ctxT_ready)
                pool.wait_ge(m_ready, b * 22 - 6)
                hold(nc, nc.gpsimd, keep)
                pool.dma_start(ctx_hi[:], ctx_d[b]).then_inc(ctx_hi_in, 16)
                root(var2, rstd2, b * 2 + 1)
                low(ctx_hi, ctx_lo, ctx_raw, ctx_hi_in, ctx_raw_in, b * 16 + 16, ctx_ready)
            root(var2, rstd2, 2 * B)

        @block.scalar
        def _(act):
            m, t, nexp = Count(), Count(), Count()
            act.wait_ge(small_in, 48)
            act.activation(gates[:], gates[:], ACT.Tanh).then_inc(gate_ready, 1)

            def high_m(out):
                act.wait_ge(m_ready, m.up())
                act.activation(out, ps_m[:, (m.n - 1) % 2, :], ACT.Copy).then_inc(m_hi, 1)

            def high_t(out):
                act.wait_ge(t_ready, t.up())
                act.activation(out, ps_t[:, (t.n - 1) % 2, :, :], ACT.Copy).then_inc(t_hi, 1)

            def exps(i):
                act.wait_ge(bias_ready, nexp.up())
                act.wait_ge(t_ready, t.now)
                act.activation(prob[:], ps_s[:, i % 2, :], ACT.Exp, bias=bias[:, i:i + 1], scale=SCALE,
                               accum_out=total[:, i:i + 1]).then_inc(p_ready, 1)

            def trans(i):
                for h in range(2):
                    high_t(pT_hi[:, 4 * h:4 * h + 4, i * P:(i + 1) * P])

            def attend(b):
                if b is not None:
                    for j in range(DC):
                        high_m(q_hi[:, j, :])
                for i in range(IT):
                    high_t(xnT_hi[:, :, i * P:(i + 1) * P])
                if b is not None:
                    m.up(4)
                for j in range(2 * DC):
                    high_m((q_hi if j < DC else k_hi)[:, j % DC, :])
                if b is not None:
                    t.up(4)
                    m.up(2)
                    router(b)
                exps(0)
                exps_then = [(1, 0), (2, 1), (3, 2)]
                for i, done in exps_then:
                    trans_wait = done
                    trans(trans_wait)
                    exps(i)
                for i in range(IT):
                    high_m(k_hi[:, i, :])
                trans(3)

            def router(b):
                act.wait_ge(lx_in, b)
                act.activation(lx[:], lx[:], ACT.Exp).then_inc(lx_ready, 1)

            attend(None)
            with act.Fori(1, B) as b:
                k = b - 1
                m.enter(k, 22), t.enter(k, 16), nexp.enter(k, 4)
                attend(b)
                m.leave(B - 1), t.leave(B - 1), nexp.leave(B - 1)
            for j in range(DC):
                high_m(q_hi[:, j, :])
            router(B)

        @block.vector
        def _(dve):
            m, t, s, steps = Count(), Count(), Count(), Count()
            hm, ht = Count(), Count()

            def then(ins):
                ins.then_inc(step, 1)
                dve.wait_ge(step, steps.up())

            def low_m(hi, lo):
                m.up()
                dve.wait_ge(m_hi, hm.up())
                dve.tensor_tensor(lo, ps_m[:, (m.n - 1) % 2, :], hi, ALU.subtract).then_inc(m_free, 1)

            def low_t(hi, lo):
                t.up()
                dve.wait_ge(t_hi, ht.up())
                dve.tensor_tensor(lo, ps_t[:, (t.n - 1) % 2, :, :], hi, ALU.subtract).then_inc(t_free, 1)

            def norm_stats(src, st, mean_var, v):
                for i in range(IT):
                    last = dve.bn_stats(st[:, i, :], src[:, i, :])
                then(last)
                hold(nc, nc.vector, keep)
                for i in range(IT):
                    last = dve.bn_aggr(mean_var[:, i, :], st[:, i, :])
                then(last)
                dve.tensor_scalar(v[:], mean_var[:, :, 1], EPS, None, ALU.add).then_inc(var_ready, 1)

            def norm_apply(src, mean_var, r, n, ready):
                dve.wait_ge(rstd_ready, n)
                for i in range(IT):
                    last = dve.tensor_scalar(src[:, i, :], src[:, i, :], mean_var[:, i, 0:1], r[:, i:i + 1],
                                             ALU.subtract, ALU.mult)
                last.then_inc(ready, 1)

            def maxima(i):
                dve.wait_ge(s_ready, s.up())
                then(dve.tensor_reduce(top[:, i:i + 1], ps_s[:, i % 2, :], AX.X, ALU.max))
                dve.tensor_scalar(bias[:, i:i + 1], top[:, i:i + 1], -SCALE, None, ALU.mult).then_inc(bias_ready, 1)

            def trans(i):
                for h in range(2):
                    o = (slice(None), slice(4 * h, 4 * h + 4), slice(i * P, (i + 1) * P))
                    low_t(pT_hi[o], pT_lo[o])

            def residual(b):
                then(dve.reciprocal(inv[:], total[:]))
                then(dve.tensor_scalar(inv[:], inv[:], gates[:, 0:1], None, ALU.mult))
                dve.wait_ge(res_in, b * 16)
                for i in range(IT):
                    dve.wait_ge(m_ready, m.up())
                    ins = dve.scalar_tensor_tensor(out=r_t[:, i, :], in0=ps_m[:, (m.n - 1) % 2, :],
                                                   scalar=inv[:, i:i + 1], in1=r_t[:, i, :],
                                                   op0=ALU.mult, op1=ALU.add)
                    ins.then_inc(m_free, 1)
                dve.wait_ge(m_free, m.now)
                norm_stats(r_t, stats2, mv2, var2)

            def route(b):
                for i in range(IT):
                    dve.wait_ge(t_ready, t.up())
                    dve.tensor_copy(xn2T[:, :, i * P:(i + 1) * P], ps_t[:, (t.n - 1) % 2, :, :]).then_inc(t_free, 1)
                for h in range(2):
                    dve.wait_ge(m_ready, m.up())
                    ins = dve.tensor_copy(lg[:, 2 * h:2 * h + 2, :],
                                          ps_m[:, (m.n - 1) % 2, 0:2 * E].rearrange("p (i e) -> p i e", e=E))
                    ins.then_inc(m_free, 1)
                dve.wait_ge(m_free, m.now)
                then(dve.tensor_reduce(lm[:], lg[:], AX.X, ALU.max))
                dve.tensor_tensor(lx[:], lg[:], lm[:].unsqueeze(2).broadcast_to([P, IT, E]), ALU.subtract).then_inc(lx_in, 1)
                dve.wait_ge(lx_ready, b)
                then(dve.tensor_reduce(ls[:], lx[:], AX.X, ALU.add))
                then(dve.reciprocal(li[:], ls[:]))
                then(dve.tensor_tensor(lg[:], lx[:], li[:].unsqueeze(2).broadcast_to([P, IT, E]), ALU.mult))
                rows = slice(4 * B - 4, 4 * B) if b is B else bass.ds(b * 4 - 4, 4)
                dve.tensor_copy(probs[:, rows, :], lg[:])
                other = lg[:].unsqueeze(2).broadcast_to([P, IT, E, E])
                own = lg[:].unsqueeze(3).broadcast_to([P, IT, E, E])
                dve.tensor_tensor(above[:], other, own, ALU.is_gt)
                then(dve.tensor_tensor(level[:], other, own, ALU.is_equal))
                then(dve.tensor_tensor(level[:], level[:], tri[:].unsqueeze(1).broadcast_to([P, IT, E, E]), ALU.mult))
                then(dve.tensor_tensor(above[:], above[:], level[:], ALU.add))
                then(dve.tensor_reduce(ranks[:, rows, :], above[:], AX.X, ALU.add))

            def attend(b):
                if b is not None:
                    for j in range(DC):
                        low_m(q_hi[:, j, :], q_lo[:, j, :])
                for i in range(IT):
                    o = (slice(None), slice(None), slice(i * P, (i + 1) * P))
                    low_t(xnT_hi[o], xnT_lo[o])
                if b is not None:
                    residual(b)
                for j in range(2 * DC):
                    hi, lo = (q_hi, q_lo) if j < DC else (k_hi, k_lo)
                    low_m(hi[:, j % DC, :], lo[:, j % DC, :])
                    if j == 4 and b is not None:
                        dve.wait_ge(x2_out, b * 16)
                        norm_apply(r_t, mv2, rstd2, b * 2 + 1, xn2_ready)
                if b is not None:
                    route(b)
                maxima(0)
                for i in range(1, IT):
                    maxima(i)
                    trans(i - 1)
                for i in range(IT):
                    low_m(k_hi[:, i, :], k_lo[:, i, :])
                trans(IT - 1)

            dve.wait_ge(x_in, 16)
            norm_stats(x_t, stats, mv, var)
            dve.wait_ge(hi_in["wq"], 16)
            dve.wait_ge(raw_in["wq"], 16)
            dve.tensor_tensor(wq_lo[:], wq_raw[:], wq_hi[:], ALU.subtract).then_inc(w_ready["wq"], 1)
            norm_apply(x_t, mv, rstd, 1, xn_ready)
            dve.wait_ge(gate_ready, 1)
            dve.wait_ge(const_ready, 2)
            attend(None)
            with dve.Fori(1, B) as b:
                k = b - 1
                for cnt, per in ((m, 22), (t, 16), (s, 4), (steps, 18), (hm, 16), (ht, 12)):
                    cnt.enter(k, per)
                dve.wait_ge(x_in, b * 16 + 16)
                norm_stats(x_t, stats, mv, var)
                norm_apply(x_t, mv, rstd, b * 2, xn_ready)
                attend(b)
                for cnt in (m, t, s, steps, hm, ht):
                    cnt.leave(B - 1)
            for j in range(DC):
                low_m(q_hi[:, j, :], q_lo[:, j, :])
            residual(B)
            dve.wait_ge(x2_out, 16 * B)
            norm_apply(r_t, mv2, rstd2, 2 * B, xn2_ready)
            route(B)

        @block.tensor
        def _(pe):
            m, t, s = Count(), Count(), Count()

            def product(pairs, wide=None):
                m.up()
                if not isinstance(m.now, int) or m.now > 2:
                    pe.wait_ge(m_free, m.now - 2)
                tripled(pe, ps_m[:, (m.n - 1) % 2, :], pairs).then_inc(m_ready, 1)

            def transpose(tiles):
                t.up()
                if not isinstance(t.now, int) or t.now > 2:
                    pe.wait_ge(t_free, t.now - 2)
                for j, block_in in enumerate(tiles):
                    last = pe.transpose(ps_t[:, (t.n - 1) % 2, j, :], block_in, ident[:])
                last.then_inc(t_ready, 1)

            def cols(x, c, i):
                return x[0][:, c, i * P:(i + 1) * P], x[1][:, c, i * P:(i + 1) * P]

            def chunk(x, c):
                return x[0][:, c, :], x[1][:, c, :]

            xnT, q, kk, pT = (xnT_hi, xnT_lo), (q_hi, q_lo), (k_hi, k_lo), (pT_hi, pT_lo)
            wq, wk, wv, wo = (wq_hi, wq_lo), (wk_hi, wk_lo), (wv_hi, wv_lo), (wo_hi, wo_lo)
            ctxT, ctx = (ctxT_hi, ctxT_lo), (ctx_hi, ctx_lo)

            def values():
                for j in range(DC):
                    product([(cols(ctx, c, j), chunk(pT, c)) for c in range(IT)]
                            + [(cols(kk, c, j), chunk(pT, IT + c)) for c in range(IT)])

            def project():
                pe.wait_ge(m_free, m.now)
                for i in range(IT):
                    product([(cols(q, c, i), chunk(wo, c)) for c in range(DC)])

            def router(b):
                pe.wait_ge(xn2_ready, b)
                for i in range(IT):
                    transpose([r_t[:, i, c * P:(c + 1) * P] for c in range(DC)])
                pe.wait_ge(t_free, t.now)
                for h in range(2):
                    m.up()
                    pe.wait_ge(m_free, m.now - 2)
                    for i in range(2):
                        for c in range(DC):
                            n = 2 * h + i
                            last = pe.matmul(ps_m[:, (m.n - 1) % 2, i * E:(i + 1) * E],
                                             xn2T[:, c, n * P:(n + 1) * P], wg[:, c, :],
                                             start=(c == 0), stop=(c == DC - 1))
                    last.then_inc(m_ready, 1)

            def attend(b):
                if b is None:
                    pe.wait_ge(const_ready, 2)
                    pe.wait_ge(xn_ready, 1)
                else:
                    pe.wait_ge(t_free, t.now)
                    pe.wait_ge(ctx_ready, b)
                    values()
                    pe.wait_ge(xn_ready, b + 1)
                for i in range(IT):
                    transpose([x_t[:, i, c * P:(c + 1) * P] for c in range(DC)])
                if b is not None:
                    project()
                pe.wait_ge(t_free, t.now)
                for w, name in ((wq, "wq"), (wk, "wk")):
                    if b is None:
                        pe.wait_ge(w_ready[name], 1)
                    for j in range(DC):
                        product([(cols(w, c, j), chunk(xnT, c)) for c in range(DC)])
                qk = m.now
                if b is not None:
                    router(b)
                pe.wait_ge(m_free, qk)
                pe.wait_ge(ctxT_ready, 1 if b is None else b + 1)

                def scores(i):
                    s.up()
                    if b is not None or i > 1:
                        pe.wait_ge(p_ready, s.now - 2)
                    tripled(pe, ps_s[:, i % 2, 0:S], [(cols(q, c, i), chunk(ctxT, c)) for c in range(DC)])
                    tripled(pe, ps_s[:, i % 2, S:2 * S],
                            [(cols(q, c, i), chunk(kk, c)) for c in range(DC)]).then_inc(s_ready, 1)

                def turn(i):
                    pe.wait_ge(p_ready, s.base + i + 1)
                    for h in range(2):
                        transpose([prob[:, (4 * h + n) * P:(4 * h + n + 1) * P] for n in range(4)])

                scores(0)
                for i in range(1, IT):
                    scores(i)
                    turn(i - 1)
                if b is None:
                    pe.wait_ge(w_ready["wv"], 1)
                for i in range(IT):
                    product([(cols(xnT, c, i), chunk(wv, c)) for c in range(DC)])
                turn(IT - 1)

            attend(None)
            pe.wait_ge(w_ready["wo"], 1)
            pe.wait_ge(small_in, 48)
            with pe.Fori(1, B) as b:
                k = b - 1
                m.enter(k, 22), t.enter(k, 16), s.enter(k, 4)
                attend(b)
                m.leave(B - 1), t.leave(B - 1), s.leave(B - 1)
            pe.wait_ge(t_free, t.now)
            pe.wait_ge(m_free, m.now)
            pe.wait_ge(ctx_ready, B)
            values()
            project()
            router(B)


def persistent(nc):
    small = Sbuf(nc, -(-nc.sbuf_base // 32) * 32)
    keep = {}
    keep["ident"] = small("ident", [P, P], F32)
    keep["probs"] = small("probs", [P, NT, E], F32)
    keep["ranks"] = small("ranks", [P, NT, E], F32)
    keep["gates"] = small("gates", [P, 2], F32)
    keep["idle"] = small("idle", [P, 8], F32)
    keep["weights"] = small("combine_weights", [P, NT, TOPK], F32)
    keep["slots"] = small("token_slots", [P, NT, TOPK], I32)
    keep["index"] = small("slot_tokens", [P, TILES_MAX + 2], I32)
    keep["ends"] = small("expert_ends", [P, E], I32)
    keep["pairs"] = small("last_pair", [P, 1], I32)
    keep["of_tile"] = small("tile_expert", [P, TILES_MAX], I32)
    keep["at_tile"] = small("tile_weights_at", [P, TILES_MAX], I32)
    keep["fetch"] = small("tile_fetches", [P, TILES_MAX], I32)
    keep["lower"] = small("tile_splits", [P, TILES_MAX], I32)
    keep["phase_at"] = small.at
    keep["end"] = keep["phase_at"] + PHASE_SMALL
    return keep


W13 = 2 * DC * FF
W2 = 2 * D
WE = W13 + W2 + D


PHASE_SMALL = 5 * 1024


class Later:

    def __init__(self, nc, first_free):
        sb = Sbuf(nc, first_free)
        self.u_hi, self.u_lo, self.u_raw = sb.split("shared_up", [P, 2, DC, SF])
        self.d_hi, self.d_lo, self.d_raw = sb.split("shared_down", [P, SC, D])
        self.we_at = sb.at
        self.w_hi, self.w_lo, self.w_raw = sb.split("expert", [P, 2 * WE])
        self.rest_at = sb.at


class Shared:

    def __init__(self, nc, c, io, mem, keep, later, tag):
        sem = lambda n: c.enter_context(nc.semaphore(tag + n))
        sb = Sbuf(nc, later.rest_at)
        self.keep, self.later, self.mem = keep, later, mem
        self.xs = sb(tag + "xs", [P, 2, D], F32)
        self.x = sb(tag + "xT_hi", [P, DC, S], F32R), sb(tag + "xT_lo", [P, DC, S], F32R)
        self.h = sb(tag + "h_hi", [P, SC, S], F32R), sb(tag + "h_lo", [P, SC, S], F32R)
        self.gate = sb(tag + "silu", [P, 2, S], F32)
        self.hf = sb(tag + "h", [P, 2, S], F32)
        self.acc = sb(tag + "acc", [P, 2, D], F32)
        self.end = sb.at
        assert sb.at <= nc.sbuf_usable_end, sb.at
        psum = lambda n, shape: c.enter_context(nc.psum_tensor(tag + n, shape, F32))
        self.ps_t = psum("ps_t", [P, 2, 4, P])
        self.ps_u = psum("ps_u", [P, 2, 2, S])
        self.ps_y = psum("ps_y", [P, 2, D])
        self.xs_in, self.acc_in = [sem("xs0_in"), sem("xs1_in")], [sem("acc0_in"), sem("acc1_in")]
        self.out = [sem("acc0_out"), sem("acc1_out")]
        self.t_ready, self.t_hi, self.t_free = sem("t_ready"), sem("t_hi"), sem("t_free")
        self.u_ready, self.gate_ready, self.u_free = sem("u_ready"), sem("gate_ready"), sem("u_free")
        self.h_hi, self.h_lo = sem("h_hi"), sem("h_lo")
        self.y_ready, self.y_free = sem("y_ready"), sem("y_free")
        self.xn2 = mem["xn2"].rearrange("(n p) d -> n p d", p=P)
        self.x2 = mem["x2"].rearrange("(n p) d -> n p d", p=P)
        self.base = mem["base"].rearrange("(n p) d -> n p d", p=P)

    def rows(self, sp, n, b, i):
        if n * IT + i >= 2:
            sp.wait_ge(self.t_ready, n * IT + i - 1)
        sp.dma_start(self.xs[:, i % 2, :], self.xn2[b * IT + i]).then_inc(self.xs_in[i % 2], 16)

    def residual(self, sp, n, b, i):
        sp.dma_start(self.acc[:, i % 2, :], self.x2[b * IT + i]).then_inc(self.acc_in[i % 2], 16)

    def store(self, sp, n, b, i):
        sp.wait_ge(self.y_free, n * IT + i + 1)
        sp.dma_start(self.base[b * IT + i], self.acc[:, i % 2, :]).then_inc(self.out[i % 2], 16)
        sp.wait_ge(self.out[i % 2], n * 32 + (i // 2) * 16 + 16)

    def sync(self, sp, n, b, more):
        if not n:
            self.rows(sp, n, b, 0), self.rows(sp, n, b, 1)
        self.rows(sp, n, b, 2), self.rows(sp, n, b, 3)
        self.residual(sp, n, b, 0), self.residual(sp, n, b, 1)
        if more:
            self.rows(sp, n + 1, b + 1, 0), self.rows(sp, n + 1, b + 1, 1)
        for i in range(IT):
            self.store(sp, n, b, i)
            if i < 2:
                self.residual(sp, n, b, i + 2)

    def tensor(self, pe, n, up_ready=lambda: None, down_ready=lambda: None):
        later = self.later
        x, h, up, down = self.x, self.h, (later.u_hi, later.u_lo), (later.d_hi, later.d_lo)
        first = n == 0
        for i in range(IT):
            if i >= 2 or not first:
                pe.wait_ge(self.t_free, n * IT + i - 1)
            pe.wait_ge(self.xs_in[i % 2], n * 32 + (i // 2) * 16 + 16)
            for c in range(DC):
                last = pe.transpose(self.ps_t[:, i % 2, c, :], self.xs[:, i % 2, c * P:(c + 1) * P],
                                    self.keep["ident"][:])
            last.then_inc(self.t_ready, 1)
        pe.wait_ge(self.t_free, n * IT + IT)
        up_ready()
        for j in range(SC):
            if j >= 2 or not first:
                pe.wait_ge(self.u_free, n * SC + j - 1)
            rows = P if j < SC - 1 else ST
            for k in range(2):
                pairs = [([w[:, k, c, j * P:j * P + rows] for w in up], [v[:, c, :] for v in x])
                         for c in range(DC)]
                last = tripled(pe, self.ps_u[0:rows, j % 2, k, :], pairs)
            last.then_inc(self.u_ready, 1)
        pe.wait_ge(self.h_lo, n * SC + SC)
        down_ready()
        for i in range(IT):
            if i >= 2 or not first:
                pe.wait_ge(self.y_free, n * IT + i - 1)
            pairs = []
            for j in range(SC):
                rows = P if j < SC - 1 else ST
                pairs.append(([v[0:rows, j, i * P:(i + 1) * P] for v in h], [w[0:rows, j, :] for w in down]))
            tripled(pe, self.ps_y[:, i % 2, :], pairs).then_inc(self.y_ready, 1)

    def scalar(self, act, n):
        for i in range(IT):
            act.wait_ge(self.t_ready, n * IT + i + 1)
            act.activation(self.x[0][:, :, i * P:(i + 1) * P], self.ps_t[:, i % 2, :, :], ACT.Copy).then_inc(self.t_hi, 1)

        def high(j):
            rows = P if j < SC - 1 else ST
            act.wait_ge(self.u_free, n * SC + j + 1)
            act.activation(self.h[0][0:rows, j, :], self.hf[0:rows, j % 2, :], ACT.Copy).then_inc(self.h_hi, 1)

        for j in range(SC):
            rows = P if j < SC - 1 else ST
            act.wait_ge(self.u_ready, n * SC + j + 1)
            act.activation(self.gate[0:rows, j % 2, :], self.ps_u[0:rows, j % 2, 0, :], ACT.Silu).then_inc(self.gate_ready, 1)
            if j:
                high(j - 1)
        high(SC - 1)

    def vector(self, dve, n, between=lambda j: None):
        for i in range(IT):
            o = (slice(None), slice(None), slice(i * P, (i + 1) * P))
            dve.wait_ge(self.t_hi, n * IT + i + 1)
            dve.tensor_tensor(self.x[1][o], self.ps_t[:, i % 2, :, :], self.x[0][o], ALU.subtract).then_inc(self.t_free, 1)

        def low(j):
            rows = P if j < SC - 1 else ST
            dve.wait_ge(self.h_hi, n * SC + j + 1)
            dve.tensor_tensor(self.h[1][0:rows, j, :], self.hf[0:rows, j % 2, :], self.h[0][0:rows, j, :],
                              ALU.subtract).then_inc(self.h_lo, 1)

        for j in range(SC):
            rows = P if j < SC - 1 else ST
            dve.wait_ge(self.gate_ready, n * SC + j + 1)
            if n * SC + j >= 2:
                dve.wait_ge(self.h_lo, n * SC + j - 1)
            dve.tensor_tensor(self.hf[0:rows, j % 2, :], self.ps_u[0:rows, j % 2, 1, :], self.gate[0:rows, j % 2, :],
                              ALU.mult).then_inc(self.u_free, 1)
            if j:
                low(j - 1)
            between(j)
        low(SC - 1)
        for i in range(IT):
            dve.wait_ge(self.y_ready, n * IT + i + 1)
            dve.wait_ge(self.acc_in[i % 2], n * 32 + (i // 2) * 16 + 16)
            dve.scalar_tensor_tensor(out=self.acc[:, i % 2, :], in0=self.ps_y[:, i % 2, :],
                                     scalar=self.keep["gates"][:, 1:2], in1=self.acc[:, i % 2, :],
                                     op0=ALU.mult, op1=ALU.add).then_inc(self.y_free, 1)


def expert_parts(io):
    w13 = io["w13"].rearrange("e m (c p) f -> m e p c f", p=P)
    w2a = io["w2"][:, 0:2 * P, :].rearrange("e (c p) d -> e p c d", p=P)
    w2b = io["w2"][:, 2 * P:FF, :]
    return w13, w2a, w2b


def load_expert(eng, w, base, io, e, sem):
    w13, w2a, w2b = expert_parts(io)

    def cols(rows, start, n):
        return w[0:rows, start:start + n] if isinstance(base, int) else w[0:rows, bass.ds(base + start, n)]

    base0 = base if isinstance(base, int) else 0
    for m in range(2):
        eng.dma_start(cols(P, base0 + m * DC * FF, DC * FF).rearrange("p (c f) -> p c f", c=DC), w13[m][e]).then_inc(sem, 16)
    eng.dma_start(cols(P, base0 + W13, W2).rearrange("p (c d) -> p c d", c=2), w2a[e]).then_inc(sem, 16)
    eng.dma_start(cols(FT, base0 + W13 + W2, D), w2b[e]).then_inc(sem, 16)


def split_expert(eng, later, base, sem):
    def cols(w, rows, start, n):
        return w[0:rows, start:start + n] if isinstance(base, int) else w[0:rows, bass.ds(base + start, n)]

    base0 = base if isinstance(base, int) else 0
    for rows, start, n, last in ((P, base0, W13 + W2, False), (FT, base0 + W13 + W2, D, True)):
        hi, lo, raw = (cols(w, rows, start, n) for w in (later.w_hi, later.w_lo, later.w_raw))
        ins = eng.tensor_tensor(lo, raw, hi, ALU.subtract)
        if last:
            ins.then_inc(sem, 1)


def routing_phase(nc, io, mem, keep, later):
    with ExitStack() as c:
        sh = Shared(nc, c, io, mem, keep, later, "b_")
        sem = lambda n: c.enter_context(nc.semaphore("b_" + n))
        over = Sbuf(nc, later.we_at + 4 * WE)
        row_hot = over("slot_hot", [P, NT * TOPK, P], F16)
        assert over.at <= later.we_at + 8 * WE
        over = Sbuf(nc, later.we_at + 12 * WE)
        tile_hot = over("tile_hot", [P, NT * TOPK, TILES_MAX], F16)
        f = {k: over("r_" + k, [P, NT, E], F32) for k in ("within", "totals", "s0", "s1", "slot", "one")}
        assert over.at <= later.we_at + 16 * WE
        small = Sbuf(nc, keep["phase_at"])
        mask, strict, ones = small("mask", [P, NT * E], F16), small("strict", [P, P], F16), small("ones", [P, P], F16)
        lane, lane_i = small("lane", [P, P], F32), small("lane_i", [P, P], I32)
        token, token_i = small("token", [P, NT], F32), small("token_i", [P, NT], I32)
        e_f = {k: small("e_" + k, [P, E], F32) for k in ("n", "tiles", "c0", "c1", "base", "first", "last", "fetch", "lower")}
        e_i = small("e_int", [P, E], I32)
        odd = small("odd", [P, 1], I32)
        odd_f = small("odd_f", [P, 1], F32)
        hi_i, lo_i = small("tile_no_i", [P, NT * TOPK], I32), small("row_no_i", [P, NT * TOPK], I32)
        tile_no, row_no = small("tile_no", [P, NT * TOPK], F32), small("row_no", [P, NT * TOPK], F32)
        slot_f = small("slot_f", [P, NT, TOPK], F32)
        t_f = small("per_tile", [P, TILES_MAX], F32)
        assert small.at <= keep["end"], small.at
        grid = Sbuf(nc, sh.end)("grid", [P, TILES_MAX, E], F32)

        raw_in = {k: sem(k + "_raw_in") for k in ("up", "down", "first")}
        hi_in = {k: sem(k + "_hi_in") for k in ("up", "down", "first")}
        w_ready = {k: sem(k + "_ready") for k in ("up", "down")}
        first_ready = keep["first_ready"]
        mask_ready, made, const_ready = sem("mask_ready"), sem("made"), sem("const_ready")
        counted, taken = sem("counted"), sem("counts_taken")
        hot_ready, listed = sem("hot_ready"), sem("listed")
        step = sem("dve_step")
        block = c.enter_context(nc.Block())
        down = io["w2s"][0:(SC - 1) * P, :].rearrange("(c p) d -> p c d", p=P)
        down_rest = io["w2s"][(SC - 1) * P:SF, :]
        up = io["w13s"].rearrange("m (c p) f -> m p c f", p=P)

        @block.sync
        def _(sp):
            for k in range(2):
                sp.dma_start(later.u_raw[:, k, :, :], up[k]).then_inc(raw_in["up"], 16)
            sp.dma_start(later.d_raw[:, 0:SC - 1, :], down).then_inc(raw_in["down"], 16)
            sp.dma_start(later.d_raw[0:ST, SC - 1, :], down_rest).then_inc(raw_in["down"], 16)
            load_expert(sp, later.w_raw, 0, io, 0, raw_in["first"])
            sh.sync(sp, 0, 0, True)
            sh.sync(sp, 1, 1, False)

        @block.gpsimd
        def _(pool):
            for k in range(2):
                pool.dma_start(later.u_hi[:, k, :, :], up[k]).then_inc(hi_in["up"], 16)
            pool.dma_start(later.d_hi[:, 0:SC - 1, :], down).then_inc(hi_in["down"], 16)
            pool.dma_start(later.d_hi[0:ST, SC - 1, :], down_rest).then_inc(hi_in["down"], 16)
            pool.memset(strict[:], 1.0).then_inc(made, 1)
            pool.memset(ones[:], 1.0).then_inc(made, 1)
            pool.iota(lane_i[:], [[1, P]], base=0, channel_multiplier=0).then_inc(made, 1)
            pool.iota(token_i[:], [[P, NT]], base=0, channel_multiplier=1).then_inc(made, 1)
            pool.wait_ge(made, 4)
            pool.affine_select(out=strict[:], in_=strict[:], compare_op=ALU.is_gt, fill=0.0, base=0,
                               pattern=[[1, P]], channel_multiplier=-1).then_inc(const_ready, 1)
            pool.tensor_copy(lane[:], lane_i[:]).then_inc(const_ready, 1)
            pool.tensor_copy(token[:], token_i[:]).then_inc(const_ready, 1)
            load_expert(pool, later.w_hi, 0, io, 0, hi_in["first"])
            pool.wait_ge(hi_in["up"], 32)
            pool.wait_ge(raw_in["up"], 32)
            for k in range(2):
                pool.tensor_tensor(later.u_lo[:, k, :, :], later.u_raw[:, k, :, :], later.u_hi[:, k, :, :],
                                   ALU.subtract).then_inc(w_ready["up"], 1)
            pool.wait_ge(hi_in["down"], 32)
            pool.wait_ge(raw_in["down"], 32)
            for a, r in ((slice(0, SC - 1), P), (slice(SC - 1, SC), ST)):
                pool.tensor_tensor(later.d_lo[0:r, a, :], later.d_raw[0:r, a, :], later.d_hi[0:r, a, :],
                                   ALU.subtract).then_inc(w_ready["down"], 1)
            pool.wait_ge(hi_in["first"], 64)
            pool.wait_ge(raw_in["first"], 64)
            split_expert(pool, later, 0, first_ready)

        @block.scalar
        def _(act):
            sh.scalar(act, 0)
            sh.scalar(act, 1)

        @block.vector
        def _(dve):
            steps = Count()
            ps_c = sh.ps_y

            def then(ins):
                ins.then_inc(step, 1)
                dve.wait_ge(step, steps.up())

            def running(src, a, b, n, cut):
                d = 1
                then(dve.tensor_copy(a[:], src))
                while d < n:
                    dve.tensor_copy(cut(b, 0, d), cut(a, 0, d))
                    then(dve.tensor_tensor(cut(b, d, n), cut(a, d, n), cut(a, 0, n - d), ALU.add))
                    a, b, d = b, a, 2 * d
                return a

            def count():
                incl = running(f["totals"][:], f["s0"], f["s1"], NT, lambda x, p, q: x[:, p:q, :])
                then(dve.tensor_copy(e_i[:], incl[:, NT - 1, :]))
                then(dve.tensor_tensor(f["slot"][:], incl[:], f["totals"][:], ALU.subtract))
                then(dve.tensor_tensor(f["slot"][:], f["slot"][:], f["within"][:], ALU.add))
                then(dve.tensor_scalar(e_i[:], e_i[:], P - 1, None, ALU.add))
                then(dve.tensor_scalar(e_i[:], e_i[:], P.bit_length() - 1, None, ALU.logical_shift_right))
                then(dve.tensor_scalar(e_f["tiles"][:], e_i[:], 1.0, None, ALU.max))
                cum = running(e_f["tiles"][:], e_f["c0"], e_f["c1"], E, lambda x, p, q: x[:, p:q])
                then(dve.tensor_tensor(e_f["first"][:], cum[:], e_f["tiles"][:], ALU.subtract))
                then(dve.tensor_scalar(e_f["base"][:], e_f["first"][:], float(P), None, ALU.mult))
                then(dve.tensor_tensor(f["slot"][:], f["slot"][:],
                                       e_f["base"][:].unsqueeze(1).broadcast_to([P, NT, E]), ALU.add))
                keep["cum"] = cum

            def choose(ks):
                for k in ks:
                    for what, out in ((f["slot"], slot_f), (keep["probs"], keep["weights"])):
                        then(dve.scalar_tensor_tensor(out=f["one"][:], in0=keep["ranks"][:], scalar=float(k),
                                                      in1=what[:], op0=ALU.is_equal, op1=ALU.mult))
                        then(dve.tensor_reduce(out[:, :, k], f["one"][:], AX.X, ALU.add))

            def number():
                then(dve.tensor_scalar(keep["weights"][:], keep["weights"][:], keep["gates"][:, 1:2], None, ALU.mult))
                then(dve.tensor_copy(keep["slots"][:], slot_f[:]))
                flat = keep["slots"][:].rearrange("p j k -> p (j k)")
                dve.tensor_scalar(hi_i[:], flat, P.bit_length() - 1, None, ALU.logical_shift_right)
                then(dve.tensor_scalar(lo_i[:], flat, P - 1, None, ALU.bitwise_and))
                dve.tensor_copy(tile_no[:], hi_i[:])
                then(dve.tensor_copy(row_no[:], lo_i[:]))

            def one_hot(j):
                n = NT * TOPK
                for i in range(j * n // 5, (j + 1) * n // 5):
                    dve.tensor_scalar(row_hot[:, i, :], lane[:], row_no[:, i:i + 1], None, ALU.is_equal)
                    last = dve.tensor_scalar(tile_hot[:, i, :], lane[:, 0:TILES_MAX], tile_no[:, i:i + 1],
                                             token[:, i // TOPK:i // TOPK + 1], ALU.is_equal, ALU.mult)
                last.then_inc(hot_ready, 1)

            def per_tile(rows, op, out, last_e=E, plus=None):
                then(dve.tensor_tensor(grid[:, :, 0:last_e], lane[:, 0:TILES_MAX].unsqueeze(2).broadcast_to([P, TILES_MAX, last_e]),
                                       rows.unsqueeze(1).broadcast_to([P, TILES_MAX, last_e]), op))
                then(dve.tensor_reduce(t_f[:], grid[:, :, 0:last_e], AX.X, ALU.add))
                if plus is not None:
                    then(dve.tensor_scalar(t_f[:], t_f[:], float(E - 1), plus, ALU.min, ALU.add))
                then(dve.tensor_copy(out[:], t_f[:]))

            def schedule():
                cum = keep["cum"]
                then(dve.tensor_copy(odd[:], cum[:, E - 1:E]))
                then(dve.tensor_scalar(odd[:], odd[:], -1, None, ALU.add))
                then(dve.tensor_scalar(keep["pairs"][:], odd[:], 1, None, ALU.logical_shift_right))
                then(dve.tensor_copy(keep["ends"][:], cum[:]))
                per_tile(cum[:], ALU.is_ge, keep["of_tile"], plus=1.0)
                then(dve.tensor_scalar(keep["at_tile"][:], keep["of_tile"][:], 1, None, ALU.add))
                then(dve.tensor_scalar(keep["at_tile"][:], keep["at_tile"][:], 1, None, ALU.bitwise_and))
                then(dve.tensor_scalar(keep["at_tile"][:], keep["at_tile"][:], float(WE), None, ALU.mult))

            def schedule2():
                cum = keep["cum"]
                per_tile(e_f["first"][:, 1:E - 1], ALU.is_equal, keep["fetch"], E - 2)
                dve.tensor_scalar(e_f["last"][:], cum[:], -1.0, None, ALU.add)
                then(dve.tensor_scalar(e_f["lower"][:], e_f["first"][:], 2.0, None, ALU.add))
                then(dve.tensor_tensor(e_f["lower"][:], e_f["lower"][:], e_f["last"][:], ALU.min))
                per_tile(e_f["lower"][:, 0:E - 1], ALU.is_equal, keep["lower"], E - 1)

            dve.tensor_scalar(mask[:], keep["ranks"][:].rearrange("p j e -> p (j e)"), float(TOPK), None,
                              ALU.is_lt).then_inc(mask_ready, 1)
            dve.wait_ge(counted, 1)
            dve.tensor_copy(f["within"][:], ps_c[:, 0, 0:NT * E].rearrange("p (j e) -> p j e", e=E))
            dve.tensor_copy(f["totals"][:], ps_c[:, 1, 0:NT * E].rearrange("p (j e) -> p j e", e=E)).then_inc(taken, 1)
            dve.wait_ge(taken, 1)
            dve.wait_ge(const_ready, 3)
            work = [count, lambda: choose((0, 1)), lambda: (choose((2, 3)), number()), schedule, schedule2]
            sh.vector(dve, 0, lambda j: work[j]() if j < len(work) else None)
            sh.vector(dve, 1, lambda j: one_hot(j) if j < 5 else None)
            dve.wait_ge(listed, 1)
            then(dve.memset(keep["index"][:], 0))
            dve.tensor_copy(keep["index"][:, 0:TILES_MAX], sh.ps_t[:, 0, 0, 0:TILES_MAX]).then_inc(step, 1)
            dve.wait_ge(step, steps.up())

        @block.tensor
        def _(pe):
            pe.wait_ge(const_ready, 3)
            pe.wait_ge(mask_ready, 1)
            pe.matmul(sh.ps_y[:, 0, 0:NT * E], strict[:], mask[:], start=True, stop=True)
            pe.matmul(sh.ps_y[:, 1, 0:NT * E], ones[:], mask[:], start=True, stop=True).then_inc(counted, 1)
            pe.wait_ge(taken, 1)
            sh.tensor(pe, 0, lambda: pe.wait_ge(w_ready["up"], 2), lambda: pe.wait_ge(w_ready["down"], 2))
            sh.tensor(pe, 1)
            pe.wait_ge(hot_ready, 5)
            n = NT * TOPK
            for i in range(n):
                last = pe.matmul(sh.ps_t[:, 0, 0, 0:TILES_MAX], row_hot[:, i, :], tile_hot[:, i, :],
                                 start=(i == 0), stop=(i == n - 1))
            last.then_inc(listed, 1)


def expert_phase(nc, io, mem, keep, later):
    with ExitStack() as c:
        sem = lambda n: c.enter_context(nc.semaphore("c_" + n))
        sb = Sbuf(nc, later.rest_at)
        xg = [sb(f"xg{u}", [P, D], F32) for u in range(2)]
        x = [(sb(f"xT_hi{u}", [P, DC, P], F32R), sb(f"xT_lo{u}", [P, DC, P], F32R)) for u in range(2)]
        gate = [sb(f"gate{u}", [P, FF], F32) for u in range(2)]
        hf = [sb(f"hf{u}", [P, FF], F32) for u in range(2)]
        h = [(sb(f"hT_hi{u}", [P, FC, P], F32R), sb(f"hT_lo{u}", [P, FC, P], F32R)) for u in range(2)]
        y = [sb(f"y{u}", [P, D], F32) for u in range(2)]
        column = [sb(f"column{u}", [P, 1], I32) for u in range(2)]
        zeros = sb("zeros", [P, D], F32)
        assert sb.at <= nc.sbuf_usable_end, sb.at
        ps_u = c.enter_context(nc.psum_tensor("c_ps_u", [P, 2, 2, 512], F32))
        ps_x = c.enter_context(nc.psum_tensor("c_ps_x", [P, 4, P], F32))
        ps_h = c.enter_context(nc.psum_tensor("c_ps_h", [P, 4, P], F32))
        ps_y = c.enter_context(nc.psum_tensor("c_ps_y", [P, 2, D], F32))
        gathered = [sem("gathered0"), sem("gathered1")]
        x_turned, x_hi, x_split = sem("x_turned"), sem("x_hi"), sem("x_split")
        u_ready, gate_ready, h_ready = sem("u_ready"), sem("gate_ready"), sem("h_ready")
        h_turned, h_hi, h_split = sem("h_turned"), sem("h_hi"), sem("h_split")
        y_ready, y_taken = sem("y_ready"), sem("y_taken")
        y_out = sem("y_out")
        raw_in, hi_in, w_ready = sem("raw_in"), sem("hi_in"), keep["first_ready"]
        column_ready, zeros_ready, rest_out = sem("column_ready"), sem("zeros_ready"), sem("rest_out")
        block = c.enter_context(nc.Block())
        y_d = mem["y"].rearrange("(t p) d -> t p d", p=P)

        def number(eng, t, k, low, high):
            at = keep[k][0:1, t:t + 1] if isinstance(t, int) else keep[k][0:1, bass.ds(t, 1)]
            return eng.value_load(at, min_val=low, max_val=high)

        def wait(eng, s, value):
            if not isinstance(value, int) or value > 0:
                eng.wait_ge(s, value)

        def tiles(eng, step):
            step(0, 0)
            step(1, 1)
            last = number(eng, 0, "pairs", E // 2 - 1, TILES_MAX // 2 - 1)
            with eng.Fori(1, last + 1) as i:
                step(i * 2, 0)
                step(i * 2 + 1, 1)
            return last

        @block.sync
        def _(sp):
            load_expert(sp, later.w_raw, WE, io, 1, raw_in)
            with sp.Fori(1, E // 2) as i:
                for u in range(2):
                    sp.wait_ge(y_ready, number(sp, i * 2 + (u - 2), "ends", 1, TILES_MAX))
                    load_expert(sp, later.w_raw, u * WE, io, i * 2 + u, raw_in)
            sp.wait_ge(zeros_ready, 1)
            last = number(sp, 0, "pairs", E // 2 - 1, TILES_MAX // 2 - 1)
            with sp.Fori(0, REST) as t:
                sp.dma_start(y_d[last * 2 + 2 + t], zeros[:]).then_inc(rest_out, 16)
            sp.wait_ge(rest_out, REST * 16)

        @block.gpsimd
        def _(pool):
            load_expert(pool, later.w_hi, WE, io, 1, hi_in)

            def gather(t, u, column):
                pool.indirect_dma_start(xg[u][:], None, mem["xn2"],
                                        bass.IndirectOffsetOnAxis(ap=column, axis=0)).then_inc(gathered[u], 16)

            pool.memset(zeros[:], 0.0).then_inc(zeros_ready, 1)
            for u in range(2):
                gather(u, u, keep["index"][:, u:u + 1])

            def step(t, u):
                pool.wait_ge(gathered[u], (t + (2 - u)) * 8)
                pool.tensor_copy(column[u][:], keep["index"][:, t + 2:t + 3] if isinstance(t, int)
                                 else keep["index"][:, bass.ds(t + 2, 1)]).then_inc(column_ready, 1)
                pool.wait_ge(x_turned, t + 1)
                pool.wait_ge(column_ready, t + 1)
                hold(nc, nc.gpsimd, keep)
                gather(t, u, column[u][:])
                flag = number(pool, t, "fetch", 0, 1)
                with pool.If(flag == 1):
                    wait(pool, y_ready, t)
                    e = number(pool, t, "of_tile", 1, E - 1)
                    base = number(pool, t, "at_tile", 0, WE)
                    load_expert(pool, later.w_hi, WE - base, io, e, hi_in)
                with pool.Else():
                    pass

            pairs = tiles(pool, step)
            for u in range(2):
                pool.wait_ge(gathered[u], pairs * 16 + 16)

        @block.scalar
        def _(act):
            def turn(t, u):
                act.wait_ge(x_turned, t + 1)
                act.activation(x[u][0][:], ps_x[:], ACT.Copy).then_inc(x_hi, 1)

            def take(t, u):
                act.wait_ge(y_ready, t + 1)
                wait(act, y_out, t * 16)
                act.activation(y[u][:], ps_y[:, u, :], ACT.Copy).then_inc(y_taken, 1)
                act.wait_ge(y_taken, t + 1)
                act.dma_start(y_d[t], y[u][:]).then_inc(y_out, 16)

            def step(t, u):
                act.wait_ge(u_ready, t + 1)
                act.activation(gate[u][:], ps_u[:, u, 0, 0:FF], ACT.Silu).then_inc(gate_ready, 1)
                turn(t + 1, 1 - u)
                if not isinstance(t, int) or t > 0:
                    take(t - 1, 1 - u)
                act.wait_ge(h_turned, t + 1)
                act.activation(h[u][0][:, 0:2, :], ps_h[:, 0:2, :], ACT.Copy)
                act.activation(h[u][0][0:FT, 2, :], ps_h[0:FT, 2, :], ACT.Copy).then_inc(h_hi, 1)

            turn(0, 0)
            last = tiles(act, step)
            take(last * 2 + 1, 1)
            act.wait_ge(y_out, last * 32 + 32)
            hold(nc, nc.scalar, keep)

        @block.vector
        def _(dve):
            def turn(t, u):
                dve.wait_ge(x_hi, t + 1)
                dve.tensor_tensor(x[u][1][:], ps_x[:], x[u][0][:], ALU.subtract).then_inc(x_split, 1)

            def step(t, u):
                dve.wait_ge(gate_ready, t + 1)
                dve.tensor_tensor(hf[u][:], ps_u[:, u, 1, 0:FF], gate[u][:], ALU.mult).then_inc(h_ready, 1)
                turn(t + 1, 1 - u)
                dve.wait_ge(h_hi, t + 1)
                dve.tensor_tensor(h[u][1][:, 0:2, :], ps_h[:, 0:2, :], h[u][0][:, 0:2, :], ALU.subtract)
                dve.tensor_tensor(h[u][1][0:FT, 2, :], ps_h[0:FT, 2, :], h[u][0][0:FT, 2, :],
                                  ALU.subtract).then_inc(h_split, 1)
                flag = number(dve, t, "lower", 0, 1)
                with dve.If(flag == 1):
                    e = number(dve, t, "of_tile", 1, E)
                    base = number(dve, t, "at_tile", 0, WE)
                    dve.wait_ge(hi_in, e * 64)
                    dve.wait_ge(raw_in, e * 64)
                    hold(nc, nc.vector, keep)
                    split_expert(dve, later, WE - base, w_ready)
                with dve.Else():
                    pass

            turn(0, 0)
            tiles(dve, step)

        @block.tensor
        def _(pe):
            def turn(t, u):
                pe.wait_ge(gathered[u], (t + (2 - u)) * 8)
                wait(pe, x_split, t)
                for k in range(DC):
                    last = pe.transpose(ps_x[:, k, :], xg[u][:, k * P:(k + 1) * P], keep["ident"][:])
                last.then_inc(x_turned, 1)

            def weights(base, start, n, rows=P):
                if isinstance(base, int):
                    return [w[0:rows, base + start:base + start + n] for w in (later.w_hi, later.w_lo)]
                return [w[0:rows, bass.ds(base + start, n)] for w in (later.w_hi, later.w_lo)]

            def down(t, u, base):
                pe.wait_ge(h_split, t + 1)
                wait(pe, y_taken, t)
                pairs = []
                for j in range(FC):
                    rows = P if j < FC - 1 else FT
                    pairs.append(([v[0:rows, j, :] for v in h[u]], weights(base, W13 + j * D, D, rows)))
                tripled(pe, ps_y[:, u, :], pairs).then_inc(y_ready, 1)

            def step(t, u):
                e = number(pe, t, "of_tile", 1, E)
                base = number(pe, t, "at_tile", 0, WE)
                pe.wait_ge(x_split, t + 1)
                pe.wait_ge(w_ready, e)
                wait(pe, h_ready, t - 1)
                for k in range(2):
                    last = tripled(pe, ps_u[:, u, k, 0:FF], [
                        ([v[:, c_, :] for v in x[u]], weights(base, (k * DC + c_) * FF, FF)) for c_ in range(DC)])
                last.then_inc(u_ready, 1)
                turn(t + 1, 1 - u)
                if not isinstance(t, int) or t > 0:
                    down(t - 1, 1 - u, number(pe, t - 1, "at_tile", 0, WE))
                pe.wait_ge(h_ready, t + 1)
                wait(pe, h_split, t)
                for j in range(FC):
                    rows = P if j < FC - 1 else FT
                    last = pe.transpose(ps_h[0:rows, j, :], hf[u][:, j * P:j * P + rows], keep["ident"][:])
                last.then_inc(h_turned, 1)

            turn(0, 0)
            last = tiles(pe, step)
            down(last * 2 + 1, 1, number(pe, last * 2 + 1, "at_tile", 0, WE))


def combining_phase(nc, io, mem, keep, later, out):
    with ExitStack() as c:
        sh = Shared(nc, c, io, mem, keep, later, "d_")
        sem = lambda n: c.enter_context(nc.semaphore("d_" + n))
        over = Sbuf(nc, later.we_at)
        parts = [over(f"parts{u}", [P, TOPK, D], F32) for u in range(2)]
        total = [over(f"total{u}", [P, D], F32) for u in range(2)]
        assert over.at <= later.rest_at
        column = [over(f"d_column{u}", [P, TOPK], I32) for u in range(2)]
        parts_in, base_in, out_done = ([sem(f"{n}{u}") for u in range(2)] for n in ("parts_in", "base_in", "out_done"))
        summed, terms, column_ready = sem("summed"), sem("terms"), sem("column_ready")
        block = c.enter_context(nc.Block())
        out_d = out.rearrange("(n p) d -> n p d", p=P)
        base_d = mem["base"].rearrange("(n p) d -> n p d", p=P)

        @block.sync
        def _(sp):
            sh.sync(sp, 0, 2, True)
            sh.sync(sp, 1, 3, False)

        @block.gpsimd
        def _(pool):
            def fetch(k, u):
                if not isinstance(k, int) or k > 1:
                    pool.wait_ge(out_done[u], (k - u) * 8)
                pool.tensor_copy(column[u][:], keep["slots"][:, k, :] if isinstance(k, int)
                                 else keep["slots"][:, bass.ds(k, 1), :]).then_inc(column_ready, 1)
                pool.dma_start(total[u][:], base_d[k]).then_inc(base_in[u], 16)
                pool.wait_ge(column_ready, k + 1)
                hold(nc, nc.gpsimd, keep)
                for q in range(TOPK):
                    pool.indirect_dma_start(parts[u][:, q, :], None, mem["y"][0:TILES_MAX * P], bass.IndirectOffsetOnAxis(
                        ap=column[u][:, q:q + 1], axis=0)).then_inc(parts_in[u], 16)

            def store(k, u):
                pool.wait_ge(summed, k + 1)
                pool.dma_start(out_d[k], total[u][:]).then_inc(out_done[u], 16)

            def pairs(start, end):
                with pool.Fori(start, end) as i:
                    for u in range(2):
                        store(i * 2 + (u - 2), u)
                        fetch(i * 2 + u, u)

            fetch(0, 0)
            fetch(1, 1)
            pairs(1, NT // 4)
            for n in range(2):
                for u in range(2):
                    pool.wait_ge(sh.out[u], n * 32 + 32)
                pairs(NT // 4 + 2 * n, NT // 4 + 2 * n + 2)
            store(NT - 2, 0)
            store(NT - 1, 1)
            for u in range(2):
                pool.wait_ge(out_done[u], 8 * NT)

        @block.scalar
        def _(act):
            sh.scalar(act, 0)
            sh.scalar(act, 1)

        @block.vector
        def _(dve):
            def combine(k, u):
                dve.wait_ge(base_in[u], (k + (2 - u)) * 8)
                dve.wait_ge(parts_in[u], (k + (2 - u)) * 32)
                for q in range(TOPK):
                    w = keep["weights"][:, k, q:q + 1] if isinstance(k, int) else keep["weights"][:, bass.ds(k, 1), q]
                    ins = dve.scalar_tensor_tensor(out=total[u][:], in0=parts[u][:, q, :], scalar=w,
                                                   in1=total[u][:], op0=ALU.mult, op1=ALU.add)
                    if q < TOPK - 1:
                        ins.then_inc(terms, 1)
                        dve.wait_ge(terms, k * (TOPK - 1) + q + 1)
                    else:
                        ins.then_inc(summed, 1)

            sh.vector(dve, 0, lambda j: combine(j, j % 2))
            sh.vector(dve, 1, lambda j: combine(SC + j, j % 2))
            with dve.Fori(SC, NT // 2) as i:
                combine(i * 2, 0)
                combine(i * 2 + 1, 1)

        @block.tensor
        def _(pe):
            sh.tensor(pe, 0)
            sh.tensor(pe, 1)


def program(nc, io, out):
    mem = {k: nc.dram_tensor(k + "_dram", shape, F32, kind="Internal").ap() for k, shape in (
        ("x2", [T, D]), ("xn2", [T, D]), ("base", [T, D]), ("y", [(TILES_MAX + REST) * P, D]))}
    keep = persistent(nc)
    later = Later(nc, keep["end"])
    with nc.semaphore("expert_split") as first_ready:
        keep["first_ready"] = first_ready
        attention_phase(nc, io, mem, keep, keep["end"])
        routing_phase(nc, io, mem, keep, later)
        expert_phase(nc, io, mem, keep, later)
        combining_phase(nc, io, mem, keep, later, out)


def kernel(**inputs):
    import numpy as np
    from concourse import bacc
    from concourse.bass_utils import run_bass_kernel_spmd

    a = {k: np.asarray(v) for k, v in inputs.items()}
    arrays = {
        "x": a["x"].reshape(T, D),
        "ctx": a["ctx_2048"],
        "ctxT": a["ctx_2048"].transpose(0, 2, 1),
        "gx": a["g_xattn"],
        "gf": a["g_ffn"],
        "wg": a["L0_ffn_Wg"].T,
        "w13": np.stack([a["L0_ffn_W1"].transpose(0, 2, 1), a["L0_ffn_W3"].transpose(0, 2, 1)], axis=1),
        "w2": a["L0_ffn_W2"].transpose(0, 2, 1),
        "w13s": np.stack([a["L0_ffn_W1s"].T, a["L0_ffn_W3s"].T]),
        "w2s": a["L0_ffn_W2s"].T,
    }
    for k in ("wq", "wk", "wv", "wo"):
        arrays[k] = a["L0_xattn_" + k].T
    arrays = {k: np.ascontiguousarray(v) for k, v in arrays.items()}

    nc = bacc.Bacc("TRN2", target_bir_lowering=False, num_devices=1)
    io = {k: nc.dram_tensor(k, v.shape, mybir.dt.from_np(v.dtype), kind="ExternalInput").ap()
          for k, v in arrays.items()}
    out = nc.dram_tensor("out", (T, D), F32, kind="ExternalOutput").ap()
    program(nc, io, out)
    r = run_bass_kernel_spmd(nc, [arrays], core_ids=[0])
    return r.results[0]["out"].reshape(B, S, D)
```

```python
from contextlib import ExitStack

import concourse.bass as bass
from concourse import mybir

F32 = mybir.dt.float32
F32R = mybir.dt.float32r
F16 = mybir.dt.float16
I32 = mybir.dt.int32
ALU = mybir.AluOpType
ACT = mybir.ActivationFunctionType
AX = mybir.AxisListType

P = 128
B, S, D = 4, 512, 512
T = B * S
NT = T // P
IT = S // P
DC = D // P
KC = 2 * S // P
E, FF, TOPK = 16, 352, 4
FC = 3
FT = FF - 2 * P
SF = 704
SC = 6
ST = SF - 5 * P
TILES_MAX = 80
QUAD = 4
REST = TILES_MAX - T * TOPK // P
EPS = 1e-5
SCALE = float(D) ** -0.5


class Count:

    def __init__(self, start=0):
        self.base, self.n = start, 0

    def up(self, k=1):
        self.n += k
        return self.base + self.n

    @property
    def now(self):
        return self.base + self.n

    def enter(self, i, per):
        self.start, self.per = self.base + self.n, per
        self.base, self.n = i * per + self.start, 0

    def leave(self, passes):
        assert self.n == self.per, (self.n, self.per)
        self.base, self.n = self.start + passes * self.per, 0


def hold(nc, eng, keep, at=3):
    idle = keep["idle"]
    if eng is nc.vector:
        eng.memset(idle[:, 0:1], 0.0)
    elif eng is nc.scalar:
        eng.activation(idle[:, 1:2], idle[:, 2:3], ACT.Copy)
    else:
        eng.tensor_tensor(idle[:, at:at + 1], idle[:, 4:5], idle[:, 4:5], ALU.add)


TERMS = ((0, 0), (0, 1), (1, 0))


def tripled(pe, out, pairs, ahead=lambda c: None):
    n = 0
    for c, (a, b) in enumerate(pairs):
        ahead(c)
        for i, j in TERMS:
            last = pe.matmul(out, a[i], b[j], start=(n == 0), stop=(n == 3 * len(pairs) - 1))
            n += 1
    return last


class Sbuf:

    def __init__(self, nc, at):
        self.nc, self.at = nc, at

    def __call__(self, name, shape, dt):
        size = {F32: 4, F32R: 4, I32: 4, F16: 2}[dt]
        for n in shape[1:]:
            size *= n
        t = self.nc.alloc_sbuf_tensor_at(name, shape, dt, offset=self.at)
        self.at += -(-size // 32) * 32
        return t

    def split(self, name, shape):
        hi = self(name + "_hi", shape, F32R)
        at = self.at
        lo = self(name + "_lo", shape, F32R)
        end, self.at = self.at, at
        raw = self(name + "_raw", shape, F32)
        self.at = end
        return hi, lo, raw


def attention_phase(nc, io, mem, keep, later, first_free):
    sb = Sbuf(nc, first_free)
    wq_hi, wq_lo, wq_raw = sb.split("wq", [P, DC, D])
    wk_hi, wk_lo, wk_raw = sb.split("wk", [P, DC, D])
    wv_hi, wv_lo, wv_raw = sb.split("wv", [P, DC, D])
    wo_hi, wo_lo, wo_raw = sb.split("wo", [P, DC, D])
    ctxT_hi, ctxT_lo, ctxT_raw = sb.split("ctxT", [P, DC, S])
    ctx_hi, ctx_lo, ctx_raw = sb.split("ctx", [P, IT, D])
    xnT_hi, xnT_lo = sb("xnT_hi", [P, DC, S], F32R), sb("xnT_lo", [P, DC, S], F32R)
    q_hi, q_lo = sb("q_hi", [P, DC, S], F32R), sb("q_lo", [P, DC, S], F32R)
    k_hi, k_lo = sb("k_hi", [P, DC, S], F32R), sb("k_lo", [P, DC, S], F32R)
    prob = sb("prob", [P, 2 * S], F32)
    at = sb.at
    pT_hi, pT_lo = sb("pT_hi", [P, KC, S], F32R), sb("pT_lo", [P, KC, S], F32R)
    over = Sbuf(nc, at)
    xn2T = over("xn2T", [P, DC, S], F32)
    over = Sbuf(nc, at + 4 * KC * S)
    above = over("above", [P, IT, E, E], F32)
    level = over("level", [P, IT, E, E], F32)
    x_t = sb("x_t", [P, IT, D], F32)
    r_t = sb("r_t", [P, IT, D], F32)
    assert sb.at <= nc.sbuf_usable_end, sb.at

    ident, probs, ranks, gates = (keep[k] for k in ("ident", "probs", "ranks", "gates"))
    small = Sbuf(nc, keep["phase_at"])
    wg = small("router_w", [P, DC, E], F32)
    tri = small("lower_index", [P, E, E], F32)
    half = small("minus_half", [P, IT], F32)
    stats = small("ln_stats", [P, IT, 6], F32)
    mv = small("ln_mv", [P, IT, 2], F32)
    var = small("ln_var", [P, IT], F32)
    rstd = small("ln_rstd", [P, IT], F32)
    stats2 = small("ln2_stats", [P, IT, 6], F32)
    mv2 = small("ln2_mv", [P, IT, 2], F32)
    var2 = small("ln2_var", [P, IT], F32)
    rstd2 = small("ln2_rstd", [P, IT], F32)
    top = small("row_max", [P, IT], F32)
    bias = small("exp_bias", [P, IT], F32)
    total = small("exp_total", [P, IT], F32)
    inv = small("out_scale", [P, IT], F32)
    lg = small("router_logits", [P, IT, E], F32)
    lx = small("router_exps", [P, IT, E], F32)
    lm = small("router_max", [P, IT], F32)
    ls = small("router_sum", [P, IT], F32)
    li = small("router_inv", [P, IT], F32)

    assert small.at <= first_free

    x_d = io["x"].rearrange("(b i p) d -> b p i d", b=B, p=P)
    x2_d = mem["x2"].rearrange("(b i p) d -> b p i d", b=B, p=P)
    xn2_d = mem["xn2"].rearrange("(b i p) d -> b p i d", b=B, p=P)
    ctx_d, ctxT_d = io["ctx"], io["ctxT"]
    w_d = {k: io[k] for k in ("wq", "wk", "wv", "wo")}

    with ExitStack() as c:
        sem = lambda n: c.enter_context(nc.semaphore(n))
        ps_s = c.enter_context(nc.psum_tensor("ps_scores", [P, 2, 2 * S], F32))
        ps_t = c.enter_context(nc.psum_tensor("ps_transposed", [P, 2, 4, P], F32))
        ps_m = c.enter_context(nc.psum_tensor("ps_products", [P, 2, D], F32))
        x_in, res_in = sem("x_in"), sem("res_in")
        raw_in = {k: sem(k + "_raw_in") for k in ("wq", "wk", "wv", "wo")}
        ctxT_raw_in, ctx_raw_in, small_in = sem("ctxT_raw_in"), sem("ctx_raw_in"), sem("small_in")
        hi_in = {k: sem(k + "_hi_in") for k in ("wq", "wk", "wv", "wo")}
        ctxT_hi_in, ctx_hi_in = sem("ctxT_hi_in"), sem("ctx_hi_in")
        w_ready = {k: sem(k + "_ready") for k in ("wq", "wk", "wv", "wo")}
        ctxT_ready, ctx_ready = sem("ctxT_ready"), sem("ctx_ready")
        made, const_ready = sem("made"), sem("const_ready")
        var_ready, rstd_ready = sem("var_ready"), sem("rstd_ready")
        xn_ready, xn2_ready = sem("xn_ready"), sem("xn2_ready")
        x2_out, xn2_out = sem("x2_out"), sem("xn2_out")
        m_ready, m_hi, m_free = sem("m_ready"), sem("m_hi"), sem("m_free")
        t_ready, t_hi, t_free = sem("t_ready"), sem("t_hi"), sem("t_free")
        s_ready, bias_ready, p_ready = sem("s_ready"), sem("bias_ready"), sem("p_ready")
        lx_in, lx_ready = sem("router_shifted"), sem("router_exp_ready")
        gate_ready, step = sem("gate_ready"), sem("dve_step")
        block = c.enter_context(nc.Block())

        @block.sync
        def _(sp):
            sp.dma_start(x_t[:], x_d[0]).then_inc(x_in, 16)
            for k, t in (("wq", wq_raw), ("wk", wk_raw)):
                sp.dma_start(t[:], w_d[k]).then_inc(raw_in[k], 16)
            sp.dma_start(ctxT_raw[:], ctxT_d[0]).then_inc(ctxT_raw_in, 16)
            sp.dma_start(wv_raw[:], w_d["wv"]).then_inc(raw_in["wv"], 16)
            sp.dma_start(ctx_raw[:], ctx_d[0]).then_inc(ctx_raw_in, 16)
            sp.dma_start(wo_raw[:], w_d["wo"]).then_inc(raw_in["wo"], 16)
            sp.dma_start(wg[:], io["wg"]).then_inc(small_in, 16)
            sp.dma_start(gates[:, 0:1], io["gx"].partition_broadcast(P)).then_inc(small_in, 16)
            sp.dma_start(gates[:, 1:2], io["gf"].partition_broadcast(P)).then_inc(small_in, 16)
            sp.dma_start(r_t[:], x_d[0]).then_inc(res_in, 16)

            def stores(b):
                sp.wait_ge(m_free, b * 22 + 20)
                sp.dma_start(x2_d[b], r_t[:]).then_inc(x2_out, 16)
                sp.wait_ge(xn2_ready, b + 1)
                sp.dma_start(xn2_d[b], r_t[:]).then_inc(xn2_out, 16)

            with sp.Fori(1, B) as b:
                sp.wait_ge(t_ready, b * 16 - 12)
                sp.dma_start(x_t[:], x_d[b]).then_inc(x_in, 16)
                sp.wait_ge(s_ready, b * 4)
                sp.dma_start(ctxT_raw[:], ctxT_d[b]).then_inc(ctxT_raw_in, 16)
                sp.wait_ge(m_ready, b * 22 - 6)
                sp.dma_start(ctx_raw[:], ctx_d[b]).then_inc(ctx_raw_in, 16)
                stores(b - 1)
                sp.wait_ge(t_ready, b * 16 + 4)
                sp.wait_ge(xn2_out, b * 16)
                sp.dma_start(r_t[:], x_d[b]).then_inc(res_in, 16)
            sp.wait_ge(m_ready, 22 * B - 10)
            for k in range(2):
                sp.dma_start(later.u_raw[:, k, :, :], io["u"][:, k]).then_inc(keep["up_raw_in"][k], 16)
            stores(B - 1)
            sp.wait_ge(x2_out, 16 * B)
            sp.wait_ge(xn2_out, 16 * B)

        @block.gpsimd
        def _(pool):
            pool.dma_start(wq_hi[:], w_d["wq"]).then_inc(hi_in["wq"], 16)
            pool.dma_start(wk_hi[:], w_d["wk"]).then_inc(hi_in["wk"], 16)
            pool.memset(half[:], -0.5).then_inc(made, 1)
            pool.memset(keep["idle"][:, 2:5], 0.0).then_inc(made, 1)
            pool.memset(ident[:], 0.0).then_inc(made, 1)
            pool.memset(tri[:], 1.0).then_inc(made, 1)
            pool.wait_ge(made, 4)
            pool.affine_select(out=ident[:], in_=ident[:], compare_op=ALU.not_equal, fill=1.0, base=0,
                               pattern=[[-1, P]], channel_multiplier=1).then_inc(const_ready, 1)
            pool.affine_select(out=tri[:], in_=tri[:], compare_op=ALU.is_gt, fill=0.0, base=0,
                               pattern=[[1, E], [-1, E]], channel_multiplier=0).then_inc(const_ready, 1)
            pool.dma_start(ctxT_hi[:], ctxT_d[0]).then_inc(ctxT_hi_in, 16)
            pool.dma_start(wv_hi[:], w_d["wv"]).then_inc(hi_in["wv"], 16)
            pool.dma_start(ctx_hi[:], ctx_d[0]).then_inc(ctx_hi_in, 16)
            pool.dma_start(wo_hi[:], w_d["wo"]).then_inc(hi_in["wo"], 16)

            def root(v, r, n):
                pool.wait_ge(var_ready, n)
                pool.tensor_tensor(r[:], v[:], half[:], ALU.pow).then_inc(rstd_ready, 1)

            def low(hi, lo, raw, hi_sem, raw_sem, n, ready):
                pool.wait_ge(hi_sem, n)
                pool.wait_ge(raw_sem, n)
                pool.tensor_tensor(lo[:], raw[:], hi[:], ALU.subtract).then_inc(ready, 1)

            root(var, rstd, 1)
            low(wk_hi, wk_lo, wk_raw, hi_in["wk"], raw_in["wk"], 16, w_ready["wk"])
            low(ctxT_hi, ctxT_lo, ctxT_raw, ctxT_hi_in, ctxT_raw_in, 16, ctxT_ready)
            low(wv_hi, wv_lo, wv_raw, hi_in["wv"], raw_in["wv"], 16, w_ready["wv"])
            low(ctx_hi, ctx_lo, ctx_raw, ctx_hi_in, ctx_raw_in, 16, ctx_ready)
            low(wo_hi, wo_lo, wo_raw, hi_in["wo"], raw_in["wo"], 16, w_ready["wo"])
            with pool.Fori(1, B) as b:
                pool.wait_ge(s_ready, b * 4)
                pool.dma_start(ctxT_hi[:], ctxT_d[b]).then_inc(ctxT_hi_in, 16)
                root(var, rstd, b * 2)
                low(ctxT_hi, ctxT_lo, ctxT_raw, ctxT_hi_in, ctxT_raw_in, b * 16 + 16, ctxT_ready)
                pool.wait_ge(m_ready, b * 22 - 6)
                hold(nc, nc.gpsimd, keep)
                pool.dma_start(ctx_hi[:], ctx_d[b]).then_inc(ctx_hi_in, 16)
                root(var2, rstd2, b * 2 + 1)
                low(ctx_hi, ctx_lo, ctx_raw, ctx_hi_in, ctx_raw_in, b * 16 + 16, ctx_ready)
            pool.wait_ge(m_ready, 22 * B - 10)
            for k in range(2):
                pool.dma_start(later.u_hi[:, k, :, :], io["u"][:, k]).then_inc(keep["up_hi_in"][k], 16)

            def split_up(k):
                pool.wait_ge(keep["up_hi_in"][k], 16)
                pool.wait_ge(keep["up_raw_in"][k], 16)
                pool.tensor_tensor(later.u_lo[:, k, :, :], later.u_raw[:, k, :, :], later.u_hi[:, k, :, :],
                                   ALU.subtract).then_inc(keep["up_ready"], 1)

            split_up(0)
            root(var2, rstd2, 2 * B)
            split_up(1)

        @block.scalar
        def _(act):
            m, t, nexp = Count(), Count(), Count()
            act.wait_ge(small_in, 48)
            act.activation(gates[:], gates[:], ACT.Tanh).then_inc(gate_ready, 1)

            def high_m(out):
                act.wait_ge(m_ready, m.up())
                act.activation(out, ps_m[:, (m.n - 1) % 2, :], ACT.Copy).then_inc(m_hi, 1)

            def high_t(out):
                act.wait_ge(t_ready, t.up())
                act.activation(out, ps_t[:, (t.n - 1) % 2, :, :], ACT.Copy).then_inc(t_hi, 1)

            def exps(i):
                act.wait_ge(bias_ready, nexp.up())
                act.wait_ge(t_ready, t.now)
                act.activation(prob[:], ps_s[:, i % 2, :], ACT.Exp, bias=bias[:, i:i + 1], scale=SCALE,
                               accum_out=total[:, i:i + 1]).then_inc(p_ready, 1)

            def trans(i):
                for h in range(2):
                    high_t(pT_hi[:, 4 * h:4 * h + 4, i * P:(i + 1) * P])

            def attend(b):
                if b is not None:
                    for j in range(DC):
                        high_m(q_hi[:, j, :])
                for i in range(IT):
                    high_t(xnT_hi[:, :, i * P:(i + 1) * P])
                if b is not None:
                    m.up(4)
                for j in range(2 * DC):
                    high_m((q_hi if j < DC else k_hi)[:, j % DC, :])
                if b is not None:
                    t.up(4)
                    m.up(2)
                    router(b)
                exps(0)
                exps_then = [(1, 0), (2, 1), (3, 2)]
                for i, done in exps_then:
                    trans_wait = done
                    trans(trans_wait)
                    exps(i)
                for i in range(IT):
                    high_m(k_hi[:, i, :])
                trans(3)

            def router(b):
                act.wait_ge(lx_in, b)
                act.activation(lx[:], lx[:], ACT.Exp).then_inc(lx_ready, 1)

            attend(None)
            with act.Fori(1, B) as b:
                k = b - 1
                m.enter(k, 22), t.enter(k, 16), nexp.enter(k, 4)
                attend(b)
                m.leave(B - 1), t.leave(B - 1), nexp.leave(B - 1)
            for j in range(DC):
                high_m(q_hi[:, j, :])
            router(B)

        @block.vector
        def _(dve):
            m, t, s, steps = Count(), Count(), Count(), Count()
            hm, ht = Count(), Count()

            def then(ins):
                ins.then_inc(step, 1)
                dve.wait_ge(step, steps.up())

            def low_m(hi, lo):
                m.up()
                dve.wait_ge(m_hi, hm.up())
                dve.tensor_tensor(lo, ps_m[:, (m.n - 1) % 2, :], hi, ALU.subtract).then_inc(m_free, 1)

            def low_t(hi, lo):
                t.up()
                dve.wait_ge(t_hi, ht.up())
                dve.tensor_tensor(lo, ps_t[:, (t.n - 1) % 2, :, :], hi, ALU.subtract).then_inc(t_free, 1)

            def norm_stats(src, st, mean_var, v):
                for i in range(IT):
                    last = dve.bn_stats(st[:, i, :], src[:, i, :])
                then(last)
                hold(nc, nc.vector, keep)
                for i in range(IT):
                    last = dve.bn_aggr(mean_var[:, i, :], st[:, i, :])
                then(last)
                dve.tensor_scalar(v[:], mean_var[:, :, 1], EPS, None, ALU.add).then_inc(var_ready, 1)

            def norm_apply(src, mean_var, r, n, ready):
                dve.wait_ge(rstd_ready, n)
                for i in range(IT):
                    last = dve.tensor_scalar(src[:, i, :], src[:, i, :], mean_var[:, i, 0:1], r[:, i:i + 1],
                                             ALU.subtract, ALU.mult)
                last.then_inc(ready, 1)

            def maxima(i):
                dve.wait_ge(s_ready, s.up())
                then(dve.tensor_reduce(top[:, i:i + 1], ps_s[:, i % 2, :], AX.X, ALU.max))
                dve.tensor_scalar(bias[:, i:i + 1], top[:, i:i + 1], -SCALE, None, ALU.mult).then_inc(bias_ready, 1)

            def trans(i):
                for h in range(2):
                    o = (slice(None), slice(4 * h, 4 * h + 4), slice(i * P, (i + 1) * P))
                    low_t(pT_hi[o], pT_lo[o])

            def residual(b):
                then(dve.reciprocal(inv[:], total[:]))
                then(dve.tensor_scalar(inv[:], inv[:], gates[:, 0:1], None, ALU.mult))
                dve.wait_ge(res_in, b * 16)
                for i in range(IT):
                    dve.wait_ge(m_ready, m.up())
                    ins = dve.scalar_tensor_tensor(out=r_t[:, i, :], in0=ps_m[:, (m.n - 1) % 2, :],
                                                   scalar=inv[:, i:i + 1], in1=r_t[:, i, :],
                                                   op0=ALU.mult, op1=ALU.add)
                    ins.then_inc(m_free, 1)
                dve.wait_ge(m_free, m.now)
                norm_stats(r_t, stats2, mv2, var2)

            def route(b):
                for i in range(IT):
                    dve.wait_ge(t_ready, t.up())
                    dve.tensor_copy(xn2T[:, :, i * P:(i + 1) * P], ps_t[:, (t.n - 1) % 2, :, :]).then_inc(t_free, 1)
                for h in range(2):
                    dve.wait_ge(m_ready, m.up())
                    ins = dve.tensor_copy(lg[:, 2 * h:2 * h + 2, :],
                                          ps_m[:, (m.n - 1) % 2, 0:2 * E].rearrange("p (i e) -> p i e", e=E))
                    ins.then_inc(m_free, 1)
                dve.wait_ge(m_free, m.now)
                then(dve.tensor_reduce(lm[:], lg[:], AX.X, ALU.max))
                dve.tensor_tensor(lx[:], lg[:], lm[:].unsqueeze(2).broadcast_to([P, IT, E]), ALU.subtract).then_inc(lx_in, 1)
                dve.wait_ge(lx_ready, b)
                then(dve.tensor_reduce(ls[:], lx[:], AX.X, ALU.add))
                then(dve.reciprocal(li[:], ls[:]))
                then(dve.tensor_tensor(lg[:], lx[:], li[:].unsqueeze(2).broadcast_to([P, IT, E]), ALU.mult))
                rows = slice(4 * B - 4, 4 * B) if b is B else bass.ds(b * 4 - 4, 4)
                dve.tensor_copy(probs[:, rows, :], lg[:])
                other = lg[:].unsqueeze(2).broadcast_to([P, IT, E, E])
                own = lg[:].unsqueeze(3).broadcast_to([P, IT, E, E])
                dve.tensor_tensor(above[:], other, own, ALU.is_gt)
                then(dve.tensor_tensor(level[:], other, own, ALU.is_equal))
                then(dve.tensor_tensor(level[:], level[:], tri[:].unsqueeze(1).broadcast_to([P, IT, E, E]), ALU.mult))
                then(dve.tensor_tensor(above[:], above[:], level[:], ALU.add))
                then(dve.tensor_reduce(ranks[:, rows, :], above[:], AX.X, ALU.add))

            def attend(b):
                if b is not None:
                    for j in range(DC):
                        low_m(q_hi[:, j, :], q_lo[:, j, :])
                for i in range(IT):
                    o = (slice(None), slice(None), slice(i * P, (i + 1) * P))
                    low_t(xnT_hi[o], xnT_lo[o])
                if b is not None:
                    residual(b)
                for j in range(2 * DC):
                    hi, lo = (q_hi, q_lo) if j < DC else (k_hi, k_lo)
                    low_m(hi[:, j % DC, :], lo[:, j % DC, :])
                    if j == 4 and b is not None:
                        dve.wait_ge(x2_out, b * 16)
                        norm_apply(r_t, mv2, rstd2, b * 2 + 1, xn2_ready)
                if b is not None:
                    route(b)
                maxima(0)
                for i in range(1, IT):
                    maxima(i)
                    trans(i - 1)
                for i in range(IT):
                    low_m(k_hi[:, i, :], k_lo[:, i, :])
                trans(IT - 1)

            dve.wait_ge(x_in, 16)
            norm_stats(x_t, stats, mv, var)
            dve.wait_ge(hi_in["wq"], 16)
            dve.wait_ge(raw_in["wq"], 16)
            dve.tensor_tensor(wq_lo[:], wq_raw[:], wq_hi[:], ALU.subtract).then_inc(w_ready["wq"], 1)
            norm_apply(x_t, mv, rstd, 1, xn_ready)
            dve.wait_ge(gate_ready, 1)
            dve.wait_ge(const_ready, 2)
            attend(None)
            with dve.Fori(1, B) as b:
                k = b - 1
                for cnt, per in ((m, 22), (t, 16), (s, 4), (steps, 18), (hm, 16), (ht, 12)):
                    cnt.enter(k, per)
                dve.wait_ge(x_in, b * 16 + 16)
                norm_stats(x_t, stats, mv, var)
                norm_apply(x_t, mv, rstd, b * 2, xn_ready)
                attend(b)
                for cnt in (m, t, s, steps, hm, ht):
                    cnt.leave(B - 1)
            for j in range(DC):
                low_m(q_hi[:, j, :], q_lo[:, j, :])
            residual(B)
            dve.wait_ge(x2_out, 16 * B)
            norm_apply(r_t, mv2, rstd2, 2 * B, xn2_ready)
            route(B)

        @block.tensor
        def _(pe):
            m, t, s = Count(), Count(), Count()

            def product(pairs, wide=None):
                m.up()
                if not isinstance(m.now, int) or m.now > 2:
                    pe.wait_ge(m_free, m.now - 2)
                tripled(pe, ps_m[:, (m.n - 1) % 2, :], pairs).then_inc(m_ready, 1)

            def transpose(tiles):
                t.up()
                if not isinstance(t.now, int) or t.now > 2:
                    pe.wait_ge(t_free, t.now - 2)
                for j, block_in in enumerate(tiles):
                    last = pe.transpose(ps_t[:, (t.n - 1) % 2, j, :], block_in, ident[:])
                last.then_inc(t_ready, 1)

            def cols(x, c, i):
                return x[0][:, c, i * P:(i + 1) * P], x[1][:, c, i * P:(i + 1) * P]

            def chunk(x, c):
                return x[0][:, c, :], x[1][:, c, :]

            xnT, q, kk, pT = (xnT_hi, xnT_lo), (q_hi, q_lo), (k_hi, k_lo), (pT_hi, pT_lo)
            wq, wk, wv, wo = (wq_hi, wq_lo), (wk_hi, wk_lo), (wv_hi, wv_lo), (wo_hi, wo_lo)
            ctxT, ctx = (ctxT_hi, ctxT_lo), (ctx_hi, ctx_lo)

            def values():
                for j in range(DC):
                    product([(cols(ctx, c, j), chunk(pT, c)) for c in range(IT)]
                            + [(cols(kk, c, j), chunk(pT, IT + c)) for c in range(IT)])

            def project():
                pe.wait_ge(m_free, m.now)
                for i in range(IT):
                    product([(cols(q, c, i), chunk(wo, c)) for c in range(DC)])

            def router(b):
                pe.wait_ge(xn2_ready, b)
                for i in range(IT):
                    transpose([r_t[:, i, c * P:(c + 1) * P] for c in range(DC)])
                pe.wait_ge(t_free, t.now)
                for h in range(2):
                    m.up()
                    pe.wait_ge(m_free, m.now - 2)
                    for i in range(2):
                        for c in range(DC):
                            n = 2 * h + i
                            last = pe.matmul(ps_m[:, (m.n - 1) % 2, i * E:(i + 1) * E],
                                             xn2T[:, c, n * P:(n + 1) * P], wg[:, c, :],
                                             start=(c == 0), stop=(c == DC - 1))
                    last.then_inc(m_ready, 1)

            def attend(b):
                if b is None:
                    pe.wait_ge(const_ready, 2)
                    pe.wait_ge(xn_ready, 1)
                else:
                    pe.wait_ge(t_free, t.now)
                    pe.wait_ge(ctx_ready, b)
                    values()
                    pe.wait_ge(xn_ready, b + 1)
                for i in range(IT):
                    transpose([x_t[:, i, c * P:(c + 1) * P] for c in range(DC)])
                if b is not None:
                    project()
                pe.wait_ge(t_free, t.now)
                for w, name in ((wq, "wq"), (wk, "wk")):
                    if b is None:
                        pe.wait_ge(w_ready[name], 1)
                    for j in range(DC):
                        product([(cols(w, c, j), chunk(xnT, c)) for c in range(DC)])
                qk = m.now
                if b is not None:
                    router(b)
                pe.wait_ge(m_free, qk)
                pe.wait_ge(ctxT_ready, 1 if b is None else b + 1)

                def scores(i):
                    s.up()
                    if b is not None or i > 1:
                        pe.wait_ge(p_ready, s.now - 2)
                    tripled(pe, ps_s[:, i % 2, 0:S], [(cols(q, c, i), chunk(ctxT, c)) for c in range(DC)])
                    tripled(pe, ps_s[:, i % 2, S:2 * S],
                            [(cols(q, c, i), chunk(kk, c)) for c in range(DC)]).then_inc(s_ready, 1)

                def turn(i):
                    pe.wait_ge(p_ready, s.base + i + 1)
                    for h in range(2):
                        transpose([prob[:, (4 * h + n) * P:(4 * h + n + 1) * P] for n in range(4)])

                scores(0)
                for i in range(1, IT):
                    scores(i)
                    turn(i - 1)
                if b is None:
                    pe.wait_ge(w_ready["wv"], 1)
                for i in range(IT):
                    product([(cols(xnT, c, i), chunk(wv, c)) for c in range(DC)])
                turn(IT - 1)

            attend(None)
            pe.wait_ge(w_ready["wo"], 1)
            pe.wait_ge(small_in, 48)
            with pe.Fori(1, B) as b:
                k = b - 1
                m.enter(k, 22), t.enter(k, 16), s.enter(k, 4)
                attend(b)
                m.leave(B - 1), t.leave(B - 1), s.leave(B - 1)
            pe.wait_ge(t_free, t.now)
            pe.wait_ge(m_free, m.now)
            pe.wait_ge(ctx_ready, B)
            values()
            project()
            router(B)


def persistent(nc):
    small = Sbuf(nc, -(-nc.sbuf_base // 32) * 32)
    keep = {}
    keep["ident"] = small("ident", [P, P], F32)
    keep["probs"] = small("probs", [P, NT, E], F32)
    keep["ranks"] = small("ranks", [P, NT, E], F32)
    keep["gates"] = small("gates", [P, 2], F32)
    keep["idle"] = small("idle", [P, 8], F32)
    keep["weights"] = small("combine_weights", [P, NT, TOPK], F32)
    keep["slots"] = small("token_slots", [P, NT, TOPK], I32)
    keep["index"] = small("slot_tokens", [P, TILES_MAX + QUAD], I32)
    keep["last"] = small("last_quad", [P, 1], I32)
    keep["expert"] = small("tile_expert", [P, TILES_MAX], I32)
    for n in range(3):
        keep[f"at{n}"] = small(f"tile_weights_at{n}", [P, TILES_MAX], I32)
    keep["turn"] = small("tile_turn", [P, TILES_MAX], I32)
    keep["phase_at"] = small.at
    keep["end"] = keep["phase_at"] + PHASE_SMALL
    return keep


W13 = 2 * DC * FF
W2 = 2 * D
WE = W13 + W2 + D


PHASE_SMALL = 4864
BUFFERS = 3


class Later:

    def __init__(self, nc, first_free):
        sb = Sbuf(nc, first_free)
        self.u_hi, self.u_lo, self.u_raw = sb.split("shared_up", [P, 2, DC, SF])
        at = sb.at
        self.w_hi, self.w_lo, self.w_raw = sb.split("expert", [P, BUFFERS * WE])
        self.rest_at = sb.at
        self.first_hi = at
        self.second_hi, self.second_lo = at + 4 * WE, at + 4 * (BUFFERS + 1) * WE
        self.second_size = 4 * (BUFFERS - 1) * WE
        over = Sbuf(nc, self.second_hi)
        self.d_hi, self.d_lo, self.d_raw = over.split("shared_down", [P, SC, D])
        self.behind_d = over.at
        over = Sbuf(nc, self.second_hi)
        self.last_d_hi = over("last_down_hi", [P, SC, D], F32R)
        xs = [over(f"last_xs{i}", [P, D], F32) for i in range(2)]
        assert over.at <= self.second_hi + 4 * WE
        low = [Sbuf(nc, self.second_lo) for _ in range(2)]
        self.last_d_lo = low[0]("last_down_lo", [P, SC, D], F32R)
        self.last_d_raw = low[1]("last_down_raw", [P, SC, D], F32)
        self.last_xs = xs + [low[0](f"last_xs{i}", [P, D], F32) for i in range(2, 4)]
        assert low[0].at <= self.second_lo + 4 * WE
        self.free = [(self.first_hi, 4 * WE), (self.second_hi + 4 * WE, 8 * WE), (self.second_lo + 4 * WE, 4 * WE)]


class Shared:

    def __init__(self, nc, c, mem, keep, later, first, down, xs, xs_in, tag):
        sem = lambda n: c.enter_context(nc.semaphore(tag + n))
        sb = Sbuf(nc, later.rest_at)
        self.keep, self.up, self.down, self.first = keep, (later.u_hi, later.u_lo), down, first
        self.xs, self.xs_in = xs, xs_in
        self.x = sb(tag + "xT_hi", [P, DC, S], F32R), sb(tag + "xT_lo", [P, DC, S], F32R)
        self.h = sb(tag + "h_hi", [P, SC, S], F32R), sb(tag + "h_lo", [P, SC, S], F32R)
        self.gate = sb(tag + "silu", [P, 2, S], F32)
        self.hf = sb(tag + "h", [P, 2, S], F32)
        self.end = sb.at
        psum = lambda n, shape: c.enter_context(nc.psum_tensor(tag + n, shape, F32))
        self.ps_t = psum("ps_t", [P, 2, 4, P])
        self.ps_u = psum("ps_u", [P, 2, 2, S])
        self.ps_y = psum("ps_y", [P, 2, D])
        self.t_ready, self.t_hi, self.t_free = sem("t_ready"), sem("t_hi"), sem("t_free")
        self.u_ready, self.gate_ready, self.u_free = sem("u_ready"), sem("gate_ready"), sem("u_free")
        self.h_hi, self.h_lo = sem("h_hi"), sem("h_lo")
        self.y_ready, self.y_free = sem("y_ready"), sem("y_free")
        self.xn2 = mem["xn2"].rearrange("(n p) d -> n p d", p=P)

    @staticmethod
    def rows(j):
        return P if j < SC - 1 else ST

    def load(self, sp, n, i):
        if n:
            sp.wait_ge(self.t_ready, i + 1)
        sp.dma_start(self.xs[i][:], self.xn2[(self.first + n) * IT + i]).then_inc(self.xs_in[n][i], 16)

    def tensor(self, pe, up_ready, down_ready, between=lambda n, i: None):
        def turn(n, i):
            if n * IT + i >= 2:
                pe.wait_ge(self.t_free, n * IT + i - 1)
            pe.wait_ge(self.xs_in[n][i], 16)
            for c in range(DC):
                last = pe.transpose(self.ps_t[:, i % 2, c, :], self.xs[i][:, c * P:(c + 1) * P], self.keep["ident"][:])
            last.then_inc(self.t_ready, 1)

        def up(n, j):
            if n * SC + j >= 2:
                pe.wait_ge(self.u_free, n * SC + j - 1)
            rows = self.rows(j)
            for k in range(2):
                pairs = [([w[:, k, c, j * P:j * P + rows] for w in self.up], [v[:, c, :] for v in self.x])
                         for c in range(DC)]
                last = tripled(pe, self.ps_u[0:rows, j % 2, k, :], pairs)
            last.then_inc(self.u_ready, 1)

        def down(n, i):
            if n * IT + i >= 2:
                pe.wait_ge(self.y_free, n * IT + i - 1)
            pairs = [([v[0:self.rows(j), j, i * P:(i + 1) * P] for v in self.h],
                      [w[0:self.rows(j), j, :] for w in self.down]) for j in range(SC)]
            split = (lambda j: pe.wait_ge(self.h_lo, n * SC + j + 1)) if i == 0 else (lambda j: None)
            tripled(pe, self.ps_y[:, i % 2, :], pairs, split).then_inc(self.y_ready, 1)

        for i in range(IT):
            turn(0, i)
        up_ready()
        for n in range(2):
            pe.wait_ge(self.t_free, n * IT + IT)
            for j in range(SC):
                up(n, j)
            if n == 0:
                turn(1, 0), turn(1, 1)
                down_ready()
            for i in range(IT):
                between(n, i)
                down(n, i)
                if n == 0 and i < 2:
                    turn(1, i + 2)

    def scalar(self, act):
        def turn(n, i):
            act.wait_ge(self.t_ready, n * IT + i + 1)
            act.activation(self.x[0][:, :, i * P:(i + 1) * P], self.ps_t[:, i % 2, :, :], ACT.Copy).then_inc(self.t_hi, 1)

        def high(n, j):
            rows = self.rows(j)
            act.wait_ge(self.u_free, n * SC + j + 1)
            act.activation(self.h[0][0:rows, j, :], self.hf[0:rows, j % 2, :], ACT.Copy).then_inc(self.h_hi, 1)

        for i in range(IT):
            turn(0, i)
        for n in range(2):
            for j in range(SC):
                rows = self.rows(j)
                act.wait_ge(self.u_ready, n * SC + j + 1)
                act.activation(self.gate[0:rows, j % 2, :], self.ps_u[0:rows, j % 2, 0, :], ACT.Silu).then_inc(self.gate_ready, 1)
                if j:
                    high(n, j - 1)
            high(n, SC - 1)
            if n == 0:
                for i in range(IT):
                    turn(1, i)

    def vector(self, dve, total, between):
        def turn(n, i):
            o = (slice(None), slice(None), slice(i * P, (i + 1) * P))
            dve.wait_ge(self.t_hi, n * IT + i + 1)
            dve.tensor_tensor(self.x[1][o], self.ps_t[:, i % 2, :, :], self.x[0][o], ALU.subtract).then_inc(self.t_free, 1)

        def low(n, j):
            rows = self.rows(j)
            dve.wait_ge(self.h_hi, n * SC + j + 1)
            dve.tensor_tensor(self.h[1][0:rows, j, :], self.hf[0:rows, j % 2, :], self.h[0][0:rows, j, :],
                              ALU.subtract).then_inc(self.h_lo, 1)

        for i in range(IT):
            turn(0, i)
        for n in range(2):
            for j in range(SC):
                rows = self.rows(j)
                dve.wait_ge(self.gate_ready, n * SC + j + 1)
                if n * SC + j >= 2:
                    dve.wait_ge(self.h_lo, n * SC + j - 1)
                dve.tensor_tensor(self.hf[0:rows, j % 2, :], self.ps_u[0:rows, j % 2, 1, :], self.gate[0:rows, j % 2, :],
                                  ALU.mult).then_inc(self.u_free, 1)
                if j:
                    low(n, j - 1)
                if j < SC - 1:
                    between(n, j)
            low(n, SC - 1)
            if n == 0:
                turn(1, 0), turn(1, 1)
            between(n, SC - 1)
            for i in range(IT):
                to = total(n, i)
                dve.wait_ge(self.y_ready, n * IT + i + 1)
                dve.scalar_tensor_tensor(out=to[:], in0=self.ps_y[:, i % 2, :], scalar=self.keep["gates"][:, 1:2],
                                         in1=to[:], op0=ALU.mult, op1=ALU.add).then_inc(self.y_free, 1)
                if n == 0 and i < 2:
                    turn(1, i + 2)
                between(n, SC + i)


def part(w, rows, base, start, n):
    return w[0:rows, base + start:base + start + n] if isinstance(base, int) else w[0:rows, bass.ds(base + start, n)]


def load_expert(eng, w, base, io, e, sem):
    eng.dma_start(part(w, P, base, 0, W13 + W2), io["we"][e]).then_inc(sem, 16)
    eng.dma_start(part(w, FT, base, W13 + W2, D), io["we_rest"][e]).then_inc(sem, 16)


def split_expert(eng, later, base, sem):
    for rows, start, n in ((P, 0, W13 + W2), (FT, W13 + W2, D)):
        hi, lo, raw = (part(w, rows, base, start, n) for w in (later.w_hi, later.w_lo, later.w_raw))
        last = eng.tensor_tensor(lo, raw, hi, ALU.subtract)
    last.then_inc(sem, 1)


def load_down(eng, w, io, sem):
    eng.dma_start(w[:, 0:SC - 1, :], io["d"]).then_inc(sem, 16)
    eng.dma_start(w[0:ST, SC - 1, :], io["d_rest"]).then_inc(sem, 16)


def split_down(eng, d_hi, d_lo, d_raw, sem):
    for chunks, rows in ((slice(0, SC - 1), P), (slice(SC - 1, SC), ST)):
        hi, lo, raw = (w[0:rows, chunks, :] for w in (d_hi, d_lo, d_raw))
        eng.tensor_tensor(lo, raw, hi, ALU.subtract).then_inc(sem, 1)


def routing_phase(nc, io, mem, keep, later):
    with ExitStack() as c:
        sem = lambda n: c.enter_context(nc.semaphore("b_" + n))
        over = Sbuf(nc, later.behind_d)
        xs = [over(f"b_xs{i}", [P, D], F32) for i in range(IT)]
        assert over.at <= later.second_hi + later.second_size
        sh = Shared(nc, c, mem, keep, later, 0, (later.d_hi, later.d_lo), xs,
                    [[sem(f"xs{n}_{i}_in") for i in range(IT)] for n in range(2)], "b_")
        rest = Sbuf(nc, sh.end)
        acc = [rest(f"acc{u}", [P, D], F32) for u in range(2)]
        assert rest.at <= nc.sbuf_usable_end
        over = Sbuf(nc, later.second_lo)
        row_hot = over("slot_hot", [P, NT * TOPK, P], F16)
        tile_hot = over("tile_hot", [P, NT * TOPK, TILES_MAX], F16)
        grid = Sbuf(nc, over.at)("grid", [P, TILES_MAX, E], F32)
        f = {k: over("r_" + k, [P, NT, E], F32) for k in ("within", "totals", "s0", "s1", "slot", "one")}
        assert over.at <= later.second_lo + later.second_size
        small = Sbuf(nc, keep["phase_at"])
        mask, strict, ones = small("mask", [P, NT * E], F16), small("strict", [P, P], F16), small("ones", [P, P], F16)
        lane, lane_i = small("lane", [P, P], F32), small("lane_i", [P, P], I32)
        token, token_i = small("token", [P, NT], F32), small("token_i", [P, NT], I32)
        e_f = {k: small("e_" + k, [P, E], F32) for k in ("n", "tiles", "c0", "c1", "base", "first")}
        e_i = small("e_int", [P, E], I32)
        m3 = small("by_three", [P, TILES_MAX], I32)
        t_g = small("per_tile_too", [P, TILES_MAX], F32)
        hi_i, lo_i = small("tile_no_i", [P, NT * TOPK], I32), small("row_no_i", [P, NT * TOPK], I32)
        tile_no, row_no = small("tile_no", [P, NT * TOPK], F32), small("row_no", [P, NT * TOPK], F32)
        slot_f = small("slot_f", [P, NT, TOPK], F32)
        t_f = small("per_tile", [P, TILES_MAX], F32)
        assert small.at <= keep["end"], small.at

        raw_in = {k: sem(k + "_raw_in") for k in ("down", "first")}
        hi_in = {k: sem(k + "_hi_in") for k in ("down", "first")}
        down_ready = sem("down_ready")
        acc_in, acc_out = ([sem(f"acc{u}_{n}") for u in range(2)] for n in ("in", "out"))
        first_ready = keep["first_ready"]
        mask_ready, made, const_ready = sem("mask_ready"), sem("made"), sem("const_ready")
        counted, taken = sem("counted"), sem("counts_taken")
        hot_ready, listed = sem("hot_ready"), sem("listed")
        step = sem("dve_step")
        block = c.enter_context(nc.Block())
        x2_d = mem["x2"].rearrange("(n p) d -> n p d", p=P)
        base_d = mem["base"].rearrange("(n p) d -> n p d", p=P)

        @block.sync
        def _(sp):
            def residual(k):
                sp.dma_start(acc[k % 2][:], x2_d[k]).then_inc(acc_in[k % 2], 16)

            for i in range(IT):
                sh.load(sp, 0, i)
            load_down(sp, later.d_raw, io, raw_in["down"])
            residual(0), residual(1)
            load_expert(sp, later.w_raw, 0, io, 0, raw_in["first"])
            for i in range(IT):
                sh.load(sp, 1, i)
            for k in range(2 * IT):
                sp.wait_ge(sh.y_free, k + 1)
                sp.dma_start(base_d[k], acc[k % 2][:]).then_inc(acc_out[k % 2], 16)
                sp.wait_ge(acc_out[k % 2], (k // 2) * 16 + 16)
                if k + 2 < 2 * IT:
                    residual(k + 2)

        @block.gpsimd
        def _(pool):
            load_down(pool, later.d_hi, io, hi_in["down"])
            pool.memset(strict[:], 1.0).then_inc(made, 1)
            pool.memset(ones[:], 1.0).then_inc(made, 1)
            pool.iota(lane_i[:], [[1, P]], base=0, channel_multiplier=0).then_inc(made, 1)
            pool.iota(token_i[:], [[P, NT]], base=0, channel_multiplier=1).then_inc(made, 1)
            pool.wait_ge(made, 4)
            pool.affine_select(out=strict[:], in_=strict[:], compare_op=ALU.is_gt, fill=0.0, base=0,
                               pattern=[[1, P]], channel_multiplier=-1).then_inc(const_ready, 1)
            pool.tensor_copy(lane[:], lane_i[:]).then_inc(const_ready, 1)
            pool.tensor_copy(token[:], token_i[:]).then_inc(const_ready, 1)
            load_expert(pool, later.w_hi, 0, io, 0, hi_in["first"])
            pool.wait_ge(hi_in["down"], 32)
            pool.wait_ge(raw_in["down"], 32)
            split_down(pool, later.d_hi, later.d_lo, later.d_raw, down_ready)
            pool.wait_ge(hi_in["first"], 32)
            pool.wait_ge(raw_in["first"], 32)
            split_expert(pool, later, 0, first_ready)

        @block.scalar
        def _(act):
            sh.scalar(act)

        @block.vector
        def _(dve):
            steps = Count()
            ps_c = sh.ps_y

            def then(ins):
                ins.then_inc(step, 1)
                dve.wait_ge(step, steps.up())

            def running(src, a, b, n, cut):
                d = 1
                then(dve.tensor_copy(a[:], src))
                while d < n:
                    dve.tensor_copy(cut(b, 0, d), cut(a, 0, d))
                    then(dve.tensor_tensor(cut(b, d, n), cut(a, d, n), cut(a, 0, n - d), ALU.add))
                    a, b, d = b, a, 2 * d
                return a

            def count():
                incl = running(f["totals"][:], f["s0"], f["s1"], NT, lambda x, p, q: x[:, p:q, :])
                then(dve.tensor_copy(e_i[:], incl[:, NT - 1, :]))
                then(dve.tensor_tensor(f["slot"][:], incl[:], f["totals"][:], ALU.subtract))
                then(dve.tensor_tensor(f["slot"][:], f["slot"][:], f["within"][:], ALU.add))
                then(dve.tensor_scalar(e_i[:], e_i[:], P - 1, None, ALU.add))
                then(dve.tensor_scalar(e_i[:], e_i[:], P.bit_length() - 1, None, ALU.logical_shift_right))
                then(dve.tensor_scalar(e_f["tiles"][:], e_i[:], 1.0, None, ALU.max))
                cum = running(e_f["tiles"][:], e_f["c0"], e_f["c1"], E, lambda x, p, q: x[:, p:q])
                then(dve.tensor_tensor(e_f["first"][:], cum[:], e_f["tiles"][:], ALU.subtract))
                then(dve.tensor_scalar(e_f["base"][:], e_f["first"][:], float(P), None, ALU.mult))
                then(dve.tensor_tensor(f["slot"][:], f["slot"][:],
                                       e_f["base"][:].unsqueeze(1).broadcast_to([P, NT, E]), ALU.add))
                keep["cum"] = cum

            def choose(ks):
                for k in ks:
                    for what, out in ((f["slot"], slot_f), (keep["probs"], keep["weights"])):
                        then(dve.scalar_tensor_tensor(out=f["one"][:], in0=keep["ranks"][:], scalar=float(k),
                                                      in1=what[:], op0=ALU.is_equal, op1=ALU.mult))
                        then(dve.tensor_reduce(out[:, :, k], f["one"][:], AX.X, ALU.add))

            def number():
                then(dve.tensor_scalar(keep["weights"][:], keep["weights"][:], keep["gates"][:, 1:2], None, ALU.mult))
                then(dve.tensor_copy(keep["slots"][:], slot_f[:]))
                flat = keep["slots"][:].rearrange("p j k -> p (j k)")
                dve.tensor_scalar(hi_i[:], flat, P.bit_length() - 1, None, ALU.logical_shift_right)
                then(dve.tensor_scalar(lo_i[:], flat, P - 1, None, ALU.bitwise_and))
                dve.tensor_copy(tile_no[:], hi_i[:])
                then(dve.tensor_copy(row_no[:], lo_i[:]))

            def one_hot(j):
                n = NT * TOPK
                for i in range(j * n // 8, (j + 1) * n // 8):
                    dve.tensor_scalar(row_hot[:, i, :], lane[:], row_no[:, i:i + 1], None, ALU.is_equal)
                    last = dve.tensor_scalar(tile_hot[:, i, :], lane[:, 0:TILES_MAX], tile_no[:, i:i + 1],
                                             token[:, i // TOPK:i // TOPK + 1], ALU.is_equal, ALU.mult)
                last.then_inc(hot_ready, 1)

            def per_tile(rows, op, out, n):
                then(dve.tensor_tensor(grid[:, :, 0:n], lane[:, 0:TILES_MAX].unsqueeze(2).broadcast_to([P, TILES_MAX, n]),
                                       rows.unsqueeze(1).broadcast_to([P, TILES_MAX, n]), op))
                then(dve.tensor_reduce(out, grid[:, :, 0:n], AX.X, ALU.add))

            def schedule():
                cum = keep["cum"]
                then(dve.tensor_copy(keep["last"][:], cum[:, E - 1:E]))
                then(dve.tensor_scalar(keep["last"][:], keep["last"][:], -1, None, ALU.add))
                then(dve.tensor_scalar(keep["last"][:], keep["last"][:], QUAD.bit_length() - 1, None, ALU.logical_shift_right))
                per_tile(cum[:], ALU.is_ge, t_f[:], E)
                then(dve.tensor_scalar(keep["expert"][:], t_f[:], float(E - 1), None, ALU.min))

            def places(ns):
                for n in ns:
                    at = keep[f"at{n}"]
                    then(dve.tensor_scalar(at[:], keep["expert"][:], n, None, ALU.add))
                    then(dve.tensor_scalar(m3[:], at[:], 11, None, ALU.mult))
                    then(dve.tensor_scalar(m3[:], m3[:], 5, None, ALU.logical_shift_right))
                    then(dve.scalar_tensor_tensor(out=at[:], in0=m3[:], scalar=-3.0, in1=at[:], op0=ALU.mult, op1=ALU.add))
                    then(dve.tensor_scalar(at[:], at[:], float(WE), None, ALU.mult))

            def turns():
                per_tile(e_f["first"][:, 0:E - 1], ALU.is_equal, t_f[:], E - 1)
                per_tile(e_f["first"][:, 0:E - 2], ALU.is_equal, t_g[:], E - 2)
                then(dve.tensor_tensor(keep["turn"][:], t_f[:], t_g[:], ALU.add))

            dve.tensor_scalar(mask[:], keep["ranks"][:].rearrange("p j e -> p (j e)"), float(TOPK), None,
                              ALU.is_lt).then_inc(mask_ready, 1)
            dve.wait_ge(counted, 1)
            dve.tensor_copy(f["within"][:], ps_c[:, 0, 0:NT * E].rearrange("p (j e) -> p j e", e=E))
            dve.tensor_copy(f["totals"][:], ps_c[:, 1, 0:NT * E].rearrange("p (j e) -> p j e", e=E)).then_inc(taken, 1)
            dve.wait_ge(taken, 1)
            dve.wait_ge(const_ready, 3)
            work = [count, lambda: choose((0, 1)), lambda: choose((2, 3)), number, schedule,
                    lambda: places((0, 1)), lambda: places((2,)), turns,
                    *((lambda j=j: one_hot(j)) for j in range(8))]
            assert len(work) == 16 and 2 * (SC + IT) == 20

            def between(n, k):
                at = n * (SC + IT) + k
                if at < len(work):
                    work[at]()
                elif at == len(work) + 1:
                    then(dve.memset(keep["index"][:], 0))
                    dve.wait_ge(listed, 1)
                    then(dve.tensor_copy(keep["index"][:, 0:TILES_MAX], sh.ps_t[:, 0, 0, 0:TILES_MAX]))

            def total(n, i):
                dve.wait_ge(acc_in[i % 2], n * 32 + (i // 2) * 16 + 16)
                return acc[i % 2]

            sh.vector(dve, total, between)

        @block.tensor
        def _(pe):
            pe.wait_ge(const_ready, 3)
            pe.wait_ge(mask_ready, 1)
            pe.matmul(sh.ps_y[:, 0, 0:NT * E], strict[:], mask[:], start=True, stop=True)
            pe.matmul(sh.ps_y[:, 1, 0:NT * E], ones[:], mask[:], start=True, stop=True).then_inc(counted, 1)
            pe.wait_ge(taken, 1)

            def list_slots(n, i):
                if (n, i) != (1, IT - 2):
                    return
                pe.wait_ge(hot_ready, 8)
                pe.wait_ge(sh.t_free, 2 * IT)
                slots = NT * TOPK
                for k in range(slots):
                    last = pe.matmul(sh.ps_t[:, 0, 0, 0:TILES_MAX], row_hot[:, k, :], tile_hot[:, k, :],
                                     start=(k == 0), stop=(k == slots - 1))
                last.then_inc(listed, 1)

            sh.tensor(pe, lambda: pe.wait_ge(keep["up_ready"], 2), lambda: pe.wait_ge(down_ready, 2), list_slots)


def expert_phase(nc, io, mem, keep, later):
    with ExitStack() as c:
        sem = lambda n: c.enter_context(nc.semaphore("c_" + n))
        sb = Sbuf(nc, later.rest_at)
        xg = [sb(f"xg{v}", [P, D], F32) for v in range(QUAD)]
        x = [(sb(f"xT_hi{u}", [P, DC, P], F32R), sb(f"xT_lo{u}", [P, DC, P], F32R)) for u in range(2)]
        gate = [sb(f"gate{u}", [P, FF], F32) for u in range(2)]
        hf = [sb(f"hf{u}", [P, FF], F32) for u in range(2)]
        h = [(sb(f"hT_hi{u}", [P, FC, P], F32R), sb(f"hT_lo{u}", [P, FC, P], F32R)) for u in range(2)]
        y = [sb(f"y{v}", [P, D], F32) for v in range(QUAD)]
        column = [sb(f"column{v}", [P, 1], I32) for v in range(QUAD)]
        zeros = sb("zeros", [P, D], F32)
        assert sb.at <= nc.sbuf_usable_end, sb.at
        ps_u = c.enter_context(nc.psum_tensor("c_ps_u", [P, 2, 2, 512], F32))
        ps_x = c.enter_context(nc.psum_tensor("c_ps_x", [P, 4, P], F32))
        ps_h = c.enter_context(nc.psum_tensor("c_ps_h", [P, 4, P], F32))
        ps_y = c.enter_context(nc.psum_tensor("c_ps_y", [P, 2, D], F32))
        gathered = [sem(f"gathered{v}") for v in range(QUAD)]
        x_turned, x_hi, x_split = sem("x_turned"), sem("x_hi"), sem("x_split")
        u_ready, gate_ready, h_ready = sem("u_ready"), sem("gate_ready"), sem("h_ready")
        h_turned, h_hi, h_split = sem("h_turned"), sem("h_hi"), sem("h_split")
        y_ready, y_taken = sem("y_ready"), sem("y_taken")
        y_out = [sem(f"y_out{v}") for v in range(QUAD)]
        w_in, w_ready = sem("w_in"), keep["first_ready"]
        column_ready, zeros_ready, rest_out = sem("column_ready"), sem("zeros_ready"), sem("rest_out")
        block = c.enter_context(nc.Block())
        y_d = mem["y"].rearrange("(t p) d -> t p d", p=P)
        xn2_d = mem["xn2"].rearrange("(n p) d -> n p d", p=P)

        def number(eng, t, k, low, high):
            at = keep[k][0:1, t:t + 1] if isinstance(t, int) else keep[k][0:1, bass.ds(t, 1)]
            return eng.value_load(at, min_val=low, max_val=high)

        def wait(eng, s, value):
            if not isinstance(value, int) or value > 0:
                eng.wait_ge(s, value)

        def tiles(eng, step):
            for v in range(QUAD):
                step(v, v)
            last = number(eng, 0, "last", E // QUAD - 1, TILES_MAX // QUAD - 1)
            with eng.Fori(1, last + 1) as i:
                for v in range(QUAD):
                    step(i * QUAD + v, v)
            return last

        @block.sync
        def _(sp):
            sp.wait_ge(zeros_ready, 1)
            last = number(sp, 0, "last", E // QUAD - 1, TILES_MAX // QUAD - 1)
            with sp.Fori(0, REST) as t:
                sp.dma_start(y_d[last * QUAD + QUAD + t], zeros[:]).then_inc(rest_out, 16)
            sp.wait_ge(rest_out, REST * 16)

        @block.gpsimd
        def _(pool):
            pool.memset(zeros[:], 0.0).then_inc(zeros_ready, 1)

            def gather(v, at):
                pool.indirect_dma_start(xg[v][:], None, mem["xn2"],
                                        bass.IndirectOffsetOnAxis(ap=at, axis=0)).then_inc(gathered[v], 16)

            def load(base, e):
                load_expert(pool, later.w_hi, base, io, e, w_in)
                load_expert(pool, later.w_raw, base, io, e, w_in)

            gather(0, keep["index"][:, 0:1])
            load(WE, 1)
            for v in range(1, QUAD):
                gather(v, keep["index"][:, v:v + 1])

            def step(t, v):
                pool.wait_ge(gathered[v], (t + (QUAD - v)) * 4)
                pool.tensor_copy(column[v][:], keep["index"][:, t + QUAD:t + QUAD + 1] if isinstance(t, int)
                                 else keep["index"][:, bass.ds(t + QUAD, 1)]).then_inc(column_ready, 1)
                pool.wait_ge(x_turned, t + 1)
                pool.wait_ge(column_ready, t + 1)
                hold(nc, nc.gpsimd, keep)
                gather(v, column[v][:])
                flag = number(pool, t, "turn", 0, 2)
                with pool.If(flag > 0):
                    e = number(pool, t, "expert", 0, E - 2)
                    base = number(pool, t, "at1", 0, (BUFFERS - 1) * WE)
                    pool.wait_ge(w_in, e * 64 + 64)
                    split_expert(pool, later, base, w_ready)
                    base = number(pool, t, "at2", 0, (BUFFERS - 1) * WE)
                    wait(pool, y_ready, t)
                    hold(nc, nc.gpsimd, keep, 5)
                    with pool.If(flag > 1):
                        load(base, number(pool, t, "expert", 0, E - 3) + 2)
                    with pool.Else():
                        load_down(pool, later.last_d_hi, io, keep["last_down_in"])
                        load_down(pool, later.last_d_raw, io, keep["last_down_in"])
                        for i in range(IT):
                            pool.dma_start(later.last_xs[i][:], xn2_d[2 * IT + i]).then_inc(keep["last_xs_in"][i], 16)
                with pool.Else():
                    pass

            last = tiles(pool, step)
            for v in range(QUAD):
                pool.wait_ge(gathered[v], last * 16 + 32)

        @block.scalar
        def _(act):
            def turn(t, u):
                act.wait_ge(x_turned, t + 1)
                act.activation(x[u][0][:], ps_x[:], ACT.Copy).then_inc(x_hi, 1)

            def take(t, v):
                act.wait_ge(y_ready, t + 1)
                wait(act, y_out[v], (t - v) * 4)
                act.activation(y[v][:], ps_y[:, v % 2, :], ACT.Copy).then_inc(y_taken, 1)
                act.wait_ge(y_taken, t + 1)
                act.dma_start(y_d[t], y[v][:]).then_inc(y_out[v], 16)

            def step(t, v):
                u = v % 2
                act.wait_ge(u_ready, t + 1)
                act.activation(gate[u][:], ps_u[:, u, 0, 0:FF], ACT.Silu).then_inc(gate_ready, 1)
                turn(t + 1, 1 - u)
                if not isinstance(t, int) or t > 0:
                    take(t - 1, (v - 1) % QUAD)
                act.wait_ge(h_turned, t + 1)
                act.activation(h[u][0][:, 0:2, :], ps_h[:, 0:2, :], ACT.Copy)
                act.activation(h[u][0][0:FT, 2, :], ps_h[0:FT, 2, :], ACT.Copy).then_inc(h_hi, 1)

            turn(0, 0)
            last = tiles(act, step)
            take(last * QUAD + (QUAD - 1), QUAD - 1)
            for v in range(QUAD):
                act.wait_ge(y_out[v], last * 16 + 16)
            hold(nc, nc.scalar, keep)

        @block.vector
        def _(dve):
            def turn(t, u):
                dve.wait_ge(x_hi, t + 1)
                dve.tensor_tensor(x[u][1][:], ps_x[:], x[u][0][:], ALU.subtract).then_inc(x_split, 1)

            def step(t, v):
                u = v % 2
                dve.wait_ge(gate_ready, t + 1)
                dve.tensor_tensor(hf[u][:], ps_u[:, u, 1, 0:FF], gate[u][:], ALU.mult).then_inc(h_ready, 1)
                turn(t + 1, 1 - u)
                dve.wait_ge(h_hi, t + 1)
                dve.tensor_tensor(h[u][1][:, 0:2, :], ps_h[:, 0:2, :], h[u][0][:, 0:2, :], ALU.subtract)
                dve.tensor_tensor(h[u][1][0:FT, 2, :], ps_h[0:FT, 2, :], h[u][0][0:FT, 2, :],
                                  ALU.subtract).then_inc(h_split, 1)

            turn(0, 0)
            tiles(dve, step)

        @block.tensor
        def _(pe):
            def turn(t, v):
                pe.wait_ge(gathered[v], (t + (QUAD - v)) * 4)
                wait(pe, x_split, t)
                for k in range(DC):
                    last = pe.transpose(ps_x[:, k, :], xg[v][:, k * P:(k + 1) * P], keep["ident"][:])
                last.then_inc(x_turned, 1)

            def weights(base, start, n, rows=P):
                return [part(w, rows, base, start, n) for w in (later.w_hi, later.w_lo)]

            def down(t, u, base):
                pe.wait_ge(h_split, t + 1)
                wait(pe, y_taken, t - 1)
                pairs = []
                for j in range(FC):
                    rows = P if j < FC - 1 else FT
                    pairs.append(([v[0:rows, j, :] for v in h[u]], weights(base, W13 + j * D, D, rows)))
                tripled(pe, ps_y[:, u, :], pairs).then_inc(y_ready, 1)

            def numbers(t):
                return number(pe, t, "expert", 0, E - 1), number(pe, t, "at0", 0, (BUFFERS - 1) * WE)

            now, before = [], []

            def step(t, v):
                u = v % 2
                e, base = numbers(t) if v == 0 else now.pop()
                pe.wait_ge(x_split, t + 1)
                pe.wait_ge(w_ready, e + 1)
                wait(pe, h_ready, t - 1)
                for k in range(2):
                    last = tripled(pe, ps_u[:, u, k, 0:FF], [
                        ([v[:, c_, :] for v in x[u]], weights(base, (k * DC + c_) * FF, FF)) for c_ in range(DC)])
                last.then_inc(u_ready, 1)
                turn(t + 1, (v + 1) % QUAD)
                if not isinstance(t, int) or t > 0:
                    down(t - 1, 1 - u, before.pop() if v else number(pe, t - 1, "at0", 0, (BUFFERS - 1) * WE))
                if v < QUAD - 1:
                    now.append(numbers(t + 1))
                    before.append(base)
                pe.wait_ge(h_ready, t + 1)
                wait(pe, h_split, t)
                for j in range(FC):
                    rows = P if j < FC - 1 else FT
                    last = pe.transpose(ps_h[0:rows, j, :], hf[u][:, j * P:j * P + rows], keep["ident"][:])
                last.then_inc(h_turned, 1)

            turn(0, 0)
            last = tiles(pe, step)
            down(last * QUAD + (QUAD - 1), 1, number(pe, last * QUAD + (QUAD - 1), "at0", 0, (BUFFERS - 1) * WE))


def combining_phase(nc, io, mem, keep, later, out):
    with ExitStack() as c:
        sem = lambda n: c.enter_context(nc.semaphore("d_" + n))
        down = later.last_d_hi, later.last_d_lo
        sh = Shared(nc, c, mem, keep, later, 2, down, later.last_xs,
                    [keep["last_xs_in"], [sem(f"xs{i}_in") for i in range(IT)]], "d_")
        assert sh.end <= nc.sbuf_usable_end
        free = [Sbuf(nc, at) for at, _ in later.free]
        parts = [free[(0, 0, 1, 1)[v]](f"parts{v}", [P, TOPK, D], F32) for v in range(4)]
        total = [free[1 if k < 4 else 2](f"total{k}", [P, D], F32) for k in range(6)]
        for place, (at, size) in zip(free, later.free):
            assert place.at <= at + size
        parts_in = [sem(f"parts{v}_in") for v in range(4)]
        total_in, total_out = ([sem(f"total{k}_{n}") for k in range(6)] for n in ("in", "out"))
        summed, terms, down_ready = sem("summed"), sem("terms"), sem("down_ready")
        block = c.enter_context(nc.Block())
        out_d = out.rearrange("(n p) d -> n p d", p=P)
        base_d = mem["base"].rearrange("(n p) d -> n p d", p=P)
        x2_d = mem["x2"].rearrange("(n p) d -> n p d", p=P)
        y_d = mem["y"][0:TILES_MAX * P]
        order = [tile for n in range(2) for tile in
                 [(2 + n) * IT + i for i in range(IT)] + [n * IT + i for i in range(IT)]]

        def place(tile):
            return (tile % 4, tile // 4 - 2) if tile >= 2 * IT else (4 + tile % 2, tile // 2)

        @block.sync
        def _(sp):
            def load(tile):
                k, before = place(tile)
                if before:
                    sp.wait_ge(total_out[k], before * 16)
                sp.dma_start(total[k][:], (x2_d if tile >= 2 * IT else base_d)[tile]).then_inc(total_in[k], 16)

            def store(tile):
                if tile >= 2 * IT:
                    sp.wait_ge(sh.y_free, tile - 2 * IT + 1)
                else:
                    sp.wait_ge(summed, order.index(tile) + 1)
                k, _ = place(tile)
                sp.dma_start(out_d[tile], total[k][:]).then_inc(total_out[k], 16)

            for tile in order[0:IT] + [0, 1]:
                load(tile)
            for i in range(IT):
                sh.load(sp, 1, i)
            for n in range(2):
                own, other = (2 + n) * IT, n * IT
                for k in (other, other + 1, own, other + 2, own + 1, other + 3, own + 2, own + 3):
                    store(k)
                    after = k + 2 if k < 2 * IT else k + IT
                    if after < (2 * IT if k < 2 * IT else NT):
                        load(after)
            for k in range(6):
                sp.wait_ge(total_out[k], 32 if k < 4 else 64)

        @block.gpsimd
        def _(pool):
            def gather(c):
                v = c % 4
                if c >= 4:
                    pool.wait_ge(summed, c - 3)
                for q in range(TOPK):
                    pool.indirect_dma_start(parts[v][:, q, :], None, y_d, bass.IndirectOffsetOnAxis(
                        ap=keep["slots"][:, order[c], q:q + 1], axis=0)).then_inc(parts_in[v], 16)

            for c in range(4):
                gather(c)
            pool.wait_ge(keep["last_down_in"], 64)
            split_down(pool, *down, later.last_d_raw, down_ready)
            for c in range(4, NT):
                gather(c)

        @block.scalar
        def _(act):
            sh.scalar(act)

        @block.vector
        def _(dve):
            def combine(c):
                k, before = place(order[c])
                dve.wait_ge(total_in[k], before * 16 + 16)
                dve.wait_ge(parts_in[c % 4], (c // 4) * 64 + 64)
                for q in range(TOPK):
                    ins = dve.scalar_tensor_tensor(out=total[k][:], in0=parts[c % 4][:, q, :],
                                                   scalar=keep["weights"][:, order[c], q:q + 1],
                                                   in1=total[k][:], op0=ALU.mult, op1=ALU.add)
                    if q < TOPK - 1:
                        ins.then_inc(terms, 1)
                        dve.wait_ge(terms, c * (TOPK - 1) + q + 1)
                    else:
                        ins.then_inc(summed, 1)

            def sum_of(n, i):
                dve.wait_ge(summed, n * 2 * IT + i + 1)
                return total[i]

            sh.vector(dve, sum_of, lambda n, k: combine(n * 2 * IT + k) if k < 2 * IT else None)

        @block.tensor
        def _(pe):
            sh.tensor(pe, lambda: None, lambda: pe.wait_ge(down_ready, 2))


def program(nc, io, out):
    mem = {k: nc.dram_tensor(k + "_dram", shape, F32, kind="Internal").ap() for k, shape in (
        ("x2", [T, D]), ("xn2", [T, D]), ("base", [T, D]), ("y", [(TILES_MAX + REST) * P, D]))}
    keep = persistent(nc)
    later = Later(nc, keep["end"])
    with ExitStack() as c:
        sem = lambda n: c.enter_context(nc.semaphore(n))
        keep["up_raw_in"], keep["up_hi_in"] = ([sem(f"up{k}_{n}_in") for k in range(2)] for n in ("raw", "hi"))
        keep["up_ready"], keep["first_ready"] = sem("up_ready"), sem("expert_split")
        keep["last_down_in"], keep["last_xs_in"] = sem("last_down_in"), [sem(f"last_xs{i}_in") for i in range(IT)]
        attention_phase(nc, io, mem, keep, later, keep["end"])
        routing_phase(nc, io, mem, keep, later)
        expert_phase(nc, io, mem, keep, later)
        combining_phase(nc, io, mem, keep, later, out)


def kernel(**inputs):
    import numpy as np
    from concourse import bacc
    from concourse.bass_utils import run_bass_kernel_spmd

    a = {k: np.asarray(v) for k, v in inputs.items()}

    def chunks(x):
        *lead, rows, n = x.shape
        return np.moveaxis(x.reshape(*lead, rows // P, P, n), -2, -3)

    w1, w3, w2 = (a["L0_ffn_W" + k].transpose(0, 2, 1) for k in "132")
    w2s = a["L0_ffn_W2s"].T
    arrays = {
        "x": a["x"].reshape(T, D),
        "ctx": chunks(a["ctx_2048"]),
        "ctxT": chunks(a["ctx_2048"].transpose(0, 2, 1)),
        "gx": a["g_xattn"],
        "gf": a["g_ffn"],
        "wg": chunks(a["L0_ffn_Wg"].T),
        "we": np.concatenate([chunks(w).reshape(E, P, -1) for w in (w1, w3, w2[:, 0:2 * P])], axis=2),
        "we_rest": w2[:, 2 * P:],
        "u": np.stack([chunks(a["L0_ffn_W1s"].T), chunks(a["L0_ffn_W3s"].T)], axis=1),
        "d": chunks(w2s[0:(SC - 1) * P]),
        "d_rest": w2s[(SC - 1) * P:],
    }
    for k in ("wq", "wk", "wv", "wo"):
        arrays[k] = chunks(a["L0_xattn_" + k].T)
    arrays = {k: np.ascontiguousarray(v) for k, v in arrays.items()}

    nc = bacc.Bacc("TRN2", target_bir_lowering=False, num_devices=1)
    io = {k: nc.dram_tensor(k, v.shape, mybir.dt.from_np(v.dtype), kind="ExternalInput").ap()
          for k, v in arrays.items()}
    out = nc.dram_tensor("out", (T, D), F32, kind="ExternalOutput").ap()
    program(nc, io, out)
    r = run_bass_kernel_spmd(nc, [arrays], core_ids=[0])
    return r.results[0]["out"].reshape(B, S, D)
```

```python
from contextlib import ExitStack

import concourse.bass as bass
from concourse import mybir

F32 = mybir.dt.float32
F32R = mybir.dt.float32r
F16 = mybir.dt.float16
I32 = mybir.dt.int32
ALU = mybir.AluOpType
ACT = mybir.ActivationFunctionType
AX = mybir.AxisListType

P = 128
B, S, D = 4, 512, 512
T = B * S
NT = T // P
IT = S // P
DC = D // P
KC = 2 * S // P
E, FF, TOPK = 16, 352, 4
FC = 3
FT = FF - 2 * P
SF = 704
SC = 6
ST = SF - 5 * P
TILES_MAX = 80
QUAD = 4
REST = TILES_MAX - T * TOPK // P
EPS = 1e-5
SCALE = float(D) ** -0.5


class Count:

    def __init__(self, start=0):
        self.base, self.n = start, 0

    def up(self, k=1):
        self.n += k
        return self.base + self.n

    @property
    def now(self):
        return self.base + self.n

    def enter(self, i, per):
        self.start, self.per = self.base + self.n, per
        self.base, self.n = i * per + self.start, 0

    def leave(self, passes):
        assert self.n == self.per, (self.n, self.per)
        self.base, self.n = self.start + passes * self.per, 0


def hold(nc, eng, keep, at=3):
    idle = keep["idle"]
    if eng is nc.vector:
        eng.memset(idle[:, 0:1], 0.0)
    elif eng is nc.scalar:
        eng.activation(idle[:, 1:2], idle[:, 2:3], ACT.Copy)
    else:
        eng.tensor_tensor(idle[:, at:at + 1], idle[:, 4:5], idle[:, 4:5], ALU.add)


TERMS = ((0, 0), (0, 1), (1, 0))


def tripled(pe, out, pairs, ahead=lambda c: None):
    n = 0
    for c, (a, b) in enumerate(pairs):
        ahead(c)
        for i, j in TERMS:
            last = pe.matmul(out, a[i], b[j], start=(n == 0), stop=(n == 3 * len(pairs) - 1))
            n += 1
    return last


def rank_experts(dve, then, p, level, lower, part, out):
    other = p.unsqueeze(2).broadcast_to([P, IT, E, E])
    own = p.unsqueeze(3).broadcast_to([P, IT, E, E])

    def larger():
        then(dve.tensor_tensor(level[:], other, own, ALU.is_gt))
        then(dve.tensor_reduce(part[:], level[:], AX.X, ALU.add))

    def equal():
        then(dve.tensor_tensor(level[:], other, own, ALU.is_equal))
        then(dve.tensor_tensor(level[:], level[:], lower[:].unsqueeze(1).broadcast_to([P, IT, E, E]), ALU.mult))

    def added():
        then(dve.tensor_reduce(out[0][:], level[:], AX.X, ALU.add))
        then(dve.tensor_tensor(out[1], part[:], out[0][:], ALU.add))

    return larger, equal, added


class Sbuf:

    def __init__(self, nc, at):
        self.nc, self.at = nc, at

    def __call__(self, name, shape, dt):
        size = {F32: 4, F32R: 4, I32: 4, F16: 2}[dt]
        for n in shape[1:]:
            size *= n
        t = self.nc.alloc_sbuf_tensor_at(name, shape, dt, offset=self.at)
        self.at += -(-size // 32) * 32
        return t

    def split(self, name, shape):
        hi = self(name + "_hi", shape, F32R)
        at = self.at
        lo = self(name + "_lo", shape, F32R)
        end, self.at = self.at, at
        raw = self(name + "_raw", shape, F32)
        self.at = end
        return hi, lo, raw


def attention_phase(nc, io, mem, keep, later, first_free):
    sb = Sbuf(nc, first_free)
    wq_hi, wq_lo, wq_raw = sb.split("wq", [P, DC, D])
    wk_hi, wk_lo, wk_raw = sb.split("wk", [P, DC, D])
    wv_hi, wv_lo, wv_raw = sb.split("wv", [P, DC, D])
    wo_hi, wo_lo, wo_raw = sb.split("wo", [P, DC, D])
    ctxT_hi, ctxT_lo, ctxT_raw = sb.split("ctxT", [P, DC, S])
    ctx_hi, ctx_lo, ctx_raw = sb.split("ctx", [P, IT, D])
    xnT_hi, xnT_lo = sb("xnT_hi", [P, DC, S], F32R), sb("xnT_lo", [P, DC, S], F32R)
    q_hi, q_lo = sb("q_hi", [P, DC, S], F32R), sb("q_lo", [P, DC, S], F32R)
    k_hi, k_lo = sb("k_hi", [P, DC, S], F32R), sb("k_lo", [P, DC, S], F32R)
    prob = sb("prob", [P, 2 * S], F32)
    at = sb.at
    pT_hi, pT_lo = sb("pT_hi", [P, KC, S], F32R), sb("pT_lo", [P, KC, S], F32R)
    over = Sbuf(nc, at)
    xn2T = over("xn2T", [P, DC, S], F32)
    x_t = sb("x_t", [P, IT, D], F32)
    r_t = sb("r_t", [P, IT, D], F32)
    level = sb("rank_level", [P, IT, E, E], F16)
    assert sb.at <= nc.sbuf_usable_end, sb.at

    ident, probs, ranks, gates = (keep[k] for k in ("ident", "probs", "ranks", "gates"))
    small = Sbuf(nc, keep["phase_at"])
    wg = small("router_w", [P, DC, E], F32)
    tri = small("lower_index", [P, E, E], F16)
    half = small("minus_half", [P, IT], F32)
    stats = small("ln_stats", [P, IT, 6], F32)
    mv = small("ln_mv", [P, IT, 2], F32)
    var = small("ln_var", [P, IT], F32)
    rstd = small("ln_rstd", [P, IT], F32)
    stats2 = small("ln2_stats", [P, IT, 6], F32)
    mv2 = small("ln2_mv", [P, IT, 2], F32)
    var2 = small("ln2_var", [P, IT], F32)
    rstd2 = small("ln2_rstd", [P, IT], F32)
    top = small("row_max", [P, IT], F32)
    bias = small("exp_bias", [P, IT], F32)
    total = small("exp_total", [P, IT], F32)
    inv = small("out_scale", [P, IT], F32)
    lg = small("router_logits", [P, IT, E], F32)
    lx = small("router_exps", [P, IT, E], F32)
    lgT = small("router_logitsT", [E, S], F32)
    larger = small("rank_larger", [P, IT, E], F32)
    equal = small("rank_equal", [P, IT, E], F32)
    lm = small("router_max", [P, IT], F32)
    ls = small("router_sum", [P, IT], F32)
    li = small("router_inv", [P, IT], F32)

    assert small.at <= first_free

    x_d = io["x"].rearrange("(b i p) d -> b p i d", b=B, p=P)
    x2_d = mem["x2"].rearrange("(b i p) d -> b p i d", b=B, p=P)
    xn2_d = mem["xn2"].rearrange("(b i p) d -> b p i d", b=B, p=P)
    ctx_d, ctxT_d = io["ctx"], io["ctxT"]
    w_d = {k: io[k] for k in ("wq", "wk", "wv", "wo")}

    with ExitStack() as c:
        sem = lambda n: c.enter_context(nc.semaphore(n))
        ps_s = c.enter_context(nc.psum_tensor("ps_scores", [P, 2, 2 * S], F32))
        ps_t = c.enter_context(nc.psum_tensor("ps_transposed", [P, 2, 4, P], F32))
        ps_m = c.enter_context(nc.psum_tensor("ps_products", [P, 2, D], F32))
        first_x_in = [sem(f"first_x{i}_in") for i in range(IT)]
        x_in, res_in = sem("x_in"), sem("res_in")
        raw_in = {k: sem(k + "_raw_in") for k in ("wq", "wk", "wv", "wo")}
        ctxT_raw_in, ctx_raw_in, small_in = sem("ctxT_raw_in"), sem("ctx_raw_in"), sem("small_in")
        hi_in = {k: sem(k + "_hi_in") for k in ("wq", "wk", "wv", "wo")}
        ctxT_hi_in, ctx_hi_in = sem("ctxT_hi_in"), sem("ctx_hi_in")
        w_ready = {k: sem(k + "_ready") for k in ("wq", "wk", "wv", "wo")}
        ctxT_ready, ctx_ready = sem("ctxT_ready"), sem("ctx_ready")
        made, const_ready = sem("made"), sem("const_ready")
        var_ready, rstd_ready = sem("var_ready"), sem("rstd_ready")
        xn_ready, xn2_ready = sem("xn_ready"), sem("xn2_ready")
        x2_out, xn2_out = sem("x2_out"), sem("xn2_out")
        m_ready, m_hi, m_free = sem("m_ready"), sem("m_hi"), sem("m_free")
        t_ready, t_hi, t_free = sem("t_ready"), sem("t_hi"), sem("t_free")
        s_ready, bias_ready, p_ready = sem("s_ready"), sem("bias_ready"), sem("p_ready")
        lx_in, lx_ready = sem("router_shifted"), sem("router_exp_ready")
        gate_ready, step = sem("gate_ready"), sem("dve_step")
        block = c.enter_context(nc.Block())

        @block.sync
        def _(sp):
            for i in range(IT):
                sp.dma_start(x_t[:, i, :], x_d[0, :, i]).then_inc(first_x_in[i], 16)
            for k, t in (("wq", wq_raw), ("wk", wk_raw)):
                sp.dma_start(t[:], w_d[k]).then_inc(raw_in[k], 16)
            sp.dma_start(ctxT_raw[:], ctxT_d[0]).then_inc(ctxT_raw_in, 16)
            sp.dma_start(wv_raw[:], w_d["wv"]).then_inc(raw_in["wv"], 16)
            sp.dma_start(ctx_raw[:], ctx_d[0]).then_inc(ctx_raw_in, 16)
            sp.dma_start(wo_raw[:], w_d["wo"]).then_inc(raw_in["wo"], 16)
            sp.dma_start(wg[:], io["wg"]).then_inc(small_in, 16)
            sp.dma_start(gates[:, 0:1], io["gx"].partition_broadcast(P)).then_inc(small_in, 16)
            sp.dma_start(gates[:, 1:2], io["gf"].partition_broadcast(P)).then_inc(small_in, 16)
            sp.dma_start(r_t[:], x_d[0]).then_inc(res_in, 16)

            def stores(b):
                sp.wait_ge(m_free, b * 22 + 20)
                sp.dma_start(x2_d[b], r_t[:]).then_inc(x2_out, 16)
                sp.wait_ge(xn2_ready, b * 4 + 4)
                sp.dma_start(xn2_d[b], (x_t if b is B - 1 else r_t)[:]).then_inc(xn2_out, 16)

            with sp.Fori(1, B) as b:
                sp.wait_ge(t_ready, b * 16 - 12)
                sp.dma_start(x_t[:], x_d[b]).then_inc(x_in, 16)
                sp.wait_ge(s_ready, b * 4)
                sp.dma_start(ctxT_raw[:], ctxT_d[b]).then_inc(ctxT_raw_in, 16)
                sp.wait_ge(m_ready, b * 22 - 6)
                sp.dma_start(ctx_raw[:], ctx_d[b]).then_inc(ctx_raw_in, 16)
                stores(b - 1)
                sp.wait_ge(t_ready, b * 16 + 4)
                sp.wait_ge(xn2_out, b * 16)
                sp.dma_start(r_t[:], x_d[b]).then_inc(res_in, 16)
            sp.wait_ge(m_ready, 22 * B - 10)
            for k in range(2):
                sp.dma_start(later.u_raw[:, k, :, :], io["u"][:, k]).then_inc(keep["up_raw_in"][k], 16)
            for i in range(IT - 1):
                sp.dma_start(later.first_xs[i][:], mem["xn2"][i * P:(i + 1) * P]).then_inc(keep["first_xs_in"][i], 16)
            stores(B - 1)
            sp.wait_ge(x2_out, 16 * B)
            sp.wait_ge(xn2_out, 16 * B)

        @block.gpsimd
        def _(pool):
            pool.dma_start(wq_hi[:], w_d["wq"]).then_inc(hi_in["wq"], 16)
            pool.dma_start(wk_hi[:], w_d["wk"]).then_inc(hi_in["wk"], 16)
            pool.memset(half[:], -0.5).then_inc(made, 1)
            pool.memset(keep["idle"][:, 2:5], 0.0).then_inc(made, 1)
            pool.memset(ident[:], 0.0).then_inc(made, 1)
            pool.memset(tri[:], 1.0).then_inc(made, 1)
            pool.wait_ge(made, 4)
            pool.affine_select(out=ident[:], in_=ident[:], compare_op=ALU.not_equal, fill=1.0, base=0,
                               pattern=[[-1, P]], channel_multiplier=1).then_inc(const_ready, 1)
            pool.affine_select(out=tri[:], in_=tri[:], compare_op=ALU.is_gt, fill=0.0, base=0,
                               pattern=[[1, E], [-1, E]], channel_multiplier=0).then_inc(const_ready, 1)
            pool.dma_start(ctxT_hi[:], ctxT_d[0]).then_inc(ctxT_hi_in, 16)
            pool.dma_start(wv_hi[:], w_d["wv"]).then_inc(hi_in["wv"], 16)
            def root(v, r, n):
                pool.wait_ge(var_ready, n)
                pool.tensor_tensor(r[:], v[:], half[:], ALU.pow).then_inc(rstd_ready, 1)

            def low(hi, lo, raw, hi_sem, raw_sem, n, ready):
                pool.wait_ge(hi_sem, n)
                pool.wait_ge(raw_sem, n)
                pool.tensor_tensor(lo[:], raw[:], hi[:], ALU.subtract).then_inc(ready, 1)

            root(var, rstd, 1)
            pool.dma_start(ctx_hi[:], ctx_d[0]).then_inc(ctx_hi_in, 16)
            low(wq_hi, wq_lo, wq_raw, hi_in["wq"], raw_in["wq"], 16, w_ready["wq"])
            pool.dma_start(wo_hi[:], w_d["wo"]).then_inc(hi_in["wo"], 16)
            low(wk_hi, wk_lo, wk_raw, hi_in["wk"], raw_in["wk"], 16, w_ready["wk"])
            low(ctxT_hi, ctxT_lo, ctxT_raw, ctxT_hi_in, ctxT_raw_in, 16, ctxT_ready)
            low(wv_hi, wv_lo, wv_raw, hi_in["wv"], raw_in["wv"], 16, w_ready["wv"])
            low(ctx_hi, ctx_lo, ctx_raw, ctx_hi_in, ctx_raw_in, 16, ctx_ready)
            low(wo_hi, wo_lo, wo_raw, hi_in["wo"], raw_in["wo"], 16, w_ready["wo"])
            with pool.Fori(1, B) as b:
                pool.wait_ge(s_ready, b * 4)
                pool.dma_start(ctxT_hi[:], ctxT_d[b]).then_inc(ctxT_hi_in, 16)
                root(var, rstd, b * 2)
                low(ctxT_hi, ctxT_lo, ctxT_raw, ctxT_hi_in, ctxT_raw_in, b * 16 + 16, ctxT_ready)
                pool.wait_ge(m_ready, b * 22 - 6)
                hold(nc, nc.gpsimd, keep)
                pool.dma_start(ctx_hi[:], ctx_d[b]).then_inc(ctx_hi_in, 16)
                root(var2, rstd2, b * 2 + 1)
                low(ctx_hi, ctx_lo, ctx_raw, ctx_hi_in, ctx_raw_in, b * 16 + 16, ctx_ready)
            pool.wait_ge(m_ready, 22 * B - 10)
            for k in range(2):
                pool.dma_start(later.u_hi[:, k, :, :], io["u"][:, k]).then_inc(keep["up_hi_in"][k], 16)

            def split_up(k):
                pool.wait_ge(keep["up_hi_in"][k], 16)
                pool.wait_ge(keep["up_raw_in"][k], 16)
                pool.tensor_tensor(later.u_lo[:, k, :, :], later.u_raw[:, k, :, :], later.u_hi[:, k, :, :],
                                   ALU.subtract).then_inc(keep["up_ready"], 1)

            split_up(0)
            root(var2, rstd2, 2 * B)
            split_up(1)

        @block.scalar
        def _(act):
            m, t, nexp = Count(), Count(), Count()
            def high_m(out):
                act.wait_ge(m_ready, m.up())
                act.activation(out, ps_m[:, (m.n - 1) % 2, :], ACT.Copy).then_inc(m_hi, 1)

            def high_t(out):
                act.wait_ge(t_ready, t.up())
                act.activation(out, ps_t[:, (t.n - 1) % 2, :, :], ACT.Copy).then_inc(t_hi, 1)

            def exps(i):
                act.wait_ge(bias_ready, nexp.up())
                act.wait_ge(t_ready, t.now)
                act.activation(prob[:], ps_s[:, i % 2, :], ACT.Exp, bias=bias[:, i:i + 1], scale=SCALE,
                               accum_out=total[:, i:i + 1]).then_inc(p_ready, 1)

            def trans(i):
                for h in range(2):
                    high_t(pT_hi[:, 4 * h:4 * h + 4, i * P:(i + 1) * P])

            def attend(b):
                for i in range(IT):
                    if b is not None:
                        high_m(q_hi[:, i, :])
                    high_t(xnT_hi[:, :, i * P:(i + 1) * P])
                if b is not None:
                    m.up(4)
                for j in range(2 * DC):
                    high_m((q_hi if j < DC else k_hi)[:, j % DC, :])
                if b is not None:
                    t.up(4), m.up(2)
                exps(0)
                for i in range(1, IT):
                    trans(i - 1)
                    exps(i)
                    if i == 1 and b is not None:
                        router(b)
                for i in range(IT - 1):
                    high_m(k_hi[:, i, :])
                trans(IT - 1)
                high_m(k_hi[:, IT - 1, :])

            def router(b):
                act.wait_ge(lx_in, b)
                act.activation(lx[:], lx[:], ACT.Exp).then_inc(lx_ready, 1)

            attend(None)
            act.wait_ge(small_in, 48)
            act.activation(gates[:], gates[:], ACT.Tanh).then_inc(gate_ready, 1)
            with act.Fori(1, B) as b:
                k = b - 1
                m.enter(k, 22), t.enter(k, 16), nexp.enter(k, 4)
                attend(b)
                m.leave(B - 1), t.leave(B - 1), nexp.leave(B - 1)
            for j in range(DC):
                high_m(q_hi[:, j, :])
            router(B)

        @block.vector
        def _(dve):
            m, t, s, steps = Count(), Count(), Count(), Count()
            hm, ht = Count(), Count()

            def then(ins):
                ins.then_inc(step, 1)
                dve.wait_ge(step, steps.up())

            def low_m(hi, lo):
                m.up()
                dve.wait_ge(m_hi, hm.up())
                dve.tensor_tensor(lo, ps_m[:, (m.n - 1) % 2, :], hi, ALU.subtract).then_inc(m_free, 1)

            def low_t(hi, lo):
                t.up()
                dve.wait_ge(t_hi, ht.up())
                dve.tensor_tensor(lo, ps_t[:, (t.n - 1) % 2, :, :], hi, ALU.subtract).then_inc(t_free, 1)

            def norm_sums(mean_var, st, v):
                hold(nc, nc.vector, keep)
                for i in range(IT):
                    last = dve.bn_aggr(mean_var[:, i, :], st[:, i, :])
                then(last)
                dve.tensor_scalar(v[:], mean_var[:, :, 1], EPS, None, ALU.add).then_inc(var_ready, 1)

            def norm_apply(out, src, mean_var, r, n, ready):
                dve.wait_ge(rstd_ready, n)
                for i in range(IT):
                    dve.tensor_scalar(out[:, i, :], src[:, i, :], mean_var[:, i, 0:1], r[:, i:i + 1],
                                      ALU.subtract, ALU.mult).then_inc(ready, 1)

            def maxima(i):
                dve.wait_ge(s_ready, s.up())
                then(dve.tensor_reduce(top[:, i:i + 1], ps_s[:, i % 2, :], AX.X, ALU.max))
                dve.tensor_scalar(bias[:, i:i + 1], top[:, i:i + 1], -SCALE, None, ALU.mult).then_inc(bias_ready, 1)

            def trans(i):
                for h in range(2):
                    o = (slice(None), slice(4 * h, 4 * h + 4), slice(i * P, (i + 1) * P))
                    low_t(pT_hi[o], pT_lo[o])

            def residual(b):
                then(dve.reciprocal(inv[:], total[:]))
                then(dve.tensor_scalar(inv[:], inv[:], gates[:, 0:1], None, ALU.mult))
                dve.wait_ge(res_in, b * 16)
                for i in range(IT):
                    dve.wait_ge(m_ready, m.up())
                    ins = dve.scalar_tensor_tensor(out=r_t[:, i, :], in0=ps_m[:, (m.n - 1) % 2, :],
                                                   scalar=inv[:, i:i + 1], in1=r_t[:, i, :],
                                                   op0=ALU.mult, op1=ALU.add)
                    ins.then_inc(m_free, 1)
                    dve.wait_ge(m_free, m.now)
                    last = dve.bn_stats(stats2[:, i, :], r_t[:, i, :])
                then(last)
                norm_sums(mv2, stats2, var2)

            def route_turn(i):
                dve.wait_ge(t_ready, t.up())
                dve.tensor_copy(xn2T[:, :, i * P:(i + 1) * P], ps_t[:, (t.n - 1) % 2, :, :]).then_inc(t_free, 1)

            def route(b):
                rows = slice(4 * B - 4, 4 * B) if b is B else bass.ds(b * 4 - 4, 4)

                def logits():
                    dve.wait_ge(m_ready, m.up())
                    dve.tensor_copy(lgT[:], ps_m[0:E, (m.n - 1) % 2, :]).then_inc(m_free, 1)

                def shifted():
                    dve.wait_ge(m_ready, m.up())
                    dve.tensor_copy(lg[:], ps_m[:, (m.n - 1) % 2, 0:IT * E].rearrange("p (i e) -> p i e", e=E)
                                    ).then_inc(m_free, 1)
                    dve.wait_ge(m_free, m.now)
                    then(dve.tensor_reduce(lm[:], lg[:], AX.X, ALU.max))
                    dve.tensor_tensor(lx[:], lg[:], lm[:].unsqueeze(2).broadcast_to([P, IT, E]), ALU.subtract).then_inc(lx_in, 1)

                def softmax():
                    dve.wait_ge(lx_ready, b)
                    then(dve.tensor_reduce(ls[:], lx[:], AX.X, ALU.add))
                    then(dve.reciprocal(li[:], ls[:]))
                    then(dve.tensor_tensor(lg[:], lx[:], li[:].unsqueeze(2).broadcast_to([P, IT, E]), ALU.mult))
                    dve.tensor_copy(probs[:, rows, :], lg[:])

                return (logits, shifted, softmax,
                        *rank_experts(dve, then, lg[:], level, tri, larger, (equal, ranks[:, rows, :])))

            def attend(b):
                for i in range(IT):
                    if b is not None:
                        low_m(q_hi[:, i, :], q_lo[:, i, :])
                    o = (slice(None), slice(None), slice(i * P, (i + 1) * P))
                    low_t(xnT_hi[o], xnT_lo[o])
                if b is not None:
                    residual(b)
                for j in range(2 * DC):
                    hi, lo = (q_hi, q_lo) if j < DC else (k_hi, k_lo)
                    low_m(hi[:, j % DC, :], lo[:, j % DC, :])
                    if b is not None:
                        if j == DC - 1:
                            dve.wait_ge(x2_out, b * 16)
                            norm_apply(r_t, r_t, mv2, rstd2, b * 2 + 1, xn2_ready)
                        if j >= DC:
                            route_turn(j - DC)
                nothing = lambda: None
                logits, shifted, softmax, larger_, equal_, added = route(b) if b is not None else [nothing] * 6
                maxima(0)
                logits()
                maxima(1)
                shifted()
                trans(0)
                maxima(2)
                softmax()
                trans(1)
                maxima(3)
                larger_()
                trans(2)
                for i, other in enumerate((equal_, added, nothing)):
                    low_m(k_hi[:, i, :], k_lo[:, i, :])
                    other()
                trans(IT - 1)
                low_m(k_hi[:, IT - 1, :], k_lo[:, IT - 1, :])

            for i in range(IT):
                dve.wait_ge(first_x_in[i], 16)
                last = dve.bn_stats(stats[:, i, :], x_t[:, i, :])
            then(last)
            norm_sums(mv, stats, var)
            norm_apply(x_t, x_t, mv, rstd, 1, xn_ready)
            attend(None)
            dve.wait_ge(gate_ready, 1)
            dve.wait_ge(const_ready, 2)
            with dve.Fori(1, B) as b:
                k = b - 1
                for cnt, per in ((m, 22), (t, 16), (s, 4), (steps, 20), (hm, 16), (ht, 12)):
                    cnt.enter(k, per)
                dve.wait_ge(x_in, b * 16)
                for i in range(IT):
                    last = dve.bn_stats(stats[:, i, :], x_t[:, i, :])
                then(last)
                norm_sums(mv, stats, var)
                norm_apply(x_t, x_t, mv, rstd, b * 2, xn_ready)
                attend(b)
                for cnt in (m, t, s, steps, hm, ht):
                    cnt.leave(B - 1)
            for j in range(DC):
                low_m(q_hi[:, j, :], q_lo[:, j, :])
            residual(B)
            norm_apply(x_t, r_t, mv2, rstd2, 2 * B, xn2_ready)
            for i in range(IT):
                route_turn(i)
            for part in route(B)[0:3]:
                part()

        @block.tensor
        def _(pe):
            m, t, s = Count(), Count(), Count()

            def product(pairs, ahead=lambda c: None):
                m.up()
                if not isinstance(m.now, int) or m.now > 2:
                    pe.wait_ge(m_free, m.now - 2)
                tripled(pe, ps_m[:, (m.n - 1) % 2, :], pairs, ahead).then_inc(m_ready, 1)

            def transpose(tiles):
                t.up()
                if not isinstance(t.now, int) or t.now > 2:
                    pe.wait_ge(t_free, t.now - 2)
                for j, block_in in enumerate(tiles):
                    last = pe.transpose(ps_t[:, (t.n - 1) % 2, j, :], block_in, ident[:])
                last.then_inc(t_ready, 1)

            def cols(x, c, i):
                return x[0][:, c, i * P:(i + 1) * P], x[1][:, c, i * P:(i + 1) * P]

            def chunk(x, c):
                return x[0][:, c, :], x[1][:, c, :]

            xnT, q, kk, pT = (xnT_hi, xnT_lo), (q_hi, q_lo), (k_hi, k_lo), (pT_hi, pT_lo)
            wq, wk, wv, wo = (wq_hi, wq_lo), (wk_hi, wk_lo), (wv_hi, wv_lo), (wo_hi, wo_lo)
            ctxT, ctx = (ctxT_hi, ctxT_lo), (ctx_hi, ctx_lo)

            def turn_x(b, i):
                pe.wait_ge(xn_ready, i + 1 if b is None else b * 4 + (i + 1))
                transpose([x_t[:, i, c * P:(c + 1) * P] for c in range(DC)])

            def values(between=lambda j: None):
                split = m.now
                pe.wait_ge(t_free, t.now)

                def new_values(c):
                    if c == IT:
                        pe.wait_ge(m_free, split)

                for j in range(DC):
                    product([(cols(ctx, c, j), chunk(pT, c)) for c in range(IT)]
                            + [(cols(kk, c, j), chunk(pT, IT + c)) for c in range(IT)],
                            new_values if j == 0 else lambda c: None)
                    between(j)

            def project():
                split = m.now

                def output(c):
                    if c == 0:
                        pe.wait_ge(m_free, split - 1)
                    if c == DC - 1:
                        pe.wait_ge(m_free, split)

                for i in range(IT):
                    product([(cols(q, c, i), chunk(wo, c)) for c in range(DC)], output if i == 0 else lambda c: None)

            def turn_r(b, i):
                src = x_t if b is B else r_t
                pe.wait_ge(xn2_ready, b * 4 + (i - 3))
                transpose([src[:, i, c * P:(c + 1) * P] for c in range(DC)])

            def logits():
                pe.wait_ge(t_free, t.now)
                m.up()
                pe.wait_ge(m_free, m.now - 2)
                for c in range(DC):
                    last = pe.matmul(ps_m[0:E, (m.n - 1) % 2, :], wg[:, c, :], xn2T[:, c, :],
                                     start=(c == 0), stop=(c == DC - 1))
                last.then_inc(m_ready, 1)

            def turn_logits():
                m.up()
                for i in range(IT):
                    last = pe.transpose(ps_m[:, (m.n - 1) % 2, i * E:(i + 1) * E], lgT[:, i * P:(i + 1) * P],
                                        ident[0:E, 0:E])
                last.then_inc(m_ready, 1)

            def attend(b):
                if b is None:
                    pe.wait_ge(const_ready, 2)
                    for i in range(IT):
                        turn_x(b, i)
                else:
                    pe.wait_ge(ctx_ready, b)
                    values(lambda j: turn_x(b, j))
                    project()
                pe.wait_ge(t_free, t.now)
                if b is None:
                    pe.wait_ge(w_ready["wq"], 1)
                for j in range(DC):
                    product([(cols(wq, c, j), chunk(xnT, c)) for c in range(DC)])
                queries = m.now
                if b is None:
                    pe.wait_ge(w_ready["wk"], 1)
                for j in range(DC):
                    product([(cols(wk, c, j), chunk(xnT, c)) for c in range(DC)])
                    if b is not None:
                        turn_r(b, j)
                keys = m.now
                pe.wait_ge(m_free, queries)
                pe.wait_ge(ctxT_ready, 1 if b is None else b + 1)

                def scores(i):
                    s.up()
                    if b is not None or i > 1:
                        pe.wait_ge(p_ready, s.now - 2)
                    tripled(pe, ps_s[:, i % 2, 0:S], [(cols(q, c, i), chunk(ctxT, c)) for c in range(DC)])
                    if i == 0:
                        pe.wait_ge(m_free, keys)
                    if i == 1 and b is not None:
                        pe.wait_ge(m_free, m.now)
                    tripled(pe, ps_s[:, i % 2, S:2 * S],
                            [(cols(q, c, i), chunk(kk, c)) for c in range(DC)]).then_inc(s_ready, 1)

                def turn(i):
                    pe.wait_ge(p_ready, s.base + i + 1)
                    for h in range(2):
                        transpose([prob[:, (4 * h + n) * P:(4 * h + n + 1) * P] for n in range(4)])

                scores(0)
                if b is not None:
                    logits()
                for i in range(1, IT):
                    scores(i)
                    if i == 1 and b is not None:
                        turn_logits()
                    turn(i - 1)
                if b is None:
                    pe.wait_ge(w_ready["wv"], 1)
                for i in range(IT):
                    if i == IT - 1:
                        turn(i)
                    product([(cols(xnT, c, i), chunk(wv, c)) for c in range(DC)])

            attend(None)
            pe.wait_ge(w_ready["wo"], 1)
            pe.wait_ge(small_in, 48)
            with pe.Fori(1, B) as b:
                k = b - 1
                m.enter(k, 22), t.enter(k, 16), s.enter(k, 4)
                attend(b)
                m.leave(B - 1), t.leave(B - 1), s.leave(B - 1)
            pe.wait_ge(ctx_ready, B)
            values()
            project()
            for i in range(IT):
                turn_r(B, i)
            logits()
            pe.wait_ge(m_free, m.now)
            turn_logits()


def persistent(nc):
    small = Sbuf(nc, -(-nc.sbuf_base // 32) * 32)
    keep = {}
    keep["ident"] = small("ident", [P, P], F32)
    keep["probs"] = small("probs", [P, NT, E], F32)
    keep["ranks"] = small("ranks", [P, NT, E], F32)
    keep["gates"] = small("gates", [P, 2], F32)
    keep["idle"] = small("idle", [P, 8], F32)
    keep["weights"] = small("combine_weights", [P, NT, TOPK], F32)
    keep["slots"] = small("token_slots", [P, NT, TOPK], I32)
    keep["index"] = small("slot_tokens", [P, TILES_MAX + QUAD], I32)
    keep["last"] = small("last_quad", [P, 1], I32)
    keep["expert"] = small("tile_expert", [P, TILES_MAX], I32)
    for n in range(3):
        keep[f"at{n}"] = small(f"tile_weights_at{n}", [P, TILES_MAX], I32)
    keep["turn"] = small("tile_turn", [P, TILES_MAX], I32)
    keep["phase_at"] = small.at
    keep["end"] = keep["phase_at"] + PHASE_SMALL
    return keep


W13 = 2 * DC * FF
W2 = 2 * D
WE = W13 + W2 + D


PHASE_SMALL = 4864
BUFFERS = 3


class Later:

    def __init__(self, nc, first_free):
        sb = Sbuf(nc, first_free)
        self.u_hi, self.u_lo, self.u_raw = sb.split("shared_up", [P, 2, DC, SF])
        at = sb.at
        self.w_hi, self.w_lo, self.w_raw = sb.split("expert", [P, BUFFERS * WE])
        self.rest_at = sb.at
        self.xg = [sb(f"xg{v}", [P, D], F32) for v in range(QUAD)]
        self.behind_xg = sb.at
        self.first_hi = at
        self.second_hi, self.second_lo = at + 4 * WE, at + 4 * (BUFFERS + 1) * WE
        self.second_size = 4 * (BUFFERS - 1) * WE
        over = Sbuf(nc, self.second_hi)
        last = over("first_xs3", [P, D], F32)
        over.at = first_free + 4 * 4 * DC * D * 2
        self.first_xs = [over(f"first_xs{i}", [P, D], F32) for i in range(IT - 1)] + [last]
        self.d_hi, self.d_lo, self.d_raw = over.split("shared_down", [P, SC, D])
        assert over.at <= self.second_hi + self.second_size
        over = Sbuf(nc, self.second_hi)
        self.last_d_hi = over("last_down_hi", [P, SC, D], F32R)
        xs = [over(f"last_xs{i}", [P, D], F32) for i in range(2)]
        assert over.at <= self.second_hi + 4 * WE
        low = [Sbuf(nc, self.second_lo) for _ in range(2)]
        self.last_d_lo = low[0]("last_down_lo", [P, SC, D], F32R)
        self.last_d_raw = low[1]("last_down_raw", [P, SC, D], F32)
        self.last_xs = xs + [low[0](f"last_xs{i}", [P, D], F32) for i in range(2, 4)]
        assert low[0].at <= self.second_lo + 4 * WE
        self.free = [(self.first_hi, 4 * WE), (self.second_hi + 4 * WE, 8 * WE), (self.second_lo + 4 * WE, 4 * WE)]


class Shared:

    def __init__(self, nc, c, mem, keep, later, first, down, xs, xs_in, tag):
        sem = lambda n: c.enter_context(nc.semaphore(tag + n))
        sb = Sbuf(nc, later.rest_at)
        self.keep, self.up, self.down, self.first = keep, (later.u_hi, later.u_lo), down, first
        self.xs, self.xs_in = xs, xs_in
        self.x = sb(tag + "xT_hi", [P, DC, S], F32R), sb(tag + "xT_lo", [P, DC, S], F32R)
        self.h = sb(tag + "h_hi", [P, SC, S], F32R), sb(tag + "h_lo", [P, SC, S], F32R)
        self.gate = sb(tag + "silu", [P, 2, S], F32)
        self.hf = sb(tag + "h", [P, 2, S], F32)
        self.end = sb.at
        psum = lambda n, shape: c.enter_context(nc.psum_tensor(tag + n, shape, F32))
        self.ps_t = psum("ps_t", [P, 2, 4, P])
        self.ps_u = psum("ps_u", [P, 2, 2, S])
        self.ps_y = psum("ps_y", [P, 2, D])
        self.t_ready, self.t_hi, self.t_free = sem("t_ready"), sem("t_hi"), sem("t_free")
        self.u_ready, self.gate_ready, self.u_free = sem("u_ready"), sem("gate_ready"), sem("u_free")
        self.h_hi, self.h_lo = sem("h_hi"), sem("h_lo")
        self.y_ready, self.y_free = sem("y_ready"), sem("y_free")
        self.xn2 = mem["xn2"].rearrange("(n p) d -> n p d", p=P)

    @staticmethod
    def rows(j):
        return P if j < SC - 1 else ST

    def load(self, sp, n, i):
        if n:
            sp.wait_ge(self.t_ready, i + 1)
        sp.dma_start(self.xs[i][:], self.xn2[(self.first + n) * IT + i]).then_inc(self.xs_in[n][i], 16)

    def tensor(self, pe, up_ready, down_ready, ahead_up=lambda n, j: None, ahead_down=lambda n, i: None):
        def turn(n, i):
            if n * IT + i >= 2:
                pe.wait_ge(self.t_free, n * IT + i - 1)
            pe.wait_ge(self.xs_in[n][i], 16)
            for c in range(DC):
                last = pe.transpose(self.ps_t[:, i % 2, c, :], self.xs[i][:, c * P:(c + 1) * P], self.keep["ident"][:])
            last.then_inc(self.t_ready, 1)

        def up(n, j):
            if n * SC + j >= 2:
                pe.wait_ge(self.u_free, n * SC + j - 1)
            rows = self.rows(j)
            for k in range(2):
                pairs = [([w[:, k, c, j * P:j * P + rows] for w in self.up], [v[:, c, :] for v in self.x])
                         for c in range(DC)]
                last = tripled(pe, self.ps_u[0:rows, j % 2, k, :], pairs)
            last.then_inc(self.u_ready, 1)

        def down(n, i):
            if n * IT + i >= 2:
                pe.wait_ge(self.y_free, n * IT + i - 1)
            pairs = [([v[0:self.rows(j), j, i * P:(i + 1) * P] for v in self.h],
                      [w[0:self.rows(j), j, :] for w in self.down]) for j in range(SC)]
            split = (lambda j: pe.wait_ge(self.h_lo, n * SC + j + 1)) if i == 0 else (lambda j: None)
            tripled(pe, self.ps_y[:, i % 2, :], pairs, split).then_inc(self.y_ready, 1)

        for i in range(IT):
            turn(0, i)
        up_ready()
        for n in range(2):
            pe.wait_ge(self.t_free, n * IT + IT)
            for j in range(SC):
                ahead_up(n, j)
                up(n, j)
            if n == 0:
                turn(1, 0), turn(1, 1)
                down_ready()
            for i in range(IT):
                ahead_down(n, i)
                down(n, i)
                if n == 0 and i < 2:
                    turn(1, i + 2)

    def scalar(self, act):
        def turn(n, i):
            act.wait_ge(self.t_ready, n * IT + i + 1)
            act.activation(self.x[0][:, :, i * P:(i + 1) * P], self.ps_t[:, i % 2, :, :], ACT.Copy).then_inc(self.t_hi, 1)

        def high(n, j):
            rows = self.rows(j)
            act.wait_ge(self.u_free, n * SC + j + 1)
            act.activation(self.h[0][0:rows, j, :], self.hf[0:rows, j % 2, :], ACT.Copy).then_inc(self.h_hi, 1)

        for i in range(IT):
            turn(0, i)
        for n in range(2):
            for j in range(SC):
                rows = self.rows(j)
                act.wait_ge(self.u_ready, n * SC + j + 1)
                act.activation(self.gate[0:rows, j % 2, :], self.ps_u[0:rows, j % 2, 0, :], ACT.Silu).then_inc(self.gate_ready, 1)
                if j:
                    high(n, j - 1)
            high(n, SC - 1)
            if n == 0:
                for i in range(IT):
                    turn(1, i)

    def vector(self, dve, total, between):
        def turn(n, i):
            o = (slice(None), slice(None), slice(i * P, (i + 1) * P))
            dve.wait_ge(self.t_hi, n * IT + i + 1)
            dve.tensor_tensor(self.x[1][o], self.ps_t[:, i % 2, :, :], self.x[0][o], ALU.subtract).then_inc(self.t_free, 1)

        def low(n, j):
            rows = self.rows(j)
            dve.wait_ge(self.h_hi, n * SC + j + 1)
            dve.tensor_tensor(self.h[1][0:rows, j, :], self.hf[0:rows, j % 2, :], self.h[0][0:rows, j, :],
                              ALU.subtract).then_inc(self.h_lo, 1)

        for i in range(IT):
            turn(0, i)
        for n in range(2):
            for j in range(SC):
                rows = self.rows(j)
                dve.wait_ge(self.gate_ready, n * SC + j + 1)
                if n * SC + j >= 2:
                    dve.wait_ge(self.h_lo, n * SC + j - 1)
                dve.tensor_tensor(self.hf[0:rows, j % 2, :], self.ps_u[0:rows, j % 2, 1, :], self.gate[0:rows, j % 2, :],
                                  ALU.mult).then_inc(self.u_free, 1)
                if j:
                    low(n, j - 1)
                if j < SC - 1:
                    between(n, j)
            low(n, SC - 1)
            if n == 0:
                turn(1, 0), turn(1, 1)
            between(n, SC - 1)
            for i in range(IT):
                to = total(n, i)
                dve.wait_ge(self.y_ready, n * IT + i + 1)
                dve.scalar_tensor_tensor(out=to[:], in0=self.ps_y[:, i % 2, :], scalar=self.keep["gates"][:, 1:2],
                                         in1=to[:], op0=ALU.mult, op1=ALU.add).then_inc(self.y_free, 1)
                if n == 0 and i < 2:
                    turn(1, i + 2)
                between(n, SC + i)


def part(w, rows, base, start, n):
    return w[0:rows, base + start:base + start + n] if isinstance(base, int) else w[0:rows, bass.ds(base + start, n)]


def load_expert(eng, w, base, io, e, sem):
    eng.dma_start(part(w, P, base, 0, W13 + W2), io["we"][e]).then_inc(sem, 16)
    eng.dma_start(part(w, FT, base, W13 + W2, D), io["we_rest"][e]).then_inc(sem, 16)


def split_expert(eng, later, base, sem):
    for rows, start, n in ((P, 0, W13 + W2), (FT, W13 + W2, D)):
        hi, lo, raw = (part(w, rows, base, start, n) for w in (later.w_hi, later.w_lo, later.w_raw))
        last = eng.tensor_tensor(lo, raw, hi, ALU.subtract)
    last.then_inc(sem, 1)


def load_down(eng, w, io, sem):
    eng.dma_start(w[:, 0:SC - 1, :], io["d"]).then_inc(sem, 16)
    eng.dma_start(w[0:ST, SC - 1, :], io["d_rest"]).then_inc(sem, 16)


def split_down(eng, d_hi, d_lo, d_raw, sem):
    for chunks, rows in ((slice(0, SC - 1), P), (slice(SC - 1, SC), ST)):
        hi, lo, raw = (w[0:rows, chunks, :] for w in (d_hi, d_lo, d_raw))
        eng.tensor_tensor(lo, raw, hi, ALU.subtract).then_inc(sem, 1)


def routing_phase(nc, io, mem, keep, later):
    with ExitStack() as c:
        sem = lambda n: c.enter_context(nc.semaphore("b_" + n))
        sh = Shared(nc, c, mem, keep, later, 0, (later.d_hi, later.d_lo), later.first_xs,
                    [keep["first_xs_in"], [sem(f"xs{i}_in") for i in range(IT)]], "b_")
        rest = Sbuf(nc, sh.end)
        acc = [rest(f"acc{u}", [P, D], F32) for u in range(2)]
        assert rest.at <= nc.sbuf_usable_end
        over = Sbuf(nc, later.second_lo)
        level = over("b_rank_level", [P, IT, E, E], F16)
        larger, equal = over("b_rank_larger", [P, IT, E], F32), over("b_rank_equal", [P, IT, E], F32)
        lower = over("b_lower_index", [P, E, E], F16)
        over = Sbuf(nc, later.second_lo)
        row_hot = over("slot_hot", [P, NT * TOPK, P], F16)
        tile_hot = over("tile_hot", [P, NT * TOPK, TILES_MAX], F16)
        grid = Sbuf(nc, over.at)("grid", [P, TILES_MAX, E], F32)
        f = {k: over("r_" + k, [P, NT, E], F32) for k in ("within", "totals", "s0", "s1", "slot", "one")}
        assert over.at <= later.second_lo + later.second_size
        small = Sbuf(nc, keep["phase_at"])
        mask, strict, ones = small("mask", [P, NT * E], F16), small("strict", [P, P], F16), small("ones", [P, P], F16)
        lane, lane_i = small("lane", [P, P], F32), small("lane_i", [P, P], I32)
        token, token_i = small("token", [P, NT], F32), small("token_i", [P, NT], I32)
        e_f = {k: small("e_" + k, [P, E], F32) for k in ("n", "tiles", "c0", "c1", "base", "first")}
        e_i = small("e_int", [P, E], I32)
        m3 = small("by_three", [P, TILES_MAX], I32)
        t_g = small("per_tile_too", [P, TILES_MAX], F32)
        hi_i, lo_i = small("tile_no_i", [P, NT * TOPK], I32), small("row_no_i", [P, NT * TOPK], I32)
        tile_no, row_no = small("tile_no", [P, NT * TOPK], F32), small("row_no", [P, NT * TOPK], F32)
        slot_f = small("slot_f", [P, NT, TOPK], F32)
        t_f = small("per_tile", [P, TILES_MAX], F32)
        assert small.at <= keep["end"], small.at

        raw_in = {k: sem(k + "_raw_in") for k in ("down", "first")}
        hi_in = {k: sem(k + "_hi_in") for k in ("down", "first")}
        down_ready = sem("down_ready")
        acc_in, acc_out = ([sem(f"acc{u}_{n}") for u in range(2)] for n in ("in", "out"))
        first_ready = keep["first_ready"]
        mask_ready, made, const_ready = sem("mask_ready"), sem("made"), sem("const_ready")
        counted, taken = sem("counted"), sem("counts_taken")
        hot_ready, listed, index_ready = sem("hot_ready"), sem("listed"), sem("index_ready")
        step = sem("dve_step")
        block = c.enter_context(nc.Block())
        x2_d = mem["x2"].rearrange("(n p) d -> n p d", p=P)
        base_d = mem["base"].rearrange("(n p) d -> n p d", p=P)

        @block.sync
        def _(sp):
            def residual(k):
                sp.dma_start(acc[k % 2][:], x2_d[k]).then_inc(acc_in[k % 2], 16)

            sh.load(sp, 0, IT - 1)
            load_down(sp, later.d_raw, io, raw_in["down"])
            residual(0), residual(1)
            load_expert(sp, later.w_raw, 0, io, 0, raw_in["first"])
            for i in range(IT):
                sh.load(sp, 1, i)
            for k in range(2 * IT):
                sp.wait_ge(sh.y_free, k + 1)
                sp.dma_start(base_d[k], acc[k % 2][:]).then_inc(acc_out[k % 2], 16)
                sp.wait_ge(acc_out[k % 2], (k // 2) * 16 + 16)
                if k + 2 < 2 * IT:
                    residual(k + 2)

        @block.gpsimd
        def _(pool):
            load_down(pool, later.d_hi, io, hi_in["down"])
            pool.memset(strict[:], 1.0).then_inc(made, 1)
            pool.memset(ones[:], 1.0).then_inc(made, 1)
            pool.iota(lane_i[:], [[1, P]], base=0, channel_multiplier=0).then_inc(made, 1)
            pool.iota(token_i[:], [[P, NT]], base=0, channel_multiplier=1).then_inc(made, 1)
            pool.memset(lower[:], 1.0).then_inc(made, 1)
            pool.wait_ge(made, 5)
            pool.affine_select(out=lower[:], in_=lower[:], compare_op=ALU.is_gt, fill=0.0, base=0,
                               pattern=[[1, E], [-1, E]], channel_multiplier=0).then_inc(const_ready, 1)
            pool.affine_select(out=strict[:], in_=strict[:], compare_op=ALU.is_gt, fill=0.0, base=0,
                               pattern=[[1, P]], channel_multiplier=-1).then_inc(const_ready, 1)
            pool.tensor_copy(lane[:], lane_i[:]).then_inc(const_ready, 1)
            pool.tensor_copy(token[:], token_i[:]).then_inc(const_ready, 1)
            load_expert(pool, later.w_hi, 0, io, 0, hi_in["first"])
            pool.wait_ge(hi_in["down"], 32)
            pool.wait_ge(raw_in["down"], 32)
            split_down(pool, later.d_hi, later.d_lo, later.d_raw, down_ready)
            pool.wait_ge(hi_in["first"], 32)
            pool.wait_ge(raw_in["first"], 32)
            split_expert(pool, later, 0, first_ready)
            pool.wait_ge(index_ready, 1)
            pool.wait_ge(sh.u_ready, 2 * SC)
            for v in range(QUAD):
                pool.indirect_dma_start(later.xg[v][:], None, mem["xn2"], bass.IndirectOffsetOnAxis(
                    ap=keep["index"][:, v:v + 1], axis=0)).then_inc(keep["gathered"][v], 16)

        @block.scalar
        def _(act):
            sh.scalar(act)

        @block.vector
        def _(dve):
            steps = Count()
            ps_c = sh.ps_y

            def then(ins):
                ins.then_inc(step, 1)
                dve.wait_ge(step, steps.up())

            def running(src, a, b, n, cut):
                d = 1
                then(dve.tensor_copy(a[:], src))
                while d < n:
                    dve.tensor_copy(cut(b, 0, d), cut(a, 0, d))
                    then(dve.tensor_tensor(cut(b, d, n), cut(a, d, n), cut(a, 0, n - d), ALU.add))
                    a, b, d = b, a, 2 * d
                return a

            def count():
                incl = running(f["totals"][:], f["s0"], f["s1"], NT, lambda x, p, q: x[:, p:q, :])
                then(dve.tensor_copy(e_i[:], incl[:, NT - 1, :]))
                then(dve.tensor_tensor(f["slot"][:], incl[:], f["totals"][:], ALU.subtract))
                then(dve.tensor_tensor(f["slot"][:], f["slot"][:], f["within"][:], ALU.add))
                then(dve.tensor_scalar(e_i[:], e_i[:], P - 1, None, ALU.add))
                then(dve.tensor_scalar(e_i[:], e_i[:], P.bit_length() - 1, None, ALU.logical_shift_right))
                then(dve.tensor_scalar(e_f["tiles"][:], e_i[:], 1.0, None, ALU.max))
                cum = running(e_f["tiles"][:], e_f["c0"], e_f["c1"], E, lambda x, p, q: x[:, p:q])
                then(dve.tensor_tensor(e_f["first"][:], cum[:], e_f["tiles"][:], ALU.subtract))
                then(dve.tensor_scalar(e_f["base"][:], e_f["first"][:], float(P), None, ALU.mult))
                then(dve.tensor_tensor(f["slot"][:], f["slot"][:],
                                       e_f["base"][:].unsqueeze(1).broadcast_to([P, NT, E]), ALU.add))
                keep["cum"] = cum

            def choose(ks):
                for k in ks:
                    for what, out in ((f["slot"], slot_f), (keep["probs"], keep["weights"])):
                        then(dve.scalar_tensor_tensor(out=f["one"][:], in0=keep["ranks"][:], scalar=float(k),
                                                      in1=what[:], op0=ALU.is_equal, op1=ALU.mult))
                        then(dve.tensor_reduce(out[:, :, k], f["one"][:], AX.X, ALU.add))

            def number():
                then(dve.tensor_scalar(keep["weights"][:], keep["weights"][:], keep["gates"][:, 1:2], None, ALU.mult))
                then(dve.tensor_copy(keep["slots"][:], slot_f[:]))
                flat = keep["slots"][:].rearrange("p j k -> p (j k)")
                dve.tensor_scalar(hi_i[:], flat, P.bit_length() - 1, None, ALU.logical_shift_right)
                then(dve.tensor_scalar(lo_i[:], flat, P - 1, None, ALU.bitwise_and))
                dve.tensor_copy(tile_no[:], hi_i[:])
                then(dve.tensor_copy(row_no[:], lo_i[:]))

            def one_hot(j):
                n = NT * TOPK
                for i in range(j * n // 8, (j + 1) * n // 8):
                    dve.tensor_scalar(row_hot[:, i, :], lane[:], row_no[:, i:i + 1], None, ALU.is_equal)
                    last = dve.tensor_scalar(tile_hot[:, i, :], lane[:, 0:TILES_MAX], tile_no[:, i:i + 1],
                                             token[:, i // TOPK:i // TOPK + 1], ALU.is_equal, ALU.mult)
                last.then_inc(hot_ready, 1)

            def per_tile(rows, op, out, n):
                then(dve.tensor_tensor(grid[:, :, 0:n], lane[:, 0:TILES_MAX].unsqueeze(2).broadcast_to([P, TILES_MAX, n]),
                                       rows.unsqueeze(1).broadcast_to([P, TILES_MAX, n]), op))
                then(dve.tensor_reduce(out, grid[:, :, 0:n], AX.X, ALU.add))

            def schedule():
                cum = keep["cum"]
                then(dve.tensor_copy(keep["last"][:], cum[:, E - 1:E]))
                then(dve.tensor_scalar(keep["last"][:], keep["last"][:], -1, None, ALU.add))
                then(dve.tensor_scalar(keep["last"][:], keep["last"][:], QUAD.bit_length() - 1, None, ALU.logical_shift_right))
                per_tile(cum[:], ALU.is_ge, t_f[:], E)
                then(dve.tensor_scalar(keep["expert"][:], t_f[:], float(E - 1), None, ALU.min))

            def places(ns):
                for n in ns:
                    at = keep[f"at{n}"]
                    then(dve.tensor_scalar(at[:], keep["expert"][:], n, None, ALU.add))
                    then(dve.tensor_scalar(m3[:], at[:], 11, None, ALU.mult))
                    then(dve.tensor_scalar(m3[:], m3[:], 5, None, ALU.logical_shift_right))
                    then(dve.scalar_tensor_tensor(out=at[:], in0=m3[:], scalar=-3.0, in1=at[:], op0=ALU.mult, op1=ALU.add))
                    then(dve.tensor_scalar(at[:], at[:], float(WE), None, ALU.mult))

            def turns():
                per_tile(e_f["first"][:, 0:E - 1], ALU.is_equal, t_f[:], E - 1)
                per_tile(e_f["first"][:, 0:E - 2], ALU.is_equal, t_g[:], E - 2)
                then(dve.tensor_tensor(keep["turn"][:], t_f[:], t_g[:], ALU.add))

            def rank():
                dve.wait_ge(const_ready, 4)
                last = slice((B - 1) * IT, B * IT)
                for part in rank_experts(dve, then, keep["probs"][:, last, :], level, lower, larger,
                                         (equal, keep["ranks"][:, last, :])):
                    part()

            def choices():
                dve.tensor_scalar(mask[:], keep["ranks"][:].rearrange("p j e -> p (j e)"), float(TOPK), None,
                                  ALU.is_lt).then_inc(mask_ready, 1)

            def counts():
                dve.wait_ge(counted, 1)
                dve.tensor_copy(f["within"][:], ps_c[:, 0, 0:NT * E].rearrange("p (j e) -> p j e", e=E))
                dve.tensor_copy(f["totals"][:], ps_c[:, 1, 0:NT * E].rearrange("p (j e) -> p j e", e=E)).then_inc(taken, 1)
                dve.wait_ge(taken, 1)
                count()

            work = [rank, choices, lambda: None, counts, lambda: choose((0, 1)), lambda: choose((2, 3)),
                    lambda: (number(), schedule()), lambda: places(range(BUFFERS)), turns,
                    *((lambda j=j: one_hot(j)) for j in range(8))]
            assert len(work) == 2 * (SC + IT) - 3

            def between(n, k):
                at = n * (SC + IT) + k
                if at < len(work):
                    work[at]()
                elif at == len(work):
                    then(dve.memset(keep["index"][:], 0))
                    dve.wait_ge(listed, 1)
                    dve.tensor_copy(keep["index"][:, 0:TILES_MAX], sh.ps_t[:, 0, 0, 0:TILES_MAX]).then_inc(index_ready, 1)

            def total(n, i):
                dve.wait_ge(acc_in[i % 2], n * 32 + (i // 2) * 16 + 16)
                return acc[i % 2]

            sh.vector(dve, total, between)

        @block.tensor
        def _(pe):
            def count_masks(n, j):
                if (n, j) != (0, 3):
                    return
                pe.wait_ge(const_ready, 4)
                pe.wait_ge(mask_ready, 1)
                pe.matmul(sh.ps_y[:, 0, 0:NT * E], strict[:], mask[:], start=True, stop=True)
                pe.matmul(sh.ps_y[:, 1, 0:NT * E], ones[:], mask[:], start=True, stop=True).then_inc(counted, 1)

            def down_ready_and_free():
                pe.wait_ge(down_ready, 2)
                pe.wait_ge(taken, 1)

            def list_slots(n, i):
                if (n, i) != (1, IT - 2):
                    return
                pe.wait_ge(hot_ready, 8)
                pe.wait_ge(sh.t_free, 2 * IT)
                slots = NT * TOPK
                for k in range(slots):
                    last = pe.matmul(sh.ps_t[:, 0, 0, 0:TILES_MAX], row_hot[:, k, :], tile_hot[:, k, :],
                                     start=(k == 0), stop=(k == slots - 1))
                last.then_inc(listed, 1)

            sh.tensor(pe, lambda: pe.wait_ge(keep["up_ready"], 2), down_ready_and_free, count_masks, list_slots)


def expert_phase(nc, io, mem, keep, later):
    with ExitStack() as c:
        sem = lambda n: c.enter_context(nc.semaphore("c_" + n))
        sb = Sbuf(nc, later.behind_xg)
        xg, gathered = later.xg, keep["gathered"]
        x = [(sb(f"xT_hi{u}", [P, DC, P], F32R), sb(f"xT_lo{u}", [P, DC, P], F32R)) for u in range(2)]
        gate = [sb(f"gate{u}", [P, FF], F32) for u in range(2)]
        hf = [sb(f"hf{u}", [P, FF], F32) for u in range(2)]
        h = [(sb(f"hT_hi{u}", [P, FC, P], F32R), sb(f"hT_lo{u}", [P, FC, P], F32R)) for u in range(2)]
        y = [sb(f"y{v}", [P, D], F32) for v in range(QUAD)]
        column = [sb(f"column{v}", [P, 1], I32) for v in range(QUAD)]
        zeros = sb("zeros", [P, D], F32)
        assert sb.at <= nc.sbuf_usable_end, sb.at
        ps_u = c.enter_context(nc.psum_tensor("c_ps_u", [P, 2, 2, 512], F32))
        ps_x = c.enter_context(nc.psum_tensor("c_ps_x", [P, 4, P], F32))
        ps_h = c.enter_context(nc.psum_tensor("c_ps_h", [P, 4, P], F32))
        ps_y = c.enter_context(nc.psum_tensor("c_ps_y", [P, 2, D], F32))
        x_turned, x_hi, x_split = sem("x_turned"), sem("x_hi"), sem("x_split")
        u_ready, gate_ready, h_ready = sem("u_ready"), sem("gate_ready"), sem("h_ready")
        h_turned, h_hi, h_split = sem("h_turned"), sem("h_hi"), sem("h_split")
        y_ready, y_taken = sem("y_ready"), sem("y_taken")
        y_out = [sem(f"y_out{v}") for v in range(QUAD)]
        w_in, w_ready = sem("w_in"), keep["first_ready"]
        column_ready, zeros_ready, rest_out = sem("column_ready"), sem("zeros_ready"), sem("rest_out")
        block = c.enter_context(nc.Block())
        y_d = mem["y"].rearrange("(t p) d -> t p d", p=P)
        xn2_d = mem["xn2"].rearrange("(n p) d -> n p d", p=P)

        def number(eng, t, k, low, high):
            at = keep[k][0:1, t:t + 1] if isinstance(t, int) else keep[k][0:1, bass.ds(t, 1)]
            return eng.value_load(at, min_val=low, max_val=high)

        def wait(eng, s, value):
            if not isinstance(value, int) or value > 0:
                eng.wait_ge(s, value)

        def tiles(eng, step):
            for v in range(QUAD):
                step(v, v)
            last = number(eng, 0, "last", E // QUAD - 1, TILES_MAX // QUAD - 1)
            with eng.Fori(1, last + 1) as i:
                for v in range(QUAD):
                    step(i * QUAD + v, v)
            return last

        @block.sync
        def _(sp):
            sp.wait_ge(zeros_ready, 1)
            last = number(sp, 0, "last", E // QUAD - 1, TILES_MAX // QUAD - 1)
            with sp.Fori(0, REST) as t:
                sp.dma_start(y_d[last * QUAD + QUAD + t], zeros[:]).then_inc(rest_out, 16)
            sp.wait_ge(rest_out, REST * 16)

        @block.gpsimd
        def _(pool):
            pool.memset(zeros[:], 0.0).then_inc(zeros_ready, 1)

            def gather(v, at):
                pool.indirect_dma_start(xg[v][:], None, mem["xn2"],
                                        bass.IndirectOffsetOnAxis(ap=at, axis=0)).then_inc(gathered[v], 16)

            def load(base, e):
                load_expert(pool, later.w_hi, base, io, e, w_in)
                load_expert(pool, later.w_raw, base, io, e, w_in)

            load(WE, 1)

            def step(t, v):
                pool.wait_ge(gathered[v], (t + (QUAD - v)) * 4)
                pool.tensor_copy(column[v][:], keep["index"][:, t + QUAD:t + QUAD + 1] if isinstance(t, int)
                                 else keep["index"][:, bass.ds(t + QUAD, 1)]).then_inc(column_ready, 1)
                pool.wait_ge(x_turned, t + 1)
                pool.wait_ge(column_ready, t + 1)
                hold(nc, nc.gpsimd, keep)
                gather(v, column[v][:])
                flag = number(pool, t, "turn", 0, 2)
                with pool.If(flag > 0):
                    e = number(pool, t, "expert", 0, E - 2)
                    base = number(pool, t, "at1", 0, (BUFFERS - 1) * WE)
                    pool.wait_ge(w_in, e * 64 + 64)
                    split_expert(pool, later, base, w_ready)
                    base = number(pool, t, "at2", 0, (BUFFERS - 1) * WE)
                    wait(pool, y_ready, t)
                    hold(nc, nc.gpsimd, keep, 5)
                    with pool.If(flag > 1):
                        load(base, number(pool, t, "expert", 0, E - 3) + 2)
                    with pool.Else():
                        load_down(pool, later.last_d_hi, io, keep["last_down_in"])
                        load_down(pool, later.last_d_raw, io, keep["last_down_in"])
                        for i in range(IT):
                            pool.dma_start(later.last_xs[i][:], xn2_d[2 * IT + i]).then_inc(keep["last_xs_in"][i], 16)
                with pool.Else():
                    pass

            last = tiles(pool, step)
            for v in range(QUAD):
                pool.wait_ge(gathered[v], last * 16 + 32)

        @block.scalar
        def _(act):
            def turn(t, u):
                act.wait_ge(x_turned, t + 1)
                act.activation(x[u][0][:], ps_x[:], ACT.Copy).then_inc(x_hi, 1)

            def take(t, v):
                act.wait_ge(y_ready, t + 1)
                wait(act, y_out[v], (t - v) * 4)
                act.activation(y[v][:], ps_y[:, v % 2, :], ACT.Copy).then_inc(y_taken, 1)
                act.wait_ge(y_taken, t + 1)
                act.dma_start(y_d[t], y[v][:]).then_inc(y_out[v], 16)

            def step(t, v):
                u = v % 2
                act.wait_ge(u_ready, t + 1)
                act.activation(gate[u][:], ps_u[:, u, 0, 0:FF], ACT.Silu).then_inc(gate_ready, 1)
                turn(t + 1, 1 - u)
                if not isinstance(t, int) or t > 0:
                    take(t - 1, (v - 1) % QUAD)
                act.wait_ge(h_turned, t + 1)
                act.activation(h[u][0][:, 0:2, :], ps_h[:, 0:2, :], ACT.Copy)
                act.activation(h[u][0][0:FT, 2, :], ps_h[0:FT, 2, :], ACT.Copy).then_inc(h_hi, 1)

            turn(0, 0)
            last = tiles(act, step)
            take(last * QUAD + (QUAD - 1), QUAD - 1)
            for v in range(QUAD):
                act.wait_ge(y_out[v], last * 16 + 16)
            hold(nc, nc.scalar, keep)

        @block.vector
        def _(dve):
            def turn(t, u):
                dve.wait_ge(x_hi, t + 1)
                dve.tensor_tensor(x[u][1][:], ps_x[:], x[u][0][:], ALU.subtract).then_inc(x_split, 1)

            def step(t, v):
                u = v % 2
                dve.wait_ge(gate_ready, t + 1)
                dve.tensor_tensor(hf[u][:], ps_u[:, u, 1, 0:FF], gate[u][:], ALU.mult).then_inc(h_ready, 1)
                turn(t + 1, 1 - u)
                dve.wait_ge(h_hi, t + 1)
                dve.tensor_tensor(h[u][1][:, 0:2, :], ps_h[:, 0:2, :], h[u][0][:, 0:2, :], ALU.subtract)
                dve.tensor_tensor(h[u][1][0:FT, 2, :], ps_h[0:FT, 2, :], h[u][0][0:FT, 2, :],
                                  ALU.subtract).then_inc(h_split, 1)

            turn(0, 0)
            tiles(dve, step)

        @block.tensor
        def _(pe):
            def turn(t, v):
                pe.wait_ge(gathered[v], (t + (QUAD - v)) * 4)
                wait(pe, x_split, t)
                for k in range(DC):
                    last = pe.transpose(ps_x[:, k, :], xg[v][:, k * P:(k + 1) * P], keep["ident"][:])
                last.then_inc(x_turned, 1)

            def weights(base, start, n, rows=P):
                return [part(w, rows, base, start, n) for w in (later.w_hi, later.w_lo)]

            def down(t, u, base):
                pe.wait_ge(h_split, t + 1)
                wait(pe, y_taken, t - 1)
                pairs = []
                for j in range(FC):
                    rows = P if j < FC - 1 else FT
                    pairs.append(([v[0:rows, j, :] for v in h[u]], weights(base, W13 + j * D, D, rows)))
                tripled(pe, ps_y[:, u, :], pairs).then_inc(y_ready, 1)

            def numbers(t):
                return number(pe, t, "expert", 0, E - 1), number(pe, t, "at0", 0, (BUFFERS - 1) * WE)

            now, before = [], []

            def step(t, v):
                u = v % 2
                e, base = numbers(t) if v == 0 else now.pop()
                pe.wait_ge(x_split, t + 1)
                pe.wait_ge(w_ready, e + 1)
                wait(pe, h_ready, t - 1)
                for k in range(2):
                    last = tripled(pe, ps_u[:, u, k, 0:FF], [
                        ([v[:, c_, :] for v in x[u]], weights(base, (k * DC + c_) * FF, FF)) for c_ in range(DC)])
                last.then_inc(u_ready, 1)
                turn(t + 1, (v + 1) % QUAD)
                if not isinstance(t, int) or t > 0:
                    down(t - 1, 1 - u, before.pop() if v else number(pe, t - 1, "at0", 0, (BUFFERS - 1) * WE))
                if v < QUAD - 1:
                    now.append(numbers(t + 1))
                    before.append(base)
                pe.wait_ge(h_ready, t + 1)
                wait(pe, h_split, t)
                for j in range(FC):
                    rows = P if j < FC - 1 else FT
                    last = pe.transpose(ps_h[0:rows, j, :], hf[u][:, j * P:j * P + rows], keep["ident"][:])
                last.then_inc(h_turned, 1)

            turn(0, 0)
            last = tiles(pe, step)
            down(last * QUAD + (QUAD - 1), 1, number(pe, last * QUAD + (QUAD - 1), "at0", 0, (BUFFERS - 1) * WE))


def combining_phase(nc, io, mem, keep, later, out):
    with ExitStack() as c:
        sem = lambda n: c.enter_context(nc.semaphore("d_" + n))
        down = later.last_d_hi, later.last_d_lo
        sh = Shared(nc, c, mem, keep, later, 2, down, later.last_xs,
                    [keep["last_xs_in"], [sem(f"xs{i}_in") for i in range(IT)]], "d_")
        assert sh.end <= nc.sbuf_usable_end
        free = [Sbuf(nc, at) for at, _ in later.free]
        parts = [free[(0, 0, 1, 1)[v]](f"parts{v}", [P, TOPK, D], F32) for v in range(4)]
        total = [free[1 if k < 4 else 2](f"total{k}", [P, D], F32) for k in range(6)]
        for place, (at, size) in zip(free, later.free):
            assert place.at <= at + size
        parts_in = [sem(f"parts{v}_in") for v in range(4)]
        total_in, total_out = ([sem(f"total{k}_{n}") for k in range(6)] for n in ("in", "out"))
        summed, terms, down_ready = sem("summed"), sem("terms"), sem("down_ready")
        block = c.enter_context(nc.Block())
        out_d = out.rearrange("(n p) d -> n p d", p=P)
        base_d = mem["base"].rearrange("(n p) d -> n p d", p=P)
        x2_d = mem["x2"].rearrange("(n p) d -> n p d", p=P)
        y_d = mem["y"][0:TILES_MAX * P]
        order = [tile for n in range(2) for tile in
                 [(2 + n) * IT + i for i in range(IT)] + [n * IT + i for i in range(IT)]]

        def place(tile):
            return (tile % 4, tile // 4 - 2) if tile >= 2 * IT else (4 + tile % 2, tile // 2)

        @block.sync
        def _(sp):
            def load(tile):
                k, before = place(tile)
                if before:
                    sp.wait_ge(total_out[k], before * 16)
                sp.dma_start(total[k][:], (x2_d if tile >= 2 * IT else base_d)[tile]).then_inc(total_in[k], 16)

            def store(tile):
                if tile >= 2 * IT:
                    sp.wait_ge(sh.y_free, tile - 2 * IT + 1)
                else:
                    sp.wait_ge(summed, order.index(tile) + 1)
                k, _ = place(tile)
                sp.dma_start(out_d[tile], total[k][:]).then_inc(total_out[k], 16)

            for tile in order[0:IT] + [0, 1]:
                load(tile)
            for i in range(IT):
                sh.load(sp, 1, i)
            for n in range(2):
                own, other = (2 + n) * IT, n * IT
                for k in (other, other + 1, own, other + 2, own + 1, other + 3, own + 2, own + 3):
                    store(k)
                    after = k + 2 if k < 2 * IT else k + IT
                    if after < (2 * IT if k < 2 * IT else NT):
                        load(after)
            for k in range(6):
                sp.wait_ge(total_out[k], 32 if k < 4 else 64)

        @block.gpsimd
        def _(pool):
            def gather(c):
                v = c % 4
                if c >= 4:
                    pool.wait_ge(summed, c - 3)
                for q in range(TOPK):
                    pool.indirect_dma_start(parts[v][:, q, :], None, y_d, bass.IndirectOffsetOnAxis(
                        ap=keep["slots"][:, order[c], q:q + 1], axis=0)).then_inc(parts_in[v], 16)

            for c in range(4):
                gather(c)
            pool.wait_ge(keep["last_down_in"], 64)
            split_down(pool, *down, later.last_d_raw, down_ready)
            for c in range(4, NT):
                gather(c)

        @block.scalar
        def _(act):
            sh.scalar(act)

        @block.vector
        def _(dve):
            def combine(c):
                k, before = place(order[c])
                dve.wait_ge(total_in[k], before * 16 + 16)
                dve.wait_ge(parts_in[c % 4], (c // 4) * 64 + 64)
                for q in range(TOPK):
                    ins = dve.scalar_tensor_tensor(out=total[k][:], in0=parts[c % 4][:, q, :],
                                                   scalar=keep["weights"][:, order[c], q:q + 1],
                                                   in1=total[k][:], op0=ALU.mult, op1=ALU.add)
                    if q < TOPK - 1:
                        ins.then_inc(terms, 1)
                        dve.wait_ge(terms, c * (TOPK - 1) + q + 1)
                    else:
                        ins.then_inc(summed, 1)

            def sum_of(n, i):
                dve.wait_ge(summed, n * 2 * IT + i + 1)
                return total[i]

            sh.vector(dve, sum_of, lambda n, k: combine(n * 2 * IT + k) if k < 2 * IT else None)

        @block.tensor
        def _(pe):
            sh.tensor(pe, lambda: None, lambda: pe.wait_ge(down_ready, 2))


def program(nc, io, out):
    mem = {k: nc.dram_tensor(k + "_dram", shape, F32, kind="Internal").ap() for k, shape in (
        ("x2", [T, D]), ("xn2", [T, D]), ("base", [T, D]), ("y", [(TILES_MAX + REST) * P, D]))}
    keep = persistent(nc)
    later = Later(nc, keep["end"])
    with ExitStack() as c:
        sem = lambda n: c.enter_context(nc.semaphore(n))
        keep["up_raw_in"], keep["up_hi_in"] = ([sem(f"up{k}_{n}_in") for k in range(2)] for n in ("raw", "hi"))
        keep["up_ready"], keep["first_ready"] = sem("up_ready"), sem("expert_split")
        keep["first_xs_in"], keep["gathered"] = ([sem(f"{n}{i}") for i in range(4)] for n in ("first_xs_in", "gathered"))
        keep["last_down_in"], keep["last_xs_in"] = sem("last_down_in"), [sem(f"last_xs{i}_in") for i in range(IT)]
        attention_phase(nc, io, mem, keep, later, keep["end"])
        routing_phase(nc, io, mem, keep, later)
        expert_phase(nc, io, mem, keep, later)
        combining_phase(nc, io, mem, keep, later, out)


def kernel(**inputs):
    import numpy as np
    from concourse import bacc
    from concourse.bass_utils import run_bass_kernel_spmd

    a = {k: np.asarray(v) for k, v in inputs.items()}

    def chunks(x):
        *lead, rows, n = x.shape
        return np.moveaxis(x.reshape(*lead, rows // P, P, n), -2, -3)

    w1, w3, w2 = (a["L0_ffn_W" + k].transpose(0, 2, 1) for k in "132")
    w2s = a["L0_ffn_W2s"].T
    arrays = {
        "x": a["x"].reshape(T, D),
        "ctx": chunks(a["ctx_2048"]),
        "ctxT": chunks(a["ctx_2048"].transpose(0, 2, 1)),
        "gx": a["g_xattn"],
        "gf": a["g_ffn"],
        "wg": chunks(a["L0_ffn_Wg"].T),
        "we": np.concatenate([chunks(w).reshape(E, P, -1) for w in (w1, w3, w2[:, 0:2 * P])], axis=2),
        "we_rest": w2[:, 2 * P:],
        "u": np.stack([chunks(a["L0_ffn_W1s"].T), chunks(a["L0_ffn_W3s"].T)], axis=1),
        "d": chunks(w2s[0:(SC - 1) * P]),
        "d_rest": w2s[(SC - 1) * P:],
    }
    for k in ("wq", "wk", "wv", "wo"):
        arrays[k] = chunks(a["L0_xattn_" + k].T)
    arrays = {k: np.ascontiguousarray(v) for k, v in arrays.items()}

    nc = bacc.Bacc("TRN2", target_bir_lowering=False, num_devices=1)
    io = {k: nc.dram_tensor(k, v.shape, mybir.dt.from_np(v.dtype), kind="ExternalInput").ap()
          for k, v in arrays.items()}
    out = nc.dram_tensor("out", (T, D), F32, kind="ExternalOutput").ap()
    program(nc, io, out)
    r = run_bass_kernel_spmd(nc, [arrays], core_ids=[0])
    return r.results[0]["out"].reshape(B, S, D)
```
